# Optimizing a Trainium2 kernel written in Bass

```python
import numpy as np
import jax
import jax.numpy as jnp

def _softmax(x, axis=-1):
    return jax.nn.softmax(x, axis=axis)

def _gelu(x):
    return jax.nn.gelu(x, approximate=True)

def _silu(x):
    return jax.nn.silu(x)

def _sigmoid(x):
    return jax.nn.sigmoid(x)

def _layernorm(x, axis=-1, eps=1e-05):
    m = jnp.mean(x, axis=axis, keepdims=True)
    v = jnp.var(x, axis=axis, keepdims=True)
    return (x - m) / jnp.sqrt(v + eps)

def _scatter_add(tgt, idx, src, axis=0):
    return tgt.at[idx].add(src)

def _segment_sum(src, seg, n):
    return jax.ops.segment_sum(src, seg, n)
kernel_name = 'mk_early_fusion_d1_tok_img256_r4_99dbb0'

def setup_inputs(seed: int=0):
    np.random.seed(seed)
    _w = jnp.asarray

    def _rec_inputs():
        import jax
        import jax.numpy as jnp
        _rk = jax.random.key(seed)
        x = -0.00040386 + 0.999972 * jax.random.normal(jax.random.fold_in(_rk, 1), (128, 128, 64, 3), jnp.float32)
        txt = -0.000423669 + 0.228197 * jax.random.normal(jax.random.fold_in(_rk, 2), (128, 77, 64), jnp.float32)
        return (x, txt)
    x, txt = _rec_inputs()

    def _L0_tok_setup():
        import jax, jax.numpy as jnp
        import numpy as np
        B, T, J, LAT = (128, 128, 64, 64)
        EPS = 1e-05

        def layernorm(x, g, b):
            m = jnp.mean(x, axis=-1, keepdims=True)
            v = jnp.var(x, axis=-1, keepdims=True)
            return (x - m) * jax.lax.rsqrt(v + EPS) * g + b

        def conv2d(x, w, b, pad):
            y = jax.lax.conv_general_dilated(x, w, window_strides=(1, 1), padding=pad, dimension_numbers=('NCHW', 'OIHW', 'NCHW'))
            return y + b[None, :, None, None]
        key = jax.random.key(seed)
        ks = jax.random.split(key, 10)
        s = 0.02
        return {'x': jax.random.normal(ks[0], (B, T, J, 3), dtype=jnp.float32), 'ln0_g': jnp.ones((J * 3,), jnp.float32), 'ln0_b': jnp.zeros((J * 3,), jnp.float32), 'ln1_g': jnp.ones((J * 2,), jnp.float32), 'ln1_b': jnp.zeros((J * 2,), jnp.float32), 'conv1_w': jax.random.normal(ks[1], (T, T, 5, 3), jnp.float32) * s, 'conv1_b': jnp.zeros((T,), jnp.float32), 'conv2_w': jax.random.normal(ks[2], (T, T, 5, 2), jnp.float32) * s, 'conv2_b': jnp.zeros((T,), jnp.float32), 'conv3_w': jax.random.normal(ks[3], (2 * T, T, 5, 2), jnp.float32) * s, 'conv3_b': jnp.zeros((2 * T,), jnp.float32), 'out_w': jax.random.normal(ks[4], (2 * J, LAT), jnp.float32) * s, 'out_b': jnp.zeros((LAT,), jnp.float32)}
    _L0_tok_all = _L0_tok_setup()
    _L0_tok_in = {k: v for k, v in _L0_tok_all.items() if k in ('ln0_g', 'ln0_b', 'ln1_g', 'ln1_b', 'conv1_w', 'conv1_b', 'conv2_w', 'conv2_b', 'conv3_w', 'conv3_b', 'out_w', 'out_b')}
    del _L0_tok_all

    def _L0_attn_setup():
        import jax, jax.numpy as jnp
        import numpy as np

        def softcap(x, a=10.0):
            return a * jnp.tanh(x / a)
        key = jax.random.key(seed)
        B, T, D = (4, 512, 64)
        ks = jax.random.split(key, 5)
        w = lambda k, s: jax.random.normal(k, s, dtype=jnp.float32) * 0.02
        return {'x': jax.random.normal(ks[0], (B, T, D), dtype=jnp.float32), 'Wq': w(ks[1], (D, D)), 'bq': jnp.zeros((D,), jnp.float32), 'Wk': w(ks[2], (D, D)), 'bk': jnp.zeros((D,), jnp.float32), 'Wv': w(ks[3], (D, D)), 'bv': jnp.zeros((D,), jnp.float32), 'Wg': w(ks[4], (D, 3 * D)), 'bg': jnp.zeros((3 * D,), jnp.float32), 'input_bias': -jnp.ones((D,), jnp.float32), 'norm_scale': jnp.ones((D,), jnp.float32)}
    _L0_attn_all = _L0_attn_setup()
    _L0_attn_in = {k: v for k, v in _L0_attn_all.items() if k in ('Wq', 'bq', 'Wk', 'bk', 'Wv', 'bv', 'Wg', 'bg', 'input_bias', 'norm_scale')}
    del _L0_attn_all

    def _L0_ffn_setup():
        import jax, jax.numpy as jnp
        import numpy as np
        B, S, H, F, E, K = (8, 1024, 64, 128, 16, 2)
        EPS = 1e-05
        key = jax.random.key(seed)
        ks = jax.random.split(key, 9)
        sc = 0.02
        return {'x': jax.random.normal(ks[0], (B, S, H), dtype=jnp.float32), 'gate_w': jax.random.normal(ks[1], (H, E), dtype=jnp.float32) * sc, 'gate_b': jnp.zeros((E,), dtype=jnp.float32), 'w1': jax.random.normal(ks[2], (E, H, F), dtype=jnp.float32) * sc, 'b1': jnp.zeros((E, F), dtype=jnp.float32), 'w2': jax.random.normal(ks[3], (E, F, H), dtype=jnp.float32) * sc, 'b2': jnp.zeros((E, H), dtype=jnp.float32), 'gamma': jnp.ones((H,), dtype=jnp.float32), 'beta': jnp.zeros((H,), dtype=jnp.float32)}
    _L0_ffn_all = _L0_ffn_setup()
    _L0_ffn_in = {k: v for k, v in _L0_ffn_all.items() if k in ('gate_w', 'gate_b', 'w1', 'b1', 'w2', 'b2', 'gamma', 'beta')}
    del _L0_ffn_all
    return {'x': x, 'txt': txt, 'L0_tok_ln0_g': _L0_tok_in['ln0_g'], 'L0_tok_ln0_b': _L0_tok_in['ln0_b'], 'L0_tok_ln1_g': _L0_tok_in['ln1_g'], 'L0_tok_ln1_b': _L0_tok_in['ln1_b'], 'L0_tok_conv1_w': _L0_tok_in['conv1_w'], 'L0_tok_conv1_b': _L0_tok_in['conv1_b'], 'L0_tok_conv2_w': _L0_tok_in['conv2_w'], 'L0_tok_conv2_b': _L0_tok_in['conv2_b'], 'L0_tok_conv3_w': _L0_tok_in['conv3_w'], 'L0_tok_conv3_b': _L0_tok_in['conv3_b'], 'L0_tok_out_w': _L0_tok_in['out_w'], 'L0_tok_out_b': _L0_tok_in['out_b'], 'L0_attn_Wq': _L0_attn_in['Wq'], 'L0_attn_bq': _L0_attn_in['bq'], 'L0_attn_Wk': _L0_attn_in['Wk'], 'L0_attn_bk': _L0_attn_in['bk'], 'L0_attn_Wv': _L0_attn_in['Wv'], 'L0_attn_bv': _L0_attn_in['bv'], 'L0_attn_Wg': _L0_attn_in['Wg'], 'L0_attn_bg': _L0_attn_in['bg'], 'L0_attn_input_bias': _L0_attn_in['input_bias'], 'L0_attn_norm_scale': _L0_attn_in['norm_scale'], 'L0_ffn_gate_w': _L0_ffn_in['gate_w'], 'L0_ffn_gate_b': _L0_ffn_in['gate_b'], 'L0_ffn_w1': _L0_ffn_in['w1'], 'L0_ffn_b1': _L0_ffn_in['b1'], 'L0_ffn_w2': _L0_ffn_in['w2'], 'L0_ffn_b2': _L0_ffn_in['b2'], 'L0_ffn_gamma': _L0_ffn_in['gamma'], 'L0_ffn_beta': _L0_ffn_in['beta']}

def reference(x, txt, L0_tok_ln0_g, L0_tok_ln0_b, L0_tok_ln1_g, L0_tok_ln1_b, L0_tok_conv1_w, L0_tok_conv1_b, L0_tok_conv2_w, L0_tok_conv2_b, L0_tok_conv3_w, L0_tok_conv3_b, L0_tok_out_w, L0_tok_out_b, L0_attn_Wq, L0_attn_bq, L0_attn_Wk, L0_attn_bk, L0_attn_Wv, L0_attn_bv, L0_attn_Wg, L0_attn_bg, L0_attn_input_bias, L0_attn_norm_scale, L0_ffn_gate_w, L0_ffn_gate_b, L0_ffn_w1, L0_ffn_b1, L0_ffn_w2, L0_ffn_b2, L0_ffn_gamma, L0_ffn_beta):
    import jax
    import jax.numpy as jnp

    def _L0_tok_ref(x, ln0_g, ln0_b, ln1_g, ln1_b, conv1_w, conv1_b, conv2_w, conv2_b, conv3_w, conv3_b, out_w, out_b):
        import jax, jax.numpy as jnp
        import numpy as np
        B, T, J, LAT = (128, 128, 64, 64)
        EPS = 1e-05

        def layernorm(x, g, b):
            m = jnp.mean(x, axis=-1, keepdims=True)
            v = jnp.var(x, axis=-1, keepdims=True)
            return (x - m) * jax.lax.rsqrt(v + EPS) * g + b

        def conv2d(x, w, b, pad):
            y = jax.lax.conv_general_dilated(x, w, window_strides=(1, 1), padding=pad, dimension_numbers=('NCHW', 'OIHW', 'NCHW'))
            return y + b[None, :, None, None]
        b, t, j, d = x.shape
        h = layernorm(x.reshape(b, t, j * 3), ln0_g, ln0_b).reshape(b, t, j, 3)
        h = jax.nn.relu(conv2d(h, conv1_w, conv1_b, ((2, 2), (1, 1))))
        h = layernorm(h.reshape(b, t, j * 3), ln0_g, ln0_b).reshape(b, t, j, 3)
        h = jax.nn.relu(conv2d(h, conv2_w, conv2_b, ((2, 2), (0, 0))))
        h = layernorm(h.reshape(b, t, j * 2), ln1_g, ln1_b).reshape(b, t, j, 2)
        h = jax.nn.relu(conv2d(h, conv3_w, conv3_b, ((2, 2), (0, 0))))
        h = h.reshape(b, 2 * t, j)
        res = jnp.concatenate([h[:, :t, :], h[:, t:, :]], axis=2)
        res = layernorm(res, ln1_g, ln1_b)
        return res @ out_w + out_b

    def _L0_attn_ref(x, Wq, bq, Wk, bk, Wv, bv, Wg, bg, input_bias, norm_scale):
        import jax, jax.numpy as jnp
        import numpy as np

        def softcap(x, a=10.0):
            return a * jnp.tanh(x / a)
        B, T, D = x.shape
        inv_sqrt_d = 1.0 / jnp.sqrt(jnp.asarray(D, jnp.float32))
        q = x @ Wq + bq
        k = (x @ Wk + bk) * inv_sqrt_d
        v = x @ Wv + bv
        gates = x @ Wg + bg
        i_pre, f_pre, o_pre = jnp.split(gates, 3, axis=-1)
        log_i = softcap(i_pre + input_bias)
        log_f = -jax.nn.softplus(f_pre)

        def step(carry, inp):
            M, n, m = carry
            qt, kt, vt, li, lf, op = inp
            m_next = jnp.maximum(lf + m, li)
            i_s = jnp.exp(li - m_next)
            f_s = jnp.exp(lf + m - m_next)
            M = f_s[:, :, None] * M + i_s[:, :, None] * (vt[:, :, None] * kt[:, None, :])
            n = f_s * n + i_s * kt
            h_raw = jnp.einsum('bij,bj->bi', M, qt)
            denom = jnp.maximum(jnp.abs(jnp.einsum('bi,bi->b', n, qt))[:, None], 1e-06)
            h = jax.nn.sigmoid(op) * (h_raw / denom)
            return ((M, n, m_next), h)
        M0 = jnp.zeros((B, D, D), jnp.float32)
        n0 = jnp.zeros((B, D), jnp.float32)
        m0 = jnp.zeros((B, D), jnp.float32)
        xs = tuple((jnp.swapaxes(a, 0, 1) for a in (q, k, v, log_i, log_f, o_pre)))
        _, hs = jax.lax.scan(step, (M0, n0, m0), xs)
        out = jnp.swapaxes(hs, 0, 1)
        rms = jnp.sqrt(jnp.mean(out * out, axis=-1, keepdims=True) + 1e-08)
        return out / rms * norm_scale

    def _L0_ffn_ref(x, gate_w, gate_b, w1, b1, w2, b2, gamma, beta):
        import jax, jax.numpy as jnp
        import numpy as np
        B, S, H, F, E, K = (8, 1024, 64, 128, 16, 2)
        EPS = 1e-05
        gate_logits = x @ gate_w + gate_b
        topk_vals, topk_idx = jax.lax.top_k(gate_logits, K)
        topk_w = jax.nn.softmax(topk_vals, axis=-1)
        h = jax.nn.relu(jnp.einsum('bsh,ehf->bsef', x, w1) + b1)
        expert_out = jnp.einsum('bsef,efh->bseh', h, w2) + b2
        sel = jnp.take_along_axis(expert_out, topk_idx[:, :, :, None], axis=2)
        moe = jnp.sum(topk_w[..., None] * sel, axis=2)
        y = x + moe
        mu = jnp.mean(y, axis=-1, keepdims=True)
        var = jnp.var(y, axis=-1, keepdims=True)
        return (y - mu) / jnp.sqrt(var + EPS) * gamma + beta
    h = _L0_tok_ref(x, L0_tok_ln0_g, L0_tok_ln0_b, L0_tok_ln1_g, L0_tok_ln1_b, L0_tok_conv1_w, L0_tok_conv1_b, L0_tok_conv2_w, L0_tok_conv2_b, L0_tok_conv3_w, L0_tok_conv3_b, L0_tok_out_w, L0_tok_out_b)
    h = jnp.concatenate([h, txt], axis=1)
    h = h + _L0_attn_ref(_layernorm(h, axis=-1), L0_attn_Wq, L0_attn_bq, L0_attn_Wk, L0_attn_bk, L0_attn_Wv, L0_attn_bv, L0_attn_Wg, L0_attn_bg, L0_attn_input_bias, L0_attn_norm_scale)
    h = h + _L0_ffn_ref(_layernorm(h, axis=-1), L0_ffn_gate_w, L0_ffn_gate_b, L0_ffn_w1, L0_ffn_b1, L0_ffn_w2, L0_ffn_b2, L0_ffn_gamma, L0_ffn_beta)
    return h

_drawn_inputs = setup_inputs


def setup_inputs(seed=0):
    import zlib

    import numpy as np

    out = dict(_drawn_inputs(seed))
    spreads = {'L0_tok_ln0_g': (1.0, 0.2),
     'L0_tok_ln0_b': (0.0, 0.1),
     'L0_tok_ln1_g': (1.0, 0.2),
     'L0_tok_ln1_b': (0.0, 0.1),
     'L0_tok_conv1_b': (0.0, 0.1),
     'L0_tok_conv2_b': (0.0, 0.1),
     'L0_tok_conv3_b': (0.0, 0.1),
     'L0_tok_out_b': (0.0, 0.1),
     'L0_attn_bq': (0.0, 0.1),
     'L0_attn_bk': (0.0, 0.1),
     'L0_attn_bv': (0.0, 0.1),
     'L0_attn_bg': (0.0, 0.1),
     'L0_attn_input_bias': (-1.0, 0.6),
     'L0_attn_norm_scale': (1.0, 0.2),
     'L0_ffn_gate_b': (0.0, 0.1),
     'L0_ffn_b1': (0.0, 0.8),
     'L0_ffn_b2': (0.0, 0.304),
     'L0_ffn_gamma': (1.0, 0.2),
     'L0_ffn_beta': (0.0, 0.1)}
    factors = {'L0_ffn_w1': 7.315, 'L0_ffn_w2': 5.443}
    for name, (base, spread) in spreads.items():
        noise = np.random.default_rng([zlib.crc32(name.encode()), seed]).standard_normal(out[name].shape)
        drawn = base * np.exp(spread * noise) if base else spread * noise
        out[name] = jnp.asarray(drawn.astype(out[name].dtype))
    for name, factor in factors.items():
        out[name] = (out[name] * factor).astype(out[name].dtype)
    return out
```

```python
import concourse.bass as bass
from concourse import mybir
from contextlib import ExitStack

F32 = mybir.dt.float32
F16 = mybir.dt.float16
ALU = mybir.AluOpType
ACT = mybir.ActivationFunctionType
AX = mybir.AxisListType


class Chain:

    def __init__(self, eng, sem):
        self.eng, self.sem, self.base, self.n = eng, sem, 0, 0

    def link(self, ins):
        self.n += 1
        ins.then_inc(self.sem, 1)
        self.eng.wait_ge(self.sem, self.base + self.n)

    def enter(self, i, first, per_turn):
        self.start, self.per_turn = self.base + self.n, per_turn
        self.base, self.n = i * per_turn + (self.start - first * per_turn), 0

    def leave(self, turns):
        assert self.n == self.per_turn, (self.n, self.per_turn)
        self.base, self.n = self.start + turns * self.per_turn, 0


def build(nc, a, out):
    B, T, J = 128, 128, 64
    GB = 8
    NG = B // GB
    JP = J + 4
    T2 = 77
    S = T + T2
    NP = B // 2
    XS, WS = 256.0, 1024.0
    UNSCALE = 1.0 / (XS * WS)
    EPS = 1e-5

    with ExitStack() as ctx:
        def sb(name, shape, dt=F32):
            return ctx.enter_context(nc.sbuf_tensor(name, shape, dt))

        def sem(name):
            return ctx.enter_context(nc.semaphore(name))

        conv_bank = [ctx.enter_context(nc.psum_tensor(f"conv_bank{k}", [128, 512], F32)) for k in range(2)]

        WID = {1: 15 * T, 2: 10 * T, 3: 10 * 2 * T, 4: 64}
        w_hi = {k: sb(f"w_hi{k}", [128, n], F16) for k, n in WID.items()}
        w_lo = {k: sb(f"w_lo{k}", [128, n], F16) for k, n in WID.items()}
        cb = sb("cb", [128, 5])
        eps = sb("eps", [128, 1])
        gb_raw = sb("gb_raw", [128, 4, 192])
        gam = [sb(f"gam{k}", [128, n]) for k, n in enumerate((192, 192, 128, 128))]
        bet = [sb(f"bet{k}", [128, n]) for k, n in enumerate((192, 192, 128, 128))]

        x_in = sb("x_in", [128, GB, 192])
        h_relu = [None, sb("h1", [128, 3, GB, J]), sb("h2", [128, 2, GB, J]), sb("h3", [128, GB, 2, J])]
        stats = [sb(f"stats{k}", [128, GB, 6]) for k in range(4)]
        mean = [sb(f"mean{k}", [128, GB]) for k in range(4)]
        var4 = [sb(f"var4_{k}", [128, GB]) for k in range(4)]
        spread, half_mean, gap, gap2 = (sb(n, [128, GB]) for n in ("spread", "half_mean", "gap", "gap2"))
        lnv = [sb(f"lnv{k}", [128, GB]) for k in range(4)]
        rstd = [sb(f"rstd{k}", [128, GB]) for k in range(4)]
        centred = sb("centred", [128, GB, 192])
        full = [sb(f"full{k}", [128, 3 * GB * J]) for k in range(2)]
        act1 = sb("act1", [128, 2, 3, GB, JP], F16)
        act2 = sb("act2", [128, 2, 3, GB, JP], F16)
        act3 = sb("act3", [128, 2, 2, GB, JP], F16)
        res = sb("res", [128, 2, GB, 128], F16)
        resT = sb("resT", [128, 2, GB, 128], F16)

        GP = GB // 2
        N = GP * S
        HALF = N // 2
        BLOCKS = ((0, 64), (64, 128), (128, S))
        double = [ctx.enter_context(nc.psum_tensor(f"double{k}", [128, 2, 512], F32)) for k in range(3)]
        PROJ = ("f", "i", "k", "v", "q", "o")
        ident32 = sb("ident32", [128, 128])
        w_proj = {n: sb(f"w_proj_{n}", [128, 128]) for n in PROJ}
        w_gate = sb("w_gate", [128, 32])
        centre = sb("centre", [128, 128])
        average = sb("average", [128, 128])
        total = sb("total", [128, 128])
        acol = sb("acol", [128, 8])
        bias_k, bias_i, bias_o = (sb(n, [128, 1]) for n in ("bias_k", "bias_i", "bias_o"))
        gate_bias = sb("gate_bias", [128, 16])
        eps8 = sb("eps8", [128, 1])
        one = sb("one", [128, 1])
        causal = sb("causal", [128, S + T2])
        not_start = sb("not_start", [128, N])
        names = ("tokens", "resid", "sq", "rs", "xn", "lf", "li", "kT", "vT", "qT", "o_log", "cum", "t_f",
                 "t_i", "wv", "nq", "gexp", "den", "h2", "xn2")
        arena = sb("arena", [128, len(names), GP, S])
        A = {n: arena[:, k] for k, n in enumerate(names)}
        A["h"] = A["wv"]
        raw_room = arena[:, len(names) - 8:].rearrange("p k g s -> p (k g s)")
        w_raw, at = {}, 0
        for k, n in WID.items():
            w_raw[k] = raw_room[:, at:at + n]
            at += n
        m_ext = sb("m_ext", [128, GP, S + 1])
        s_arg = sb("s_arg", [128, GP, 2])
        s_dec = sb("s_dec", [128, GP, 3])
        st = sb("st", [128, GB, S + T2])
        vt = sb("vt", [128, GP, 256])
        u1 = sb("u1", [128, GP, S])
        u2 = sb("u2", [128, GP, T2])
        tm0 = sb("tm0", [128, GB, 144])
        tm1 = sb("tm1", [128, GB, 144])

        E, F, D_ = 16, 128, 64
        CH = 41
        CHUNKS = S // CH
        PARTS = ((0, 21), (21, CH))
        QUADS = (2 * B * S // 128 + E + 3) // 4
        TILES = 4 * QUADS
        ROWS = TILES * 128
        H_SCALE, FW_SCALE = 64.0, 256.0
        room = arena[:, :, :, :].rearrange("p k g s -> p (k g s)")
        lay = [0]

        def carve(n):
            lay[0] += n
            return room[:, lay[0] - n:lay[0]]

        raw1, raw2, rawb = room[:, 0:E * F], room[:, E * F:E * F + E * D_], room[:, E * (F + D_):E * (F + 2 * D_)]
        logit = carve(S * E).rearrange("p (t e) -> p t e", e=E)
        work = carve(S * E)
        chosen = [carve(S * E).rearrange("p (t e) -> p t e", e=E) for _ in range(2)]
        work_te, work_et = work.rearrange("p (t e) -> p t e", e=E), work.rearrange("p (e t) -> p e t", e=E)
        rank = logit.rearrange("p t e -> p (t e)").rearrange("p (e t) -> p e t", e=E)
        top, which = [carve(S) for _ in range(2)], carve(S)
        gate = [carve(S) for _ in range(2)]
        slot_f = carve(S)
        slot = [carve(S).bitcast(mybir.dt.uint32) for _ in range(2)]
        tile_no, tile_exp = carve(TILES), carve(TILES)
        assert lay[0] <= 20 * N
        lay[0] = 0
        xn_part = carve(CH * D_).rearrange("p (t f) -> p t f", f=D_)
        x_tiles = [carve(4 * D_).rearrange("p (n f) -> p n f", f=D_) for _ in range(2)]
        xT = [carve(256).bitcast(F16) for _ in range(2)]
        hid = [carve(512) for _ in range(2)]
        hid_hi, hid_lo = ([carve(256).bitcast(F16) for _ in range(2)] for _ in range(2))
        o_tiles = [carve(4 * D_).rearrange("p (n f) -> p n f", f=D_) for _ in range(2)]
        assert lay[0] <= 4 * S * E
        lay[0] = 0
        got = carve(CH * 2 * D_).rearrange("p (t k f) -> p t k f", k=2, f=D_)
        stream = carve(CH * 2 * D_).rearrange("p (t k f) -> p t k f", k=2, f=D_)
        y = carve(CH * D_).rearrange("p (t f) -> p t f", f=D_)
        assert lay[0] <= 4 * S * E
        st_room = st[:, :, :].rearrange("p b s -> p (b s)")
        fw1_hi, fw1_lo = (st_room[:, 1024 * k:1024 * k + 1024].bitcast(F16) for k in range(2))
        fw2_hi, fw2_lo, fb2 = (full[0][:, 512 * k:512 * k + 512].bitcast(F16) for k in range(3))
        fb1 = sb("fb1", [128, E])
        fb1s = sb("fb1s", [128, E])
        ff_gb = sb("ff_gb", [128, 2, D_])
        row_sel = sb("row_sel", [2, 2])
        ones_h = sb("ones_h", [2, 128], F16)
        e_minus = sb("e_minus", [128, E])
        ones_s = not_start[:, 0:S]
        all_ones = sb("all_ones", [128, 128])
        before = sb("before", [128, 128])
        counts, ends, off, tiles_e = (sb(n, [128, E]) for n in ("counts", "ends", "off", "tiles_e"))
        tiles_i = sb("tiles_i", [128, E], mybir.dt.int32)
        tile_i = sb("tile_i", [128, TILES], mybir.dt.int32)
        y_mean, y_var, y_rstd = (sb(n, [128, CH]) for n in ("y_mean", "y_var", "y_rstd"))
        xs_dram = nc.dram_tensor("xs_dram", [ROWS, D_], F32).ap()
        es_dram = nc.dram_tensor("es_dram", [ROWS, D_], F32).ap()
        zeros = sb("zeros", [128, 512])

        def flat(name):
            return A[name].rearrange("p g s -> p (g s)")

        def halves2(name):
            return flat(name).rearrange("p (c n) -> p c n", c=2)

        ident = sb("ident", [128, 128], F16)
        DVE_LINKS, ACT_LINKS = 31, 12
        mid = sb("mid", [128, GP, 3])
        tok_dram = nc.dram_tensor("tok_dram", [B, S, 144], F32).ap()
        s_w = sem("weights_loaded")
        s_c = sem("constants_loaded")
        s_x = sem("x_loaded")
        s_const = sem("constants_made")
        s_pad = sem("pads_zeroed")
        s_whi = sem("weights_hi_made")
        s_wlo = sem("weights_lo_made")
        s_dve = sem("dve_chain")
        s_act = sem("act_chain")
        s_var = [sem(f"var_ready{k}") for k in range(4)]
        s_rstd = [sem(f"rstd_ready{k}") for k in range(4)]
        s_full = [sem(f"full_ready{k}") for k in range(4)]
        s_hi = [sem(f"hi_ready{k}") for k in range(4)]
        s_lo = [sem(f"lo_ready{k}") for k in range(4)]
        s_conv = [None] + [sem(f"conv_done{k}") for k in (1, 2, 3)]
        s_relu = [None] + [sem(f"relu_done{k}") for k in (1, 2, 3)]
        s_turn = sem("res_turned")
        s_rT = sem("resT_ready")
        s_tok = sem("tok_product_done")
        s_H = sem("tokens_ready")
        s_zero = sem("zeros_stored")
        s_fw = sem("expert_weights_loaded")
        s_fhi = sem("expert_weights_hi")
        s_fmade = sem("expert_weights_made")
        s_lgin = sem("logits_loaded")
        s_cnt = sem("counts_made")
        s_off = sem("offsets_made")
        s_gexp = sem("gate_exp_arg")
        s_gexp2 = sem("gate_exp")
        s_slot = sem("slots_made")
        s_tmap = sem("tile_map_made")
        s_xpart = [sem("xn_part_loaded0"), sem("xn_part_loaded1")]
        s_idx = sem("indices_staged")
        s_scat = [sem("scattered0"), sem("scattered1")]
        s_xt = [sem("x_tiles_loaded0"), sem("x_tiles_loaded1")]
        s_xturn = sem("x_tiles_turned")
        s_xhi = sem("x_hi")
        s_xlo = sem("x_lo")
        s_mm1 = sem("hidden_done")
        s_hid = sem("hidden_relu")
        s_hhi = sem("hidden_hi")
        s_hlo = sem("hidden_lo")
        s_mm2 = sem("expert_out_done")
        s_o = sem("expert_out_copied")
        s_ost = [sem("expert_out_stored0"), sem("expert_out_stored1")]
        s_got = [sem("gathered0"), sem("gathered1")]
        s_strm = [sem("stream_loaded0"), sem("stream_loaded1")]
        s_yvar = sem("y_var")
        s_yr = sem("y_rstd")
        s_yout = [sem("y_done0"), sem("y_done1")]
        s_txt = sem("text_loaded")
        s_aw = sem("attention_weights_loaded")
        s_ac = sem("attention_constants_loaded")
        s_az = sem("weights_zeroed")
        s_acon = sem("attention_constants_made")
        s_hres = sem("residual_kept")
        filled = {n: sem("filled_" + n) for n in ("cx1", "var1", "f", "i", "k", "v", "q", "o", "sc", "den", "vt", "hacc",
                                                  "ms", "cx3", "var3", "tm", "lg")}
        (s_sq1, s_rs1, s_xn, s_l1, s_lf, s_ti, s_li, s_k, s_v, s_q, s_og, s_m, s_fs_arg, s_fs, s_is_arg, s_is, s_e_arg, s_e, s_s_arg, s_s,
         s_vp, s_nq, s_st, s_vt, s_den, s_lden, s_garg, s_g, s_h, s_sq2, s_rs2, s_h2, s_sq3, s_rs3, s_xn2, s_tmA, s_tmD,
         s_lg, s_sav, s_dmax, s_fpos) = (sem(n) for n in (
            "sq1", "rs1", "xn", "l1", "lf", "ti", "li", "k_r", "v_r", "q_r", "og", "m", "fs_arg", "fs", "is_arg", "is_r", "e_arg", "e_r",
            "s_arg_r", "s_r", "vp", "nq", "st_r", "vt_r", "den_r", "lden", "garg", "g", "h_r", "sq2", "rs2", "h2", "sq3", "rs3", "xn2",
            "tmA", "tmD", "lg", "saved", "dmax", "fpos"))
        s_out2 = [sem("out_stored0"), sem("out_stored1")]
        s_done = sem("expert_rows_stored")
        s_scans = sem("rank_scans")

        block = ctx.enter_context(nc.Block())

        COLS = (3, 3, 2, 2)

        def source(k, b):
            if k == 0:
                return x_in[:, b, :].rearrange("p (j w) -> p w j", w=3)
            return h_relu[k][:, :, b, :] if k < 3 else h_relu[3][:, b, :, :]

        def full_of(k):
            w = COLS[k]
            f = full[k % 2][:, 0:w * GB * J]
            return f.rearrange("p (w b j) -> p w b j", w=w, b=GB) if k < 3 else f.rearrange("p (b w j) -> p w b j", w=w, b=GB)

        def halves(k, h):
            if k == 3:
                return res[:, h].rearrange("p b (w j) -> p w b j", w=2)
            return (act1, act2, act3)[k][:, h, :, :, 2:2 + J]

        def columns(t, k):
            return t.rearrange("p (w j) -> p w j", w=COLS[k])

        ORDER, D = [], 0
        for name, lag, reader, per, at in (
                ("c10", 0, s_relu[1], 3, 1), ("tok", 2, s_H, 2, 2), ("ms", 3, s_rs2, 1, 1),
                ("c11", 0, s_relu[1], 3, 2), ("cx3", 3, s_xn2, 1, 1), ("cx1", 2, s_xn, 1, 1),
                ("c12", 0, s_relu[1], 3, 3), ("var3", 3, s_rs3, 1, 1), ("var1", 2, s_rs1, 1, 1),
                ("c30", 1, s_relu[3], 2, 1), ("tm0", 3, s_tmD, 1, 1), ("tm1", 3, s_tmA, 1, 1), ("lg", 3, s_lg, 1, 1),
                ("f", 2, s_lf, 1, 1), ("i", 2, s_ti, 1, 1), ("k", 2, s_k, 1, 1), ("v", 2, s_v, 1, 1), ("q", 2, s_q, 1, 1), ("o", 2, s_og, 1, 1),
                ("c31", 1, s_relu[3], 2, 2), ("sc0", 2, s_st, 4, 1), ("sc1", 2, s_st, 4, 2), ("sc2", 2, s_st, 4, 3), ("sc3", 2, s_st, 4, 4),
                ("c20", 0, s_relu[2], 2, 1), ("den", 2, s_den, 1, 1), ("vt", 2, s_vt, 1, 1),
                ("c21", 0, s_relu[2], 2, 2), ("hacc0", 2, s_h, 2, 1), ("hacc1", 2, s_h, 2, 2), ("turned", 1, s_rT, 1, 1)):
            if name[0] == "c" and name[1] in "123":
                tile = conv_bank[(len(ORDER) - D) % 2]
            else:
                tile = double[D % 3]
                D += 1
            ORDER.append((name, lag, tile, reader, per, at))
        assert D == 24
        TURNS = NG + 3
        TILE = {name: tile for name, _, tile, _, _, _ in ORDER}
        LAG = {name: lag for name, lag, *_ in ORDER}
        BEFORE = {}
        last_in = {}
        for t in range(TURNS):
            for name, lag, tile, reader, per, at in ORDER:
                g = t - lag
                if 0 <= g < NG:
                    BEFORE[name, g] = last_in.get(id(tile))
                    last_in[id(tile)] = (reader, per, at, g)

        STEADY = 5
        LOOP = (4, NG - 1)
        for t in range(*LOOP):
            for name, lag, *_ in ORDER:
                b, c = BEFORE[name, t - lag], BEFORE[name, STEADY - lag]
                assert b[:3] == c[:3] and b[3] - t == c[3] - STEADY

        def take(pe, name, g):
            like = g if isinstance(g, int) else STEADY - LAG[name]
            before = BEFORE[name, like]
            if before:
                reader, per, at, b = before
                pe.wait_ge(reader, g * per + ((b - like) * per + at))
            return TILE[name]

        def on(g):
            return not isinstance(g, int) or 0 <= g < NG

        def half_of(q, h):
            return q // 2 if isinstance(q, int) else pair_no[id(q)]

        pair_no = {}

        def quads(eng, quad):
            quad(0, 0)
            quad(1, 1)
            with eng.Fori(1, QUADS // 2) as j:
                for h in range(2):
                    q = j * 2 + h
                    pair_no[id(q)] = j
                    quad(q, h)
            if QUADS % 2:
                quad(QUADS - 1, 0)

        def turns(eng, c, links, turn):
            for t in range(0, LOOP[0]):
                turn(t)
            with eng.Fori(*LOOP) as t:
                if c:
                    c.enter(t, LOOP[0], links)
                turn(t)
            if c:
                c.leave(LOOP[1] - LOOP[0])
            for t in range(LOOP[1], TURNS):
                turn(t)

        def wait(eng, s, count):
            if not (isinstance(count, int) and count <= 0):
                eng.wait_ge(s, count)

        def copy_turned(copy, n):
            tile = TILE[f"tm{n}"][:, :, :].rearrange("p g (k s b f) -> p k s g b f", k=2, s=2, b=2)
            for s_, (dst, rows) in enumerate(((tm0, 128), (tm1, T2))):
                for k in range(2):
                    rowsof = dst[0:rows, 4 * n:4 * n + 4, 64 * k:64 * k + 64].rearrange("p (g b) f -> p g b f", g=2)
                    last = copy(rowsof, tile[0:rows, k, s_])
            return last

        @block.sync
        def _(sp):
            for k in (1, 2, 3, 4):
                sp.dma_start(w_raw[k], a[f"w{k}"]).then_inc(s_w, 16)
            with nc.allow_non_contiguous_dma(reason="a few bias columns"):
                sp.dma_start(cb[:, 0:1], a["conv1_b"].rearrange("(p o) -> p o", o=1)).then_inc(s_c, 16)
                sp.dma_start(cb[:, 1:2], a["conv2_b"].rearrange("(p o) -> p o", o=1)).then_inc(s_c, 16)
                sp.dma_start(cb[:, 2:4], a["conv3_b"].rearrange("(h p) -> p h", h=2)).then_inc(s_c, 16)
                for h in range(2):
                    sp.dma_start(cb[64 * h:64 * h + 64, 4:5], a["out_b"].rearrange("(p o) -> p o", o=1)).then_inc(s_c, 16)
            for n, name in enumerate(("ln0_g", "ln0_b", "ln1_g", "ln1_b")):
                m = 192 if n < 2 else 128
                sp.dma_start(gb_raw[:, n, 0:m], a[name].rearrange("(o n) -> o n", o=1).to_broadcast([128, m])).then_inc(s_c, 16)

            def load_x(i):
                wait(sp, s_full[0], i)
                sp.dma_start(x_in[:, :, :].rearrange("p b f -> p (b f)"), a["x"][i]).then_inc(s_x, 16)

            load_x(0)
            sp.wait_ge(s_az, 1)
            for r in range(0, ROWS, 128 * 8):
                n = min(8, (ROWS - r) // 128)
                sp.dma_start(xs_dram[r:r + 128 * n].rearrange("(p n) f -> p (n f)", p=128), zeros[:, 0:64 * n]).then_inc(s_zero, 16)
            sp.wait_ge(s_az, 1)
            for h in range(2):
                q = slice(64 * h, 64 * h + 64)
                for n in PROJ:
                    sp.dma_start(w_proj[n][q, q], a["w_" + n]).then_inc(s_aw, 16)
                sp.dma_start(w_gate[q, 16 * h:16 * h + 16], a["gate_w"]).then_inc(s_aw, 16)
                sp.dma_start(acol[q, :], a["acol"]).then_inc(s_ac, 16)
            sp.dma_start(gate_bias[:, :], a["gate_b"].rearrange("(o n) -> o n", o=1).to_broadcast([128, 16])).then_inc(s_ac, 16)

            def text(g):
                wait(sp, s_hres, g)
                wait(sp, s_sq1, g)
                sp.dma_start(A["tokens"][:, :, T:S], a["txt"][g]).then_inc(s_txt, 16)

            def save(g):
                sp.wait_ge(s_tmD, g + 1)
                sp.wait_ge(s_tmA, g + 1)
                sp.wait_ge(s_lg, g + 1)
                rows = tok_dram[bass.ds(g * GB, GB)].rearrange("b t f -> t b f")
                sp.dma_start(rows[0:128], tm0[:, :, :]).then_inc(s_sav, 16)
                sp.dma_start(rows[128:S], tm1[0:T2, :, :]).then_inc(s_sav, 16)

            def turn(t):
                if on(t + 1):
                    load_x(t + 1)
                if on(t - 1):
                    text(t - 1)
                if on(t - 3):
                    save(t - 3)

            turns(sp, None, 0, turn)
            sp.wait_ge(s_sav, 32 * NG)
            sp.wait_ge(filled["hacc"], 2 * NG)
            sp.dma_start(raw1.rearrange("p (e f) -> p e f", e=E)[0:64], a["ffn_w1"]).then_inc(s_fw, 16)
            sp.dma_start(raw1.rearrange("p (e f) -> p e f", e=E)[64:128], a["ffn_w1"]).then_inc(s_fw, 16)
            sp.dma_start(raw2.rearrange("p (e f) -> p e f", e=E), a["ffn_w2"]).then_inc(s_fw, 16)
            for r in range(2):
                sp.dma_start(rawb[r:r + 1, :], a["ffn_b2"]).then_inc(s_fw, 16)
            sp.dma_start(fb1[:, :], a["ffn_b1"]).then_inc(s_fw, 16)
            sp.dma_start(row_sel[:, :], a["row_sel"]).then_inc(s_fw, 16)
            for k, name in enumerate(("ffn_gamma", "ffn_beta")):
                sp.dma_start(ff_gb[:, k, :], a[name].rearrange("(o n) -> o n", o=1).to_broadcast([128, D_])).then_inc(s_fw, 16)
            sp.wait_ge(s_fmade, 4)
            sp.dma_start(logit, tok_dram[:, :, 128:144]).then_inc(s_lgin, 16)
            sp.wait_ge(s_slot, 2)
            for k in range(CHUNKS):
                for h, (lo, hi) in enumerate(PARTS):
                    if k:
                        sp.wait_ge(s_scat[h], 16 * 2 * (hi - lo) * k)
                    sp.dma_start(xn_part[:, lo:hi, :], tok_dram[:, k * CH + lo:k * CH + hi, 0:D_]).then_inc(s_xpart[h], 16)
            for h, (lo, hi) in enumerate(PARTS):
                sp.wait_ge(s_scat[h], 16 * 2 * (hi - lo) * CHUNKS)

            def load_tiles(q, h):
                sp.dma_start(x_tiles[h], xs_dram[bass.ds(q * 512, 512)].rearrange("(n p) f -> p n f", p=128)).then_inc(s_xt[h], 16)

            def store_tiles(q, h):
                sp.wait_ge(s_o, q + 1)
                sp.dma_start(es_dram[bass.ds(q * 512, 512)].rearrange("(n p) f -> p n f", p=128), o_tiles[h]).then_inc(s_ost[h], 16)

            load_tiles(0, 0)
            load_tiles(1, 1)
            with sp.Fori(0, QUADS // 2 - 1) as j:
                for h in range(2):
                    sp.wait_ge(s_xturn, j * 2 + (h + 1))
                    load_tiles(j * 2 + (h + 2), h)
                for h in range(2):
                    store_tiles(j * 2 + h, h)
            q = QUADS // 2 * 2
            if QUADS % 2:
                sp.wait_ge(s_xturn, q - 1)
                load_tiles(q, 0)
            for r in range(q - 2, QUADS):
                store_tiles(r, r % 2)
            for h in range(2):
                sp.wait_ge(s_ost[h], 16 * ((QUADS + 1 - h) // 2))
            sp.sem_inc(s_done, 1)
            for k in range(CHUNKS):
                for h, (lo, hi) in enumerate(PARTS):
                    if k:
                        sp.wait_ge(s_out2[h], 16 * k)
                    sp.dma_start(stream[:, lo:hi], tok_dram[:, k * CH + lo:k * CH + hi, 0:2 * D_].rearrange("b t (k f) -> b t k f", k=2)).then_inc(s_strm[h], 16)
                for h, (lo, hi) in enumerate(PARTS):
                    sp.wait_ge(s_yout[h], k + 1)
                    sp.dma_start(out[:, k * CH + lo:k * CH + hi, :], y[:, lo:hi, :]).then_inc(s_out2[h], 16)
            for h in range(2):
                sp.wait_ge(s_out2[h], 16 * CHUNKS)

        @block.vector
        def _(dve):
            c = Chain(dve, s_dve)
            dve.memset(one[:, :], 1.0)
            dve.memset(eps8[:, :], 1e-8)
            dve.memset(m_ext[:, :, 0:1], 0.0)
            dve.memset(u1[:, :, 0:64], 0.0)
            dve.memset(not_start[:, :], 1.0)
            c.link(dve.memset(eps[:, :], EPS))
            starts = not_start[:, :].rearrange("p (g s) -> p g s", g=GP)
            for lo, _ in BLOCKS:
                dve.memset(starts[:, :, lo:lo + 1], 0.0)
            dve.wait_ge(s_c, 16 * 9)
            for k in range(4):
                for n, dst in ((0, gam[k]), (1, bet[k])):
                    raw = gb_raw[:, 2 * (k >= 2) + n, 0:64 * COLS[k]]
                    raw = raw.rearrange("p (j w) -> p w j", w=COLS[k]) if k < 3 else columns(raw, k)
                    last = dve.tensor_scalar(columns(dst[:, :], k), raw, XS, None, ALU.mult)
            c.link(last)
            for k in (1, 2, 3, 4):
                dve.wait_ge(s_w, 16 * 4)
                dve.wait_ge(s_whi, k)
                dve.scalar_tensor_tensor(w_lo[k][:, :], w_raw[k], WS, w_hi[k][:, :], ALU.mult, ALU.subtract).then_inc(s_wlo, 1)
            dve.wait_ge(s_pad, 10)
            dve.tensor_tensor(centre[:, :], ident32[:, :], average[:, :], ALU.subtract)
            dve.wait_ge(s_ac, 16 * 3)
            dve.tensor_scalar(bias_k[:, :], acol[:, 1:2], 0.125, None, ALU.mult)
            c.link(dve.tensor_tensor(bias_i[:, :], acol[:, 3:4], acol[:, 6:7], ALU.add))
            dve.tensor_scalar(bias_i[:, :], bias_i[:, :], 0.2, None, ALU.mult)
            dve.tensor_scalar(bias_o[:, :], acol[:, 5:6], -1.0, None, ALU.mult).then_inc(s_acon, 1)

            def norm(k, i, in_sem, in_count, full_free, full_count):
                dve.wait_ge(in_sem, in_count)
                for b in range(GB):
                    last = dve.bn_stats(stats[k][:, b, :], source(k, b))
                c.link(last)
                even, odd = stats[k][:, :, 0:3], stats[k][:, :, 3:6]
                dve.tensor_tensor(spread[:, :], even[:, :, 2], odd[:, :, 2], ALU.add)
                dve.tensor_scalar(half_mean[:, :], even[:, :, 1], 0.5, None, ALU.mult)
                c.link(dve.tensor_tensor(gap[:, :], even[:, :, 1], odd[:, :, 1], ALU.subtract))
                dve.scalar_tensor_tensor(mean[k][:, :], odd[:, :, 1], 0.5, half_mean[:, :], ALU.mult, ALU.add)
                c.link(dve.tensor_tensor(gap2[:, :], gap[:, :], gap[:, :], ALU.mult))
                dve.scalar_tensor_tensor(var4[k][:, :], spread[:, :], 4.0 / (64 * COLS[k]), gap2[:, :],
                                         ALU.mult, ALU.add).then_inc(s_var[k], 1)
                dve.wait_ge(s_var[k], i + 1)
                for b in range(GB):
                    last = dve.scalar_tensor_tensor(columns(centred[:, b, 0:64 * COLS[k]], k), source(k, b), mean[k][:, b:b + 1],
                                                    columns(gam[k][:, :], k), ALU.subtract, ALU.mult)
                c.link(last)
                dve.wait_ge(s_rstd[k], i + 1)
                wait(dve, full_free, full_count)
                for b in range(GB):
                    last = dve.scalar_tensor_tensor(full_of(k)[:, :, b, :], columns(centred[:, b, 0:64 * COLS[k]], k),
                                                    rstd[k][:, b:b + 1], columns(bet[k][:, :], k), ALU.mult, ALU.add)
                last.then_inc(s_full[k], 1)

            def norm0(i):
                norm(0, i, s_x, i * 16 + 16, s_lo[2], i - 1)

            def norm1(i):
                norm(1, i, s_relu[1], i * 3 + 3, s_lo[3], i - 1)

            def norm3(i, norm1_done):
                norm(3, i, s_relu[3], i * 2 + 2, s_lo[1], norm1_done)

            def norm2(i, norm0_done):
                norm(2, i, s_relu[2], i * 2 + 2, s_lo[0], norm0_done)

            def bank2(name):
                return TILE[name][:, :, 0:HALF]

            def normed(g):
                dve.wait_ge(s_rs1, g + 1)
                wait(dve, filled["o"], g)
                dve.tensor_tensor(halves2("xn"), bank2("cx1"), halves2("rs"), ALU.mult).then_inc(s_xn, 1)

            def keep(g):
                dve.wait_ge(s_H, g * 2 + 2)
                dve.wait_ge(s_txt, g * 16 + 16)
                wait(dve, s_h2, g)
                dve.tensor_copy(A["resid"], A["tokens"]).then_inc(s_hres, 1)

            def gates(g):
                dve.wait_ge(filled["f"], g + 1)
                dve.tensor_scalar(halves2("t_f"), bank2("f"), acol[:, 4:5], 0.0, ALU.add, ALU.max).then_inc(s_fpos, 1)
                dve.wait_ge(s_fpos, g + 1)
                dve.wait_ge(s_l1, g + 1)
                dve.scalar_tensor_tensor(A["lf"], A["t_f"], -1.0, A["lf"], ALU.mult, ALU.subtract).then_inc(s_lf, 1)
                dve.wait_ge(s_ti, g + 1)
                dve.tensor_scalar(A["li"], A["li"], -20.0, 10.0, ALU.mult, ALU.add).then_inc(s_li, 1)

            def scans(g):
                dve.wait_ge(s_lf, g + 1)
                dve.wait_ge(s_li, g + 1)
                for p in range(GP):
                    last = dve.tensor_tensor_scan(m_ext[:, p, 1:S + 1], A["lf"][:, p, :], A["li"][:, p, :], 0.0, ALU.add, ALU.max)
                last.then_inc(s_m, 1)
                c.link(dve.tensor_tensor_scan(flat("cum"), not_start[:, :], flat("lf"), 0.0, ALU.mult, ALU.add))
                dve.wait_ge(s_m, g + 1)
                mids = [(lo + hi) // 2 for lo, hi in BLOCKS]
                for n in range(3):
                    last = dve.tensor_copy(mid[:, :, n:n + 1], A["cum"][:, :, mids[n]:mids[n] + 1])
                c.link(last)
                for n, (lo, hi) in enumerate(BLOCKS):
                    last = dve.tensor_tensor(A["cum"][:, :, lo:hi], A["cum"][:, :, lo:hi],
                                             mid[:, :, n:n + 1].to_broadcast([128, GP, hi - lo]), ALU.subtract)
                c.link(last)
                dve.tensor_tensor(A["wv"], A["li"], A["cum"], ALU.subtract).then_inc(s_e_arg, 1)
                for n in range(2):
                    end = BLOCKS[n][1] - 1
                    last = dve.tensor_tensor(s_arg[:, :, n:n + 1], A["cum"][:, :, end:end + 1], mid[:, :, n + 1:n + 2], ALU.add)
                last.then_inc(s_s_arg, 1)
                c.link(dve.tensor_tensor(A["t_f"], A["lf"], m_ext[:, :, 0:S], ALU.add))
                dve.tensor_tensor(A["t_f"], A["t_f"], m_ext[:, :, 1:S + 1], ALU.subtract).then_inc(s_fs_arg, 1)
                dve.tensor_tensor(A["t_i"], A["li"], m_ext[:, :, 1:S + 1], ALU.subtract).then_inc(s_is_arg, 1)
                wait(dve, s_g, g)
                dve.tensor_tensor(A["gexp"], A["cum"], m_ext[:, :, 1:S + 1], ALU.subtract).then_inc(s_garg, 1)

            def weigh(g):
                dve.wait_ge(s_e, g + 1)
                dve.wait_ge(s_v, g + 1)
                dve.tensor_tensor(A["wv"], A["wv"], A["vT"], ALU.mult).then_inc(s_vp, 1)
                dve.wait_ge(s_s, g + 1)
                c.link(dve.tensor_tensor(s_dec[:, :, 2:3], s_dec[:, :, 0:1], s_dec[:, :, 1:2], ALU.mult))

            def normalizer(g):
                dve.wait_ge(s_fs, g + 1)
                dve.wait_ge(s_is, g + 1)
                dve.wait_ge(s_k, g + 1)
                dve.memset(A["t_f"][:, :, 0:1], 0.0)
                c.link(dve.tensor_tensor(A["t_i"], A["t_i"], A["kT"], ALU.mult))
                wait(dve, filled["den"], g)
                c.link(dve.tensor_tensor_scan(flat("nq"), flat("t_f"), flat("t_i"), 0.0, ALU.mult, ALU.add))
                dve.wait_ge(s_q, g + 1)
                dve.tensor_tensor(A["nq"], A["nq"], A["qT"], ALU.mult).then_inc(s_nq, 1)

            def mask(g, n):
                dve.wait_ge(filled["sc"], g * 4 + (n + 1))
                if n == 0:
                    wait(dve, filled["hacc"], g * 2)
                tile = TILE[f"sc{n}"]
                dve.tensor_tensor(st[:, 2 * n:2 * n + 2, 0:S], tile[:, :, 0:S],
                                  causal[:, 0:S].unsqueeze(1).to_broadcast([128, 2, S]), ALU.mult)
                dve.tensor_tensor(st[0:T2, 2 * n:2 * n + 2, S:], tile[0:T2, :, S:S + T2],
                                  causal[0:T2, S:].unsqueeze(1).to_broadcast([T2, 2, T2]), ALU.mult).then_inc(s_st, 1)

            def denominator(g):
                dve.wait_ge(s_den, g + 1)
                dve.tensor_scalar(A["den"], A["den"], 1e-6, None, ALU.max).then_inc(s_dmax, 1)

            def exponent(g):
                dve.wait_ge(s_garg, g * 2 + 1)
                dve.wait_ge(s_og, g + 1)
                c.link(dve.tensor_tensor(A["gexp"], A["gexp"], A["o_log"], ALU.subtract))
                dve.wait_ge(s_lden, g + 1)
                dve.tensor_tensor(A["gexp"], A["gexp"], A["den"], ALU.subtract).then_inc(s_garg, 1)

            def combine(g, n):
                dve.wait_ge(filled["hacc"], g * 2 + (n + 1))
                tile, pairs = TILE[f"hacc{n}"], slice(2 * n, 2 * n + 2)
                def dec(k, width):
                    return s_dec[:, pairs, k:k + 1].to_broadcast([128, 2, width])
                own0 = tile[:, 0, 0:2 * S].rearrange("p (g s) -> p g s", g=2)
                own12 = tile[:, 1, 0:436].rearrange("p (g s) -> p g s", g=2)
                dve.tensor_tensor(u1[:, pairs, 64:128], own0[:, :, 64:128], dec(0, 64), ALU.mult)
                dve.tensor_tensor(u1[:, pairs, 128:S], own12[:, :, 64:141], dec(1, T2), ALU.mult)
                c.link(dve.tensor_tensor(u2[:, pairs, :], own0[:, :, 128:S], dec(2, T2), ALU.mult))
                dve.tensor_tensor(u1[:, pairs, 64:128], own12[:, :, 0:64], u1[:, pairs, 64:128], ALU.add)
                c.link(dve.tensor_tensor(u1[:, pairs, 128:S], u1[:, pairs, 128:S], u2[:, pairs, :], ALU.add))
                c.link(dve.tensor_tensor(u1[:, pairs, 128:S], own12[:, :, 141:218], u1[:, pairs, 128:S], ALU.add))
                if n == 0:
                    dve.wait_ge(s_g, g + 1)
                dve.tensor_tensor(A["h"][:, pairs, 0:64], own0[:, :, 0:64], A["gexp"][:, pairs, 0:64], ALU.mult)
                dve.tensor_tensor(A["h"][:, pairs, 64:S], u1[:, pairs, 64:S], A["gexp"][:, pairs, 64:S], ALU.mult).then_inc(s_h, 1)

            def residual(g):
                dve.wait_ge(s_rs2, g + 1)
                c.link(dve.tensor_tensor(A["h"], A["h"], A["rs"], ALU.mult))
                dve.wait_ge(s_hres, g + 1)
                wait(dve, filled["tm"], g * 2)
                dve.scalar_tensor_tensor(A["h2"], A["h"], acol[:, 7:8], A["resid"], ALU.mult, ALU.add).then_inc(s_h2, 1)

            def normed2(g):
                dve.wait_ge(s_rs3, g + 1)
                wait(dve, filled["lg"], g)
                dve.tensor_tensor(halves2("xn2"), bank2("cx3"), halves2("rs"), ALU.mult).then_inc(s_xn2, 1)

            def turned_copy(g):
                dve.wait_ge(filled["tm"], g * 2 + 1)
                wait(dve, s_sav, g * 32)
                copy_turned(dve.tensor_copy, 0).then_inc(s_tmD, 1)

            def logits(g):
                dve.wait_ge(filled["lg"], g + 1)
                tile = TILE["lg"][:, 0, 0:256].rearrange("p (s b e) -> p s b e", s=2, b=GB)
                for s_, (dst, rows) in enumerate(((tm0, 128), (tm1, T2))):
                    last = dve.tensor_tensor(dst[0:rows, :, 128:144], tile[0:rows, s_],
                                             gate_bias[0:rows, :].unsqueeze(1).to_broadcast([rows, GB, 16]), ALU.add)
                last.then_inc(s_lg, 1)

            norm0(0)

            def turn(t):
                if on(t - 3):
                    residual(t - 3)
                    normed2(t - 3)
                if on(t - 2):
                    normed(t - 2)
                    keep(t - 2)
                if on(t):
                    norm1(t)
                if on(t + 1):
                    norm0(t + 1)
                if on(t - 3):
                    turned_copy(t - 3)
                    logits(t - 3)
                if on(t - 2):
                    gates(t - 2)
                    scans(t - 2)
                if on(t - 1):
                    norm3(t - 1, t + 1 if on(t) else NG)
                if on(t - 2):
                    normalizer(t - 2)
                    weigh(t - 2)
                    for n in range(4):
                        mask(t - 2, n)
                    denominator(t - 2)
                    exponent(t - 2)
                if on(t):
                    norm2(t, t + 2 if on(t + 1) else NG)
                if on(t - 2):
                    for n in range(2):
                        combine(t - 2, n)

            turns(dve, c, DVE_LINKS, turn)

            dve.wait_ge(s_fw, 16 * 9)
            dve.wait_ge(s_fhi, 3)
            dve.scalar_tensor_tensor(fw1_lo, raw1, FW_SCALE, fw1_hi, ALU.mult, ALU.subtract).then_inc(s_fmade, 1)
            dve.scalar_tensor_tensor(fw2_lo, raw2, FW_SCALE, fw2_hi, ALU.mult, ALU.subtract).then_inc(s_fmade, 1)
            c.link(dve.scalar_tensor_tensor(rawb[0:2, :], rawb[0:2, :], FW_SCALE, fb2[0:2, :], ALU.mult, ALU.subtract))
            c.link(dve.tensor_scalar(rawb[0:2, :], rawb[0:2, :], row_sel[:, 1:2], None, ALU.mult))
            dve.scalar_tensor_tensor(fb2[0:2, :], fb2[0:2, :], row_sel[:, 0:1], rawb[0:2, :], ALU.mult, ALU.add).then_inc(s_fmade, 1)
            dve.memset(ones_h[:, :], H_SCALE)
            dve.tensor_scalar(fb1s[:, :], fb1[:, :], H_SCALE, None, ALU.mult).then_inc(s_fmade, 1)

            dve.wait_ge(s_lgin, 16)
            for k in range(2):
                c.link(dve.tensor_reduce(top[k], logit, AX.X, ALU.max))
                c.link(dve.tensor_tensor(work_te, logit, top[k].unsqueeze(2).to_broadcast([128, S, E]), ALU.is_equal))
                c.link(dve.tensor_tensor(work_te, work_te, e_minus[:, :].unsqueeze(1).to_broadcast([128, S, E]), ALU.mult))
                c.link(dve.tensor_reduce(which, work_te, AX.X, ALU.min))
                c.link(dve.tensor_tensor(chosen[k], e_minus[:, :].unsqueeze(1).to_broadcast([128, S, E]),
                                         which.unsqueeze(2).to_broadcast([128, S, E]), ALU.is_equal))
                if k == 0:
                    c.link(dve.scalar_tensor_tensor(logit, chosen[0], -1e30, logit, ALU.mult, ALU.add))
            dve.tensor_tensor(gate[1], top[1], top[0], ALU.subtract).then_inc(s_gexp, 1)
            dve.memset(ones_s, 1.0)
            c.link(dve.tensor_tensor(work_et, chosen[0].rearrange("p t e -> p e t"), chosen[1].rearrange("p t e -> p e t"), ALU.add))
            for e in range(E):
                last = dve.tensor_tensor_scan(rank[:, e, :], ones_s, work_et[:, e, :], 0.0, ALU.mult, ALU.add)
            c.link(last)
            dve.tensor_copy(counts[:, :], rank[:, :, S - 1]).then_inc(s_cnt, 1)
            dve.wait_ge(s_off, 1)
            dve.tensor_copy(off[:, :], double[0][:, 0, 0:E])
            c.link(dve.tensor_scalar(tiles_i[:, :], double[0][:, 0, E:2 * E], 127.0, None, ALU.add))
            c.link(dve.tensor_scalar(tiles_i[:, :], tiles_i[:, :], 7, None, ALU.logical_shift_right))
            c.link(dve.tensor_copy(tiles_e[:, :], tiles_i[:, :]))
            c.link(dve.tensor_tensor_scan(ends[:, :], ones_s[:, 0:E], tiles_e[:, :], 0.0, ALU.mult, ALU.add))
            c.link(dve.tensor_tensor(tiles_e[:, :], ends[:, :], tiles_e[:, :], ALU.subtract))
            c.link(dve.scalar_tensor_tensor(off[:, :], tiles_e[:, :], 128.0, off[:, :], ALU.mult, ALU.add))
            c.link(dve.tensor_scalar(off[:, :], off[:, :], -1.0, None, ALU.add))
            c.link(dve.tensor_tensor(rank, rank, off[:, :].unsqueeze(2).to_broadcast([128, E, S]), ALU.add))
            for k in range(2):
                c.link(dve.tensor_tensor(work_te, chosen[k], rank.rearrange("p e t -> p t e"), ALU.mult))
                c.link(dve.tensor_reduce(slot_f, work_te, AX.X, ALU.add))
                dve.tensor_copy(slot[k], slot_f).then_inc(s_slot, 1)
            c.link(dve.memset(tile_exp, 0.0))
            dve.wait_ge(s_tmap, 1)
            for e in range(E):
                c.link(dve.scalar_tensor_tensor(tile_exp, tile_no, ends[:, e:e + 1], tile_exp, ALU.is_ge, ALU.add))
            dve.tensor_scalar(tile_i[:, :], tile_exp, float(E - 1), None, ALU.min).then_inc(s_tmap, 1)
            dve.wait_ge(s_gexp2, 1)
            c.link(dve.tensor_scalar(gate[0], gate[1], 1.0, None, ALU.add))
            c.link(dve.reciprocal(gate[0], gate[0]))
            c.link(dve.tensor_tensor(gate[1], gate[1], gate[0], ALU.mult))

            def quad(q, h):
                dve.wait_ge(s_xhi, q + 1)
                dve.scalar_tensor_tensor(xT[h][64:128, :], double[0][0:64, h, :], XS, xT[h][0:64, :], ALU.mult, ALU.subtract).then_inc(s_xlo, 1)
                dve.wait_ge(s_hhi, q + 1)
                dve.tensor_tensor(hid_lo[h], hid[h], hid_hi[h], ALU.subtract).then_inc(s_hlo, 1)
                dve.wait_ge(s_mm2, q + 1)
                if not isinstance(q, int) or q >= 2:
                    dve.wait_ge(s_ost[h], half_of(q, h) * 16)
                dve.tensor_scalar(o_tiles[h], double[2][:, h, 0:256].rearrange("p (n f) -> p n f", f=D_),
                                  1.0 / (H_SCALE * FW_SCALE), None, ALU.mult).then_inc(s_o, 1)

            quads(dve, quad)

            for k in range(CHUNKS):
                for h, (lo, hi) in enumerate(PARTS):
                    r, n = slice(lo, hi), hi - lo
                    o = slice(k * CH + lo, k * CH + hi)
                    dve.wait_ge(s_got[h], 16 * 2 * n * (k + 1))
                    def over(v):
                        return v.unsqueeze(2).to_broadcast([128, n, D_])
                    for m in range(2):
                        last = dve.tensor_tensor(got[:, r, m, :], got[:, r, m, :], over(gate[m][:, o]), ALU.mult)
                    c.link(last)
                    if k:
                        dve.wait_ge(s_out2[h], 16 * k)
                    c.link(dve.tensor_tensor(y[:, r], got[:, r, 0, :], got[:, r, 1, :], ALU.add))
                    dve.wait_ge(s_strm[h], 16 * (k + 1))
                    c.link(dve.tensor_tensor(y[:, r], y[:, r], stream[:, r, 0, :], ALU.add))
                    c.link(dve.tensor_reduce(y_mean[:, r], y[:, r], AX.X, ALU.add))
                    c.link(dve.tensor_scalar(y_mean[:, r], y_mean[:, r], 1.0 / D_, None, ALU.mult))
                    c.link(dve.tensor_tensor(y[:, r], y[:, r], over(y_mean[:, r]), ALU.subtract))
                    c.link(dve.tensor_tensor(got[:, r, 0, :], y[:, r], y[:, r], ALU.mult))
                    dve.tensor_reduce(y_var[:, r], got[:, r, 0, :], AX.X, ALU.add).then_inc(s_yvar, 1)
                    dve.wait_ge(s_yr, 2 * k + h + 1)
                    c.link(dve.tensor_tensor(y[:, r], y[:, r], over(y_rstd[:, r]), ALU.mult))
                    c.link(dve.tensor_tensor(y[:, r], y[:, r], ff_gb[:, 0, :].unsqueeze(1).to_broadcast([128, n, D_]), ALU.mult))
                    c.link(dve.tensor_tensor(y[:, r], y[:, r], ff_gb[:, 1, :].unsqueeze(1).to_broadcast([128, n, D_]), ALU.add))
                    dve.tensor_tensor(y[:, r], y[:, r], stream[:, r, 1, :], ALU.add).then_inc(s_yout[h], 1)

        @block.scalar
        def _(act):
            c = Chain(act, s_act)
            act.preload_act_table_set("natural_log_exp_and_others")
            act.wait_ge(s_w, 16 * 4)
            for k in (1, 2, 3, 4):
                act.activation(w_hi[k][:, :], w_raw[k], ACT.Copy, scale=WS).then_inc(s_whi, 1)
            act.wait_ge(s_c, 16 * 9)

            def norm(k, i, free, count):
                act.wait_ge(s_var[k], i + 1)
                c.link(act.activation(lnv[k][:, :], var4[k][:, :], ACT.Ln, bias=eps[:, 0:1], scale=0.25))
                act.activation(rstd[k][:, :], lnv[k][:, :], ACT.Exp, scale=-0.5).then_inc(s_rstd[k], 1)
                act.wait_ge(s_full[k], i + 1)
                wait(act, free, count)
                for b in range(COLS[k]):
                    last = act.activation(halves(k, 0)[:, b], full_of(k)[:, b], ACT.Copy)
                last.then_inc(s_hi[k], 1)

            def relu(k, i, w):
                n = COLS[k]
                act.wait_ge(s_conv[k], i * n + (w + 1))
                if w == 0:
                    wait(act, s_full[k], i)
                dst = h_relu[k][:, w] if k < 3 else h_relu[3][:, :, w]
                src = TILE[f"c{k}{w}"][:, :].rearrange("p (b j) -> p b j", b=GB)
                bias = (0, 0, 1, 2 + w)[k]
                act.activation(dst, src, ACT.Relu, bias=cb[:, bias:bias + 1], scale=UNSCALE).then_inc(s_relu[k], 1)

            def turned(i):
                act.wait_ge(s_turn, i + 1)
                wait(act, s_tok, i)
                act.activation(resT[:, :].rearrange("p h b t -> p h (b t)"), TILE["turned"][:, :, :].bitcast(F16), ACT.Copy).then_inc(s_rT, 1)

            def tokens(i):
                act.wait_ge(s_tok, i + 1)
                wait(act, s_hres, i)
                for h in range(2):
                    q = slice(64 * h, 64 * h + 64)
                    act.activation(A["tokens"][q, :, 0:T], TILE["tok"][q, 0, :].rearrange("p (b t) -> p b t", b=GP),
                                   ACT.Identity, bias=cb[q, 4:5], scale=UNSCALE).then_inc(s_H, 1)

            def bank2(name):
                return TILE[name][:, :, 0:HALF]

            def square(g, name, sem_in, sem_out):
                act.wait_ge(sem_in, g + 1)
                src = halves2("h") if name == "h" else bank2(name)
                act.activation(halves2("sq"), src, ACT.Square).then_inc(sem_out, 1)

            def inverse_root(g, name, sem_out, e):
                act.wait_ge(filled[name], g + 1)
                c.link(act.activation(halves2("rs"), bank2(name), ACT.Ln, bias=e[:, 0:1]))
                act.activation(A["rs"], A["rs"], ACT.Exp, scale=-0.5).then_inc(sem_out, 1)

            def forget(g):
                act.wait_ge(s_fpos, g + 1)
                wait(act, s_fs_arg, g)
                c.link(act.activation(halves2("lf"), bank2("f"), ACT.Abs, bias=acol[:, 4:5]))
                c.link(act.activation(A["lf"], A["lf"], ACT.Exp, scale=-1.0))
                act.activation(A["lf"], A["lf"], ACT.Ln, bias=one[:, 0:1]).then_inc(s_l1, 1)

            def inputs(g):
                act.wait_ge(filled["i"], g + 1)
                wait(act, s_is_arg, g)
                c.link(act.activation(halves2("li"), bank2("i"), ACT.Exp, bias=bias_i[:, 0:1], scale=0.2))
                c.link(act.activation(A["li"], A["li"], ACT.Ln, bias=one[:, 0:1]))
                act.activation(A["li"], A["li"], ACT.Exp, scale=-1.0).then_inc(s_ti, 1)

            def project(g, name, dst, bias, scale, sem_out, free, count):
                act.wait_ge(filled[name], g + 1)
                wait(act, free, count)
                act.activation(halves2(dst), bank2(name), ACT.Identity, bias=bias, scale=scale).then_inc(sem_out, 1)

            def output_gate(g):
                act.wait_ge(filled["o"], g + 1)
                wait(act, s_garg, g * 2)
                c.link(act.activation(halves2("o_log"), bank2("o"), ACT.Exp, bias=bias_o[:, 0:1], scale=-1.0))
                act.activation(A["o_log"], A["o_log"], ACT.Ln, bias=one[:, 0:1]).then_inc(s_og, 1)

            def exp_in_place(g, name, sem_in, count, sem_out, free=None, free_count=0):
                act.wait_ge(sem_in, count)
                act.activation(A[name], A[name], ACT.Exp).then_inc(sem_out, 1)

            def decays(g):
                act.wait_ge(s_s_arg, g + 1)
                wait(act, s_h, g * 2)
                act.activation(s_dec[:, :, 0:2], s_arg[:, :, :], ACT.Exp).then_inc(s_s, 1)

            def values(g):
                act.wait_ge(filled["vt"], g + 1)
                wait(act, filled["hacc"], g * 2)
                tile = TILE["vt"][:, :, :].rearrange("p c (g s) -> p c g s", g=2)
                act.activation(vt[:, :, 0:128].rearrange("p (c g) s -> p c g s", g=2), tile[:, :, :, 0:128], ACT.Copy)
                act.activation(vt[0:T2, :, 128:256].rearrange("p (c g) s -> p c g s", g=2), tile[0:T2, :, :, 128:256],
                               ACT.Copy).then_inc(s_vt, 1)

            def abs_den(g):
                act.wait_ge(filled["den"], g + 1)
                wait(act, s_garg, g * 2)
                act.activation(halves2("den"), bank2("den"), ACT.Abs).then_inc(s_den, 1)

            def log_den(g):
                act.wait_ge(s_dmax, g + 1)
                act.activation(A["den"], A["den"], ACT.Ln).then_inc(s_lden, 1)

            def turned_copy(g):
                act.wait_ge(filled["tm"], g * 2 + 2)
                wait(act, s_sav, g * 32)
                copy_turned(lambda o, i: act.activation(o, i, ACT.Copy), 1).then_inc(s_tmA, 1)

            norm(0, 0, s_conv[1], 0)
            act.wait_ge(s_acon, 1)

            def turn(t):
                if on(t):
                    relu(1, t, 0)
                if on(t - 2):
                    tokens(t - 2)
                if on(t - 3):
                    inverse_root(t - 3, "ms", s_rs2, eps8)
                if on(t):
                    relu(1, t, 1)
                if on(t - 3):
                    square(t - 3, "cx3", filled["cx3"], s_sq3)
                    inverse_root(t - 3, "var3", s_rs3, eps)
                if on(t - 2):
                    square(t - 2, "cx1", filled["cx1"], s_sq1)
                    if on(t - 3):
                        act.wait_ge(s_xn2, t - 2)
                    inverse_root(t - 2, "var1", s_rs1, eps)
                if on(t):
                    relu(1, t, 2)
                    norm(1, t, s_conv[2], t * 2)
                if on(t + 1):
                    norm(0, t + 1, s_conv[1], t * 3 + 3)
                if on(t - 1):
                    relu(3, t - 1, 0)
                if on(t - 3):
                    turned_copy(t - 3)
                if on(t - 2):
                    forget(t - 2)
                    inputs(t - 2)
                    project(t - 2, "k", "kT", bias_k[:, 0:1], 0.125, s_k, filled["sc"], (t - 2) * 4)
                    project(t - 2, "v", "vT", acol[:, 2:3], 1.0, s_v, s_vp, t - 2)
                    project(t - 2, "q", "qT", acol[:, 0:1], 1.0, s_q, filled["sc"], (t - 2) * 4)
                    output_gate(t - 2)
                if on(t - 1):
                    relu(3, t - 1, 1)
                if on(t - 2):
                    exp_in_place(t - 2, "wv", s_e_arg, t - 1, s_e)
                    decays(t - 2)
                    exp_in_place(t - 2, "t_f", s_fs_arg, t - 1, s_fs)
                    exp_in_place(t - 2, "t_i", s_is_arg, t - 1, s_is)
                if on(t - 1):
                    norm(3, t - 1, s_turn, t - 1)
                if on(t):
                    relu(2, t, 0)
                if on(t - 2):
                    abs_den(t - 2)
                    values(t - 2)
                    log_den(t - 2)
                    exp_in_place(t - 2, "gexp", s_garg, (t - 2) * 2 + 2, s_g)
                if on(t):
                    relu(2, t, 1)
                    norm(2, t, s_conv[3], t * 2)
                if on(t - 1):
                    turned(t - 1)
                if on(t - 2):
                    act.wait_ge(s_h, (t - 2) * 2 + 2)
                    act.activation(halves2("sq"), halves2("h"), ACT.Square).then_inc(s_sq2, 1)

            turns(act, c, ACT_LINKS, turn)

            act.wait_ge(s_fw, 16 * 9)
            act.activation(fw1_hi, raw1, ACT.Copy, scale=FW_SCALE).then_inc(s_fhi, 1)
            act.activation(fw2_hi, raw2, ACT.Copy, scale=FW_SCALE).then_inc(s_fhi, 1)
            act.activation(fb2[0:2, :], rawb[0:2, :], ACT.Copy, scale=FW_SCALE).then_inc(s_fhi, 1)
            act.wait_ge(s_gexp, 1)
            act.activation(gate[1], gate[1], ACT.Exp).then_inc(s_gexp2, 1)
            act.wait_ge(s_fmade, 4)
            act.wait_ge(s_tmap, 2)

            def quad(q, h):
                experts = [act.value_load(tile_i[0:1, bass.ds(q * 4 + n, 1)], min_val=0, max_val=E - 1) for n in range(4)]
                act.wait_ge(s_xturn, q + 1)
                if not isinstance(q, int) or q >= 2:
                    act.wait_ge(s_mm1, q + (-1))
                act.activation(xT[h][0:64, :], double[0][0:64, h, :], ACT.Copy, scale=XS).then_inc(s_xhi, 1)
                act.wait_ge(s_mm1, q + 1)
                if not isinstance(q, int) or q >= 2:
                    act.wait_ge(s_hlo, q + (-1))
                for n in range(4):
                    e = experts[n]
                    last = act.activation(hid[h][:, 128 * n:128 * n + 128], double[1][:, h, 128 * n:128 * n + 128], ACT.Relu,
                                          bias=fb1s[:, bass.ds(e, 1)], scale=H_SCALE / (XS * FW_SCALE))
                last.then_inc(s_hid, 1)
                act.wait_ge(s_hid, q + 1)
                if not isinstance(q, int) or q >= 2:
                    act.wait_ge(s_mm2, q + (-1))
                act.activation(hid_hi[h], hid[h], ACT.Copy).then_inc(s_hhi, 1)

            quads(act, quad)
            for k in range(CHUNKS):
                for h, (lo, hi) in enumerate(PARTS):
                    r = slice(lo, hi)
                    act.wait_ge(s_yvar, 2 * k + h + 1)
                    c.link(act.activation(y_rstd[:, r], y_var[:, r], ACT.Ln, bias=eps[:, 0:1], scale=1.0 / D_))
                    act.activation(y_rstd[:, r], y_rstd[:, r], ACT.Exp, scale=-0.5).then_inc(s_yr, 1)

        @block.gpsimd
        def _(pool):
            for n in PROJ:
                pool.memset(w_proj[n][:, :], 0.0)
            pool.memset(zeros[:, :], 0.0)
            pool.memset(w_gate[:, :], 0.0).then_inc(s_az, 1)
            pool.iota(e_minus[:, :], pattern=[[1, E]], base=-E, channel_multiplier=0, allow_small_or_imprecise_dtypes=True)
            pool.memset(before[:, :], 1.0)
            pool.memset(all_ones[:, :], 1.0)
            for k, t in enumerate((act1, act2, act3)):
                v = t[:, :, :, :, :].rearrange("p h w b j -> p (h w b) j")
                pool.memset(v[:, :, 0:2], 0.0)
                pool.memset(v[:, :, 2 + J:JP], 0.0)
            pool.memset(average[:, :], 0.0)
            pool.memset(total[:, :], 0.0)
            pool.memset(causal[:, :], 1.0)
            pool.memset(ident32[:, :], 0.0)
            pool.memset(ident[:, :], 0.0).then_inc(s_pad, 1)
            pool.wait_ge(s_pad, 1)
            for h in range(2):
                q = slice(64 * h, 64 * h + 64)
                pool.memset(average[q, q], 1.0 / 64).then_inc(s_pad, 1)
                pool.wait_ge(s_pad, 2 + 2 * h)
                pool.memset(total[q, q], 1.0).then_inc(s_pad, 1)
                pool.wait_ge(s_pad, 3 + 2 * h)
            for m in (ident, ident32):
                pool.affine_select(out=m[:, :], in_=m[:, :], compare_op=ALU.not_equal, fill=1.0, base=0,
                                   pattern=[[-1, 128]], channel_multiplier=1).then_inc(s_pad, 1)
            for lo, n in ((0, S), (S, T2)):
                pool.affine_select(out=causal[:, lo:lo + n], in_=causal[:, lo:lo + n], compare_op=ALU.is_ge, fill=0.0, base=0,
                                   pattern=[[1, n]], channel_multiplier=-1).then_inc(s_pad, 1)
            pool.affine_select(out=before[:, :], in_=before[:, :], compare_op=ALU.is_gt, fill=0.0, base=0,
                               pattern=[[1, 128]], channel_multiplier=-1).then_inc(s_pad, 1)
            pool.wait_ge(s_pad, 10)

            def low(k, i, free, count):
                pool.wait_ge(s_hi[k], i + 1)
                wait(pool, free, count)
                for w in range(COLS[k]):
                    last = pool.tensor_tensor(halves(k, 1)[:, w], full_of(k)[:, w], halves(k, 0)[:, w], ALU.subtract)
                last.then_inc(s_lo[k], 1)

            low(0, 0, s_conv[1], 0)

            def turn(t):
                if on(t):
                    low(1, t, s_conv[2], t * 2)
                if on(t + 1):
                    low(0, t + 1, s_conv[1], t * 3 + 3)
                if on(t - 1):
                    low(3, t - 1, s_turn, t - 1)
                if on(t):
                    low(2, t, s_conv[3], t * 2)

            turns(pool, None, 0, turn)

            pool.wait_ge(s_lgin, 16)
            pool.iota(tile_no, pattern=[[1, TILES]], base=0, channel_multiplier=0, allow_small_or_imprecise_dtypes=True).then_inc(s_tmap, 1)
            pool.wait_ge(s_slot, 2)
            pool.wait_ge(s_zero, 16 * -(-ROWS // 1024))
            for k in range(CHUNKS):
                for h, (lo, hi) in enumerate(PARTS):
                    pool.wait_ge(s_xpart[h], 16 * (k + 1))
                    for t in range(lo, hi):
                        for m in range(2):
                            pool.indirect_dma_start(xs_dram, bass.IndirectOffsetOnAxis(ap=slot[m][:, k * CH + t:k * CH + t + 1], axis=0),
                                                    xn_part[:, t, :], None).then_inc(s_scat[h], 16)
            pool.wait_ge(s_done, 1)
            for k in range(CHUNKS):
                for h, (lo, hi) in enumerate(PARTS):
                    if k:
                        pool.wait_ge(s_yvar, 2 * k + h - 1)
                    for t in range(lo, hi):
                        for m in range(2):
                            pool.indirect_dma_start(got[:, t, m, :], None, es_dram,
                                                    bass.IndirectOffsetOnAxis(ap=slot[m][:, k * CH + t:k * CH + t + 1], axis=0)).then_inc(s_got[h], 16)

        @block.tensor
        def _(pe):
            def conv(k, i, w):
                wide = 2 * T if k == 3 else T
                src = (act1, act2, act3)[k - 1]
                if k == 1:
                    taps = [(kh, w_in - w + 1, w_in) for w_in in range(3) if 0 <= w_in - w + 1 < 3 for kh in range(5)]
                elif k == 2:
                    taps = [(kh, kw, w + kw) for kw in range(2) for kh in range(5)]
                else:
                    taps = [(kh, kw, kw) for kw in range(2) for kh in range(5)]
                kws = 3 if k == 1 else 2
                pe.wait_ge(s_lo[k - 1], i + 1)
                dst = take(pe, f"c{k}{w}", i)[:, :].rearrange("p (b j) -> p b j", b=GB)
                n, last_n = 0, 3 * len(taps) - 1
                for kh, kw, w_in in taps:
                    o = (kh * kws + kw) * wide + (w * T if k == 3 else 0)
                    for wt, half in ((w_hi, 0), (w_hi, 1), (w_lo, 0)):
                        mm = pe.matmul(dst, wt[k][:, o:o + T], src[:, half, w_in, :, kh:kh + J], start=(n == 0), stop=(n == last_n))
                        n += 1
                mm.then_inc(s_conv[k], 1)

            def turn_result(i):
                pe.wait_ge(s_lo[3], i + 1)
                tile = take(pe, "turned", i)
                for h in range(2):
                    for b in range(GB):
                        mm = pe.transpose(tile[:, h, :].bitcast(F16)[:, 128 * b:128 * b + 128], res[:, h, b, :], ident[:, :])
                mm.then_inc(s_turn, 1)

            def tokens(i):
                pe.wait_ge(s_rT, i + 1)
                tile = take(pe, "tok", i)
                for q in range(2):
                    for n, (wt, half) in enumerate(((w_hi, 0), (w_hi, 1), (w_lo, 0))):
                        mm = pe.matmul(tile[64 * q:64 * q + 64, 0, :].rearrange("p (b t) -> p b t", b=4), wt[4][:, :],
                                       resT[:, half].rearrange("p (b q) t -> p q b t", q=2)[:, q], start=(n == 0), stop=(n == 2))
                mm.then_inc(s_tok, 1)

            def product(g, name, weights, src):
                tile = take(pe, name, g)
                for n in range(2):
                    mm = pe.matmul(tile[:, n, 0:HALF], weights[:, :], halves2(src)[:, n], start=True, stop=True)
                mm.then_inc(filled[name], 1)

            def scores(g, n):
                if n == 0:
                    pe.wait_ge(s_k, g + 1)
                    pe.wait_ge(s_q, g + 1)
                tile = take(pe, f"sc{n}", g)
                for h in range(2):
                    q = slice(64 * h, 64 * h + 64)
                    k_, q_ = A["kT"][q, n, :], A["qT"][q, n, :]
                    pe.matmul(tile[:, h, 0:S], k_[:, 0:128], q_, start=True, stop=True)
                    mm = pe.matmul(tile[0:T2, h, S:S + T2], k_[:, 128:S], q_[:, 128:S], start=True, stop=True)
                mm.then_inc(filled["sc"], 1)

            def turn_values(g):
                pe.wait_ge(s_vp, g + 1)
                tile = take(pe, "vt", g)
                for p in range(GP):
                    o = 256 * (p % 2)
                    pe.transpose(tile[:, p // 2, o:o + 128], A["wv"][:, p, 0:128], ident32[:, :])
                    mm = pe.transpose(tile[0:T2, p // 2, o + 128:o + 256], A["wv"][:, p, 128:S], ident32[:, :])
                mm.then_inc(filled["vt"], 1)

            def sums(g, n):
                pe.wait_ge(s_vt, g + 1)
                pe.wait_ge(s_st, g * 4 + 4)
                tile = take(pe, f"hacc{n}", g)
                for c_ in range(2):
                    p = 2 * n + c_
                    for h in range(2):
                        o = slice(64 * h, 64 * h + 64)
                        b = 2 * p + h
                        v0, v1, v2 = (vt[r, p, 128 * s_ + 64 * h:128 * s_ + 64 * h + 64]
                                      for r, s_ in ((slice(0, 64), 0), (slice(64, 128), 0), (slice(0, T2), 1)))
                        at = 218 * c_
                        pe.matmul(tile[o, 1, at + 141:at + 218], v2, st[0:T2, b, S:S + T2], start=True, stop=True)
                        pe.matmul(tile[o, 0, S * c_:S * c_ + S], v0, st[0:64, b, 0:S], start=True, stop=True)
                        mm = pe.matmul(tile[o, 1, at:at + 141], v1, st[64:128, b, 64:S], start=True, stop=True)
                mm.then_inc(filled["hacc"], 1)

            def turn_tokens(g, n):
                tile = take(pe, f"tm{n}", g)
                for c_ in range(2):
                    for k, name in enumerate(("xn2", "h2")):
                        src = A[name][:, 2 * n + c_, :]
                        pe.transpose(tile[:, c_, 256 * k:256 * k + 128], src[:, 0:128], ident32[:, :])
                        mm = pe.transpose(tile[0:T2, c_, 256 * k + 128:256 * k + 256], src[:, 128:S], ident32[:, :])
                mm.then_inc(filled["tm"], 1)

            def logits(g):
                tile = take(pe, "lg", g)
                for p in range(GP):
                    src = A["xn2"][:, p, :]
                    pe.matmul(tile[:, 0, 32 * p:32 * p + 32], src[:, 0:128], w_gate[:, :], start=True, stop=True)
                    mm = pe.matmul(tile[0:T2, 0, 128 + 32 * p:160 + 32 * p], src[:, 128:S], w_gate[:, :], start=True, stop=True)
                mm.then_inc(filled["lg"], 1)

            pe.wait_ge(s_wlo, 4)
            pe.wait_ge(s_pad, 10)
            pe.wait_ge(s_acon, 1)
            pe.wait_ge(s_aw, 16 * 14)

            def turn(t):
                if on(t):
                    conv(1, t, 0)
                if on(t - 2):
                    tokens(t - 2)
                if on(t - 3):
                    pe.wait_ge(s_sq2, t - 2)
                    product(t - 3, "ms", average, "sq")
                if on(t):
                    conv(1, t, 1)
                if on(t - 3):
                    pe.wait_ge(s_h2, t - 2)
                    product(t - 3, "cx3", centre, "h2")
                if on(t - 2):
                    pe.wait_ge(s_H, (t - 2) * 2 + 2)
                    pe.wait_ge(s_txt, (t - 2) * 16 + 16)
                    product(t - 2, "cx1", centre, "tokens")
                if on(t):
                    conv(1, t, 2)
                if on(t - 3):
                    pe.wait_ge(s_sq3, t - 2)
                    product(t - 3, "var3", average, "sq")
                if on(t - 2):
                    pe.wait_ge(s_sq1, t - 1)
                    product(t - 2, "var1", average, "sq")
                if on(t - 1):
                    conv(3, t - 1, 0)
                if on(t - 3):
                    pe.wait_ge(s_xn2, t - 2)
                    for n in range(2):
                        turn_tokens(t - 3, n)
                    logits(t - 3)
                if on(t - 2):
                    pe.wait_ge(s_xn, t - 1)
                    for name in PROJ:
                        product(t - 2, name, w_proj[name], "xn")
                if on(t - 1):
                    conv(3, t - 1, 1)
                if on(t - 2):
                    for n in range(4):
                        scores(t - 2, n)
                if on(t):
                    conv(2, t, 0)
                if on(t - 2):
                    pe.wait_ge(s_nq, t - 1)
                    product(t - 2, "den", total, "nq")
                    turn_values(t - 2)
                if on(t):
                    conv(2, t, 1)
                if on(t - 2):
                    for n in range(2):
                        sums(t - 2, n)
                if on(t - 1):
                    turn_result(t - 1)

            turns(pe, None, 0, turn)

            pe.wait_ge(s_cnt, 1)
            pe.matmul(double[0][:, 0, 0:E], before[:, :], counts[:, :], start=True, stop=True)
            pe.matmul(double[0][:, 0, E:2 * E], all_ones[:, :], counts[:, :], start=True, stop=True).then_inc(s_off, 1)
            pe.wait_ge(s_fmade, 4)
            pe.wait_ge(s_tmap, 2)

            def quad(q, h):
                experts = [pe.value_load(tile_i[0:1, bass.ds(q * 4 + n, 1)], min_val=0, max_val=E - 1) for n in range(4)]
                pe.wait_ge(s_xt[h], half_of(q, h) * 16 + 16)
                if not isinstance(q, int) or q >= 2:
                    pe.wait_ge(s_xlo, q + (-1))
                for n in range(4):
                    mm = pe.matmul(double[0][0:64, h, 128 * n:128 * n + 128], x_tiles[h][:, n, :], ident32[:, :], start=True, stop=True)
                mm.then_inc(s_xturn, 1)
                pe.wait_ge(s_xlo, q + 1)
                if not isinstance(q, int) or q >= 2:
                    pe.wait_ge(s_hid, q + (-1))
                for n in range(4):
                    e = experts[n]
                    dst, x_ = double[1][:, h, 128 * n:128 * n + 128], xT[h][:, 128 * n:128 * n + 128]
                    pe.matmul(dst, fw1_hi[:, bass.ds(e * F, F)], x_, start=True, stop=False)
                    mm = pe.matmul(dst, fw1_lo[:, bass.ds(e * F, F)], x_, start=False, stop=True)
                mm.then_inc(s_mm1, 1)
                pe.wait_ge(s_hlo, q + 1)
                if not isinstance(q, int) or q >= 2:
                    pe.wait_ge(s_o, q + (-1))
                for n in range(4):
                    e = experts[n]
                    dst, c_ = double[2][:, h, 64 * n:64 * n + 64], slice(128 * n, 128 * n + 128)
                    w_ = bass.ds(e * D_, D_)
                    pe.matmul(dst, hid_hi[h][:, c_], fw2_hi[:, w_], start=True, stop=False)
                    pe.matmul(dst, hid_hi[h][:, c_], fw2_lo[:, w_], start=False, stop=False)
                    pe.matmul(dst, hid_lo[h][:, c_], fw2_hi[:, w_], start=False, stop=False)
                    mm = pe.matmul(dst, ones_h[:, :], fb2[0:2, w_], start=False, stop=True)
                mm.then_inc(s_mm2, 1)

            quads(pe, quad)


def kernel(**kw):
    import numpy as np
    import concourse.bacc as bacc
    from concourse.bass_utils import run_bass_kernel_spmd as run

    nc = bacc.Bacc("TRN2", target_bir_lowering=False, num_devices=1)
    kw = {n: np.asarray(v) for n, v in kw.items()}
    k = {n[7:]: v for n, v in kw.items() if n.startswith("L0_tok")}
    at = {n[8:]: v for n, v in kw.items() if n.startswith("L0_attn")}
    ff = {n[7:]: v for n, v in kw.items() if n.startswith("L0_ffn")}
    c = np.ascontiguousarray
    bg = at["bg"]
    arr = {
        "x": c(kw["x"].reshape(16, 8, 128, 192).transpose(0, 2, 1, 3).reshape(16, 128, 1536)),
        "txt": c(kw["txt"].reshape(16, 4, 2, 77, 64).transpose(0, 2, 4, 1, 3).reshape(16, 128, 4, 77)),
        "w1": c(k["conv1_w"].transpose(1, 2, 3, 0).reshape(128, -1)),
        "w2": c(k["conv2_w"].transpose(1, 2, 3, 0).reshape(128, -1)),
        "w3": c(k["conv3_w"].transpose(1, 2, 3, 0).reshape(128, -1)),
        "w4": k["out_w"],
        **{n: k[n] for n in ("conv1_b", "conv2_b", "conv3_b", "out_b", "ln0_g", "ln0_b", "ln1_g", "ln1_b")},
        "w_q": at["Wq"], "w_k": at["Wk"], "w_v": at["Wv"],
        "w_i": c(at["Wg"][:, 0:64]), "w_f": c(at["Wg"][:, 64:128]), "w_o": c(at["Wg"][:, 128:192]),
        "acol": c(np.stack([at["bq"], at["bk"], at["bv"], bg[0:64], bg[64:128], bg[128:192], at["input_bias"], at["norm_scale"]], axis=1)),
        "gate_w": ff["gate_w"], "gate_b": ff["gate_b"],
        "ffn_w1": c(ff["w1"].transpose(1, 0, 2)), "ffn_w2": c(ff["w2"].transpose(1, 0, 2)),
        "ffn_b1": c(ff["b1"].T), "ffn_b2": c(ff["b2"].reshape(1, -1)),
        "ffn_gamma": ff["gamma"], "ffn_beta": ff["beta"],
        "row_sel": np.eye(2, dtype=np.float32),
    }
    aps = {n: nc.dram_tensor("in_" + n, v.shape, mybir.dt.from_np(v.dtype), kind="ExternalInput").ap() for n, v in arr.items()}
    o = nc.dram_tensor("o_d", (128, 205, 64), F32, kind="ExternalOutput").ap()
    build(nc, aps, o)
    r = run(nc, [{"in_" + n: v for n, v in arr.items()}], core_ids=[0])
    return r.results[0]["o_d"]
```

```python
import concourse.bass as bass
from concourse import mybir
from contextlib import ExitStack

F32 = mybir.dt.float32
F16 = mybir.dt.float16
ALU = mybir.AluOpType
ACT = mybir.ActivationFunctionType
AX = mybir.AxisListType


class Chain:

    def __init__(self, eng, sem):
        self.eng, self.sem, self.base, self.n = eng, sem, 0, 0

    def link(self, ins):
        self.n += 1
        ins.then_inc(self.sem, 1)
        self.eng.wait_ge(self.sem, self.base + self.n)

    def enter(self, i, first, per_turn):
        self.start, self.per_turn = self.base + self.n, per_turn
        self.base, self.n = i * per_turn + (self.start - first * per_turn), 0

    def leave(self, turns):
        assert self.n == self.per_turn, (self.n, self.per_turn)
        self.base, self.n = self.start + turns * self.per_turn, 0


def build(nc, a, out):
    B, T, J = 128, 128, 64
    GB = 8
    NG = B // GB
    JP = J + 4
    T2 = 77
    S = T + T2
    NP = B // 2
    XS, WS = 256.0, 1024.0
    UNSCALE = 1.0 / (XS * WS)
    EPS = 1e-5

    with ExitStack() as ctx:
        def sb(name, shape, dt=F32):
            return ctx.enter_context(nc.sbuf_tensor(name, shape, dt))

        def sem(name):
            return ctx.enter_context(nc.semaphore(name))

        conv_bank = [ctx.enter_context(nc.psum_tensor(f"conv_bank{k}", [128, 512], F32)) for k in range(2)]

        WID = {1: 15 * T, 2: 10 * T, 3: 10 * 2 * T, 4: 64}
        w_hi = {k: sb(f"w_hi{k}", [128, n], F16) for k, n in WID.items()}
        w_lo = {k: sb(f"w_lo{k}", [128, n], F16) for k, n in WID.items()}
        cb = sb("cb", [128, 5])
        eps = sb("eps", [128, 1])
        gb_raw = sb("gb_raw", [128, 4, 192])
        gam = [sb(f"gam{k}", [128, n]) for k, n in enumerate((192, 192, 128, 128))]
        bet = [sb(f"bet{k}", [128, n]) for k, n in enumerate((192, 192, 128, 128))]

        x_in = sb("x_in", [128, GB, 192])
        h_relu = [None, sb("h1", [128, 3, GB, J]), sb("h2", [128, 2, GB, J]), sb("h3", [128, GB, 2, J])]
        stats = [sb(f"stats{k}", [128, GB, 6]) for k in range(4)]
        mean = [sb(f"mean{k}", [128, GB]) for k in range(4)]
        var4 = [sb(f"var4_{k}", [128, GB]) for k in range(4)]
        spread, half_mean, gap, gap2 = (sb(n, [128, GB]) for n in ("spread", "half_mean", "gap", "gap2"))
        lnv = [sb(f"lnv{k}", [128, GB]) for k in range(4)]
        rstd = [sb(f"rstd{k}", [128, GB]) for k in range(4)]
        centred = sb("centred", [128, GB, 192])
        full = [sb(f"full{k}", [128, 3 * GB * J]) for k in range(2)]
        act1 = sb("act1", [128, 2, 3, GB, JP], F16)
        act2 = sb("act2", [128, 2, 3, GB, JP], F16)
        act3 = sb("act3", [128, 2, 2, GB, JP], F16)
        res = sb("res", [128, 2, GB, 128], F16)
        resT = sb("resT", [128, 2, GB, 128], F16)

        GP = GB // 2
        N = GP * S
        HALF = N // 2
        BLOCKS = ((0, 64), (64, 128), (128, S))
        double = [ctx.enter_context(nc.psum_tensor(f"double{k}", [128, 2, 512], F32)) for k in range(3)]
        PROJ = ("f", "i", "k", "v", "q", "o")
        ident32 = sb("ident32", [128, 128])
        w_proj = {n: sb(f"w_proj_{n}", [128, 128]) for n in PROJ}
        w_gate = sb("w_gate", [128, 32])
        centre = sb("centre", [128, 128])
        average = sb("average", [128, 128])
        total = sb("total", [128, 128])
        acol = sb("acol", [128, 8])
        bias_k, bias_i, bias_o = (sb(n, [128, 1]) for n in ("bias_k", "bias_i", "bias_o"))
        gate_bias = sb("gate_bias", [128, 16])
        eps8 = sb("eps8", [128, 1])
        one = sb("one", [128, 1])
        causal = sb("causal", [128, S + T2])
        not_start = sb("not_start", [128, N])
        names = ("tokens", "resid", "xn", "lf", "li", "kT", "vT", "qT", "o_log", "cum", "t_f",
                 "t_i", "wv", "nq", "gexp", "den", "h2", "xn2")
        arena = sb("arena", [128, len(names), GP, S])
        A = {n: arena[:, k] for k, n in enumerate(names)}
        for n, place in (("h", "wv"), ("sq", "t_f"), ("sq_b", "t_i"), ("rs", "nq"), ("rs_b", "den")):
            A[n] = A[place]
        raw_room = arena[:, 10:18].rearrange("p k g s -> p (k g s)")
        w_raw, at = {}, 0
        for k, n in WID.items():
            w_raw[k] = raw_room[:, at:at + n]
            at += n
        m_ext = sb("m_ext", [128, GP, S + 1])
        s_arg = sb("s_arg", [128, GP, 2])
        s_dec = sb("s_dec", [128, GP, 3])
        st = sb("st", [128, GB, S + T2])
        vt = sb("vt", [128, GP, 256])
        u1 = sb("u1", [128, GP, S])
        u2 = sb("u2", [128, GP, T2])
        tm0 = sb("tm0", [128, GB, 144])
        tm1 = sb("tm1", [128, GB, 144])

        E, F, D_ = 16, 128, 64
        CH = 41
        CHUNKS = S // CH
        PARTS = ((0, 21), (21, CH))
        QR = 4 * 128
        QUADS = (2 * B * S + E * (QR - 1)) // QR
        ROWS = QUADS * QR
        H_SCALE, FW_SCALE = 64.0, 256.0
        RING = 4
        room = arena[:, :, :, :].rearrange("p k g s -> p (k g s)")
        lay = [0]

        def carve(n):
            lay[0] += n
            return room[:, lay[0] - n:lay[0]]

        raw1, raw2, rawb = room[:, 0:E * F], room[:, E * F:E * F + E * D_], room[:, E * (F + D_):E * (F + 2 * D_)]
        logit = carve(S * E).rearrange("p (t e) -> p t e", e=E)
        work = carve(S * E)
        chosen = [carve(S * E).rearrange("p (t e) -> p t e", e=E) for _ in range(2)]
        work_te, work_et = work.rearrange("p (t e) -> p t e", e=E), work.rearrange("p (e t) -> p e t", e=E)
        rank = logit.rearrange("p t e -> p (t e)").rearrange("p (e t) -> p e t", e=E)
        top, which = [carve(S) for _ in range(2)], carve(S)
        gate = [carve(S) for _ in range(2)]
        slot_f = carve(S)
        slot = [carve(S).bitcast(mybir.dt.uint32) for _ in range(2)]
        quad_no, quad_exp = (h_relu[1][:, :, :, :].rearrange("p w b j -> p (w b j)")[:, k:k + QUADS] for k in (0, QUADS))
        assert lay[0] <= len(names) * N
        lay[0] = 0
        xn_part = carve(CH * D_).rearrange("p (t f) -> p t f", f=D_)
        x_tiles = [carve(4 * D_).rearrange("p (n f) -> p n f", f=D_) for _ in range(RING)]
        xT = [carve(256).bitcast(F16) for _ in range(2)]
        hid = [carve(512) for _ in range(2)]
        hid_hi, hid_lo = ([carve(256).bitcast(F16) for _ in range(2)] for _ in range(2))
        o_tiles = [carve(4 * D_).rearrange("p (n f) -> p n f", f=D_) for _ in range(RING)]
        assert lay[0] <= 4 * S * E
        lay[0] = 0
        got = carve(CH * 2 * D_).rearrange("p (t k f) -> p t k f", k=2, f=D_)
        stream = carve(CH * 2 * D_).rearrange("p (t k f) -> p t k f", k=2, f=D_)
        y = carve(CH * D_).rearrange("p (t f) -> p t f", f=D_)
        assert lay[0] <= 4 * S * E
        st_room = st[:, :, :].rearrange("p b s -> p (b s)")
        fw1_hi, fw1_lo = (st_room[:, 1024 * k:1024 * k + 1024].bitcast(F16) for k in range(2))
        fw2_hi, fw2_lo, fb2 = (full[0][:, 512 * k:512 * k + 512].bitcast(F16) for k in range(3))
        fb1 = sb("fb1", [128, E])
        fb1s = sb("fb1s", [128, E])
        ff_gb = sb("ff_gb", [128, 2, D_])
        row_sel = sb("row_sel", [2, 2])
        ones_h = sb("ones_h", [2, 128], F16)
        e_minus = sb("e_minus", [128, E])
        ones_s = not_start[:, 0:S]
        all_ones = sb("all_ones", [128, 128])
        before = sb("before", [128, 128])
        counts, ends, off, quads_e = (sb(n, [128, E]) for n in ("counts", "ends", "off", "quads_e"))
        quads_i = sb("quads_i", [128, E], mybir.dt.int32)
        quad_i = sb("quad_i", [128, QUADS], mybir.dt.int32)
        y_mean, y_var, y_rstd = (sb(n, [128, CH]) for n in ("y_mean", "y_var", "y_rstd"))
        xs_dram = nc.dram_tensor("xs_dram", [ROWS, D_], F32).ap()
        es_dram = nc.dram_tensor("es_dram", [ROWS, D_], F32).ap()
        zeros = sb("zeros", [128, 512])

        def flat(name):
            return A[name].rearrange("p g s -> p (g s)")

        def halves2(name):
            return flat(name).rearrange("p (c n) -> p c n", c=2)

        ident = sb("ident", [128, 128], F16)
        DVE_LINKS, ACT_LINKS = 31, 12
        mid = sb("mid", [128, GP, 3])
        tok_dram = nc.dram_tensor("tok_dram", [B, S, 144], F32).ap()
        s_w = sem("weights_loaded")
        s_c = sem("constants_loaded")
        s_x = sem("x_loaded")
        s_const = sem("constants_made")
        s_pad = sem("pads_zeroed")
        s_whi = sem("weights_hi_made")
        s_wlo = sem("weights_lo_made")
        s_dve = sem("dve_chain")
        s_act = sem("act_chain")
        s_var = [sem(f"var_ready{k}") for k in range(4)]
        s_rstd = [sem(f"rstd_ready{k}") for k in range(4)]
        s_full = [sem(f"full_ready{k}") for k in range(4)]
        s_hi = [sem(f"hi_ready{k}") for k in range(4)]
        s_lo = [sem(f"lo_ready{k}") for k in range(4)]
        s_conv = [None] + [sem(f"conv_done{k}") for k in (1, 2, 3)]
        s_relu = [None] + [sem(f"relu_done{k}") for k in (1, 2, 3)]
        s_turn = sem("res_turned")
        s_rT = sem("resT_ready")
        s_tok = sem("tok_product_done")
        s_H = sem("tokens_ready")
        s_zero = sem("zeros_stored")
        s_fw = sem("expert_weights_loaded")
        s_fhi = sem("expert_weights_hi")
        s_fmade = sem("expert_weights_made")
        s_lgin = sem("logits_loaded")
        s_cnt = sem("counts_made")
        s_off = sem("offsets_made")
        s_gexp = sem("gate_exp_arg")
        s_gexp2 = sem("gate_exp")
        s_slot = sem("slots_made")
        s_tmap = sem("tile_map_made")
        s_xpart = [sem("xn_part_loaded0"), sem("xn_part_loaded1")]
        s_idx = sem("indices_staged")
        s_scat = [sem("scattered0"), sem("scattered1")]
        s_xt = [sem(f"x_tiles_loaded{k}") for k in range(4)]
        s_xturn = sem("x_tiles_turned")
        s_xhi = sem("x_hi")
        s_xlo = sem("x_lo")
        s_mm1 = sem("hidden_done")
        s_hid = sem("hidden_relu")
        s_hhi = sem("hidden_hi")
        s_hlo = sem("hidden_lo")
        s_mm2 = sem("expert_out_done")
        s_o = sem("expert_out_copied")
        s_ost = [sem(f"expert_out_stored{k}") for k in range(4)]
        s_got = [sem("gathered0"), sem("gathered1")]
        s_strm = [sem("stream_loaded0"), sem("stream_loaded1")]
        s_yvar = sem("y_var")
        s_yr = sem("y_rstd")
        s_yout = [sem("y_done0"), sem("y_done1")]
        s_txt = sem("text_loaded")
        s_aw = sem("attention_weights_loaded")
        s_ac = sem("attention_constants_loaded")
        s_az = sem("weights_zeroed")
        s_acon = sem("attention_constants_made")
        s_hres = sem("residual_kept")
        filled = {n: sem("filled_" + n) for n in ("cx1", "var1", "f", "i", "k", "v", "q", "o", "sc", "den", "vt", "hacc",
                                                  "ms", "cx3", "var3", "tm", "lg")}
        (s_sq1, s_rs1, s_xn, s_l1, s_lf, s_ti, s_li, s_k, s_v, s_q, s_og, s_m, s_fs_arg, s_fs, s_is_arg, s_is, s_e_arg, s_e, s_s_arg, s_s,
         s_vp, s_nq, s_st, s_vt, s_den, s_lden, s_garg, s_g, s_h, s_sq2, s_rs2, s_h2, s_sq3, s_rs3, s_xn2, s_tmA, s_tmD,
         s_lg, s_sav, s_dmax, s_fpos, s_cx1, s_cx3) = (sem(n) for n in (
            "sq1", "rs1", "xn", "l1", "lf", "ti", "li", "k_r", "v_r", "q_r", "og", "m", "fs_arg", "fs", "is_arg", "is_r", "e_arg", "e_r",
            "s_arg_r", "s_r", "vp", "nq", "st_r", "vt_r", "den_r", "lden", "garg", "g", "h_r", "sq2", "rs2", "h2", "sq3", "rs3", "xn2",
            "tmA", "tmD", "lg", "saved", "dmax", "fpos", "cx1_copied", "cx3_copied"))
        s_out2 = [sem("out_stored0"), sem("out_stored1")]
        s_done = sem("expert_rows_stored")
        s_scans = sem("rank_scans")

        block = ctx.enter_context(nc.Block())

        COLS = (3, 3, 2, 2)

        def source(k, b):
            if k == 0:
                return x_in[:, b, :].rearrange("p (j w) -> p w j", w=3)
            return h_relu[k][:, :, b, :] if k < 3 else h_relu[3][:, b, :, :]

        def full_of(k):
            w = COLS[k]
            f = full[k % 2][:, 0:w * GB * J]
            return f.rearrange("p (w b j) -> p w b j", w=w, b=GB) if k < 3 else f.rearrange("p (b w j) -> p w b j", w=w, b=GB)

        def halves(k, h):
            if k == 3:
                return res[:, h].rearrange("p b (w j) -> p w b j", w=2)
            return (act1, act2, act3)[k][:, h, :, :, 2:2 + J]

        def columns(t, k):
            return t.rearrange("p (w j) -> p w j", w=COLS[k])

        ORDER, D = [], 0
        for name, lag, reader, per, at in (
                ("c10", 0, s_relu[1], 3, 1), ("hacc0", 3, s_h, 2, 1), ("hacc1", 3, s_h, 2, 2), ("tok", 2, s_H, 2, 2),
                ("c11", 0, s_relu[1], 3, 2), ("ms", 3, s_rs2, 1, 1), ("cx1", 2, s_cx1, 1, 1),
                ("c12", 0, s_relu[1], 3, 3), ("var1", 2, s_rs1, 1, 1), ("cx3", 3, s_cx3, 1, 1),
                ("c30", 1, s_relu[3], 2, 1), ("var3", 3, s_rs3, 1, 1), ("f", 2, s_l1, 1, 1), ("i", 2, s_ti, 1, 1), ("k", 2, s_k, 1, 1),
                ("c31", 1, s_relu[3], 2, 2), ("v", 2, s_v, 1, 1), ("q", 2, s_q, 1, 1), ("o", 2, s_og, 1, 1),
                ("c20", 0, s_relu[2], 2, 1), ("tm0", 3, s_tmD, 1, 1), ("tm1", 3, s_tmA, 1, 1), ("lg", 3, s_lg, 1, 1),
                ("sc0", 2, s_st, 4, 1), ("sc1", 2, s_st, 4, 2), ("sc2", 2, s_st, 4, 3), ("sc3", 2, s_st, 4, 4),
                ("c21", 0, s_relu[2], 2, 2), ("den", 2, s_den, 1, 1), ("vt", 2, s_vt, 1, 1), ("turned", 1, s_rT, 1, 1)):
            if name[0] == "c" and name[1] in "123":
                tile = conv_bank[(len(ORDER) - D) % 2]
            else:
                tile = double[D % 3]
                D += 1
            ORDER.append((name, lag, tile, reader, per, at))
        assert D == 24
        TURNS = NG + 3
        TILE = {name: tile for name, _, tile, _, _, _ in ORDER}
        LAG = {name: lag for name, lag, *_ in ORDER}
        BEFORE = {}
        last_in = {}
        for t in range(TURNS):
            for name, lag, tile, reader, per, at in ORDER:
                g = t - lag
                if 0 <= g < NG:
                    BEFORE[name, g] = last_in.get(id(tile))
                    last_in[id(tile)] = (reader, per, at, g)

        STEADY = 5
        LOOP = (4, NG - 1)
        for t in range(*LOOP):
            for name, lag, *_ in ORDER:
                b, c = BEFORE[name, t - lag], BEFORE[name, STEADY - lag]
                assert b[:3] == c[:3] and b[3] - t == c[3] - STEADY

        def take(pe, name, g):
            like = g if isinstance(g, int) else STEADY - LAG[name]
            before = BEFORE[name, like]
            if before:
                reader, per, at, b = before
                pe.wait_ge(reader, g * per + ((b - like) * per + at))
            return TILE[name]

        def on(g):
            return not isinstance(g, int) or 0 <= g < NG

        def slots(eng, slot):
            last = (QUADS - RING) // RING
            for j in range(2 * RING):
                slot(j // RING, j % RING)
            with eng.Fori(2, last) as m:
                for h in range(RING):
                    slot(m, h)
            for j in range(last * RING, QUADS + 3):
                slot(j // RING, j % RING)

        def behind(m, h, lag):
            q = m * RING + (h - lag)
            if isinstance(q, int) and not 0 <= q < QUADS:
                return None
            return q, m + (h - lag) // RING, (h - lag) % RING, (h - lag) % 2

        def turns(eng, c, links, turn):
            for t in range(0, LOOP[0]):
                turn(t)
            with eng.Fori(*LOOP) as t:
                if c:
                    c.enter(t, LOOP[0], links)
                turn(t)
            if c:
                c.leave(LOOP[1] - LOOP[0])
            for t in range(LOOP[1], TURNS):
                turn(t)

        def wait(eng, s, count):
            if not (isinstance(count, int) and count <= 0):
                eng.wait_ge(s, count)

        def copy_turned(copy, n):
            tile = TILE[f"tm{n}"][:, :, :].rearrange("p g (k s b f) -> p k s g b f", k=2, s=2, b=2)
            for s_, (dst, rows) in enumerate(((tm0, 128), (tm1, T2))):
                for k in range(2):
                    rowsof = dst[0:rows, 4 * n:4 * n + 4, 64 * k:64 * k + 64].rearrange("p (g b) f -> p g b f", g=2)
                    last = copy(rowsof, tile[0:rows, k, s_])
            return last

        @block.sync
        def _(sp):
            for k in (1, 2, 3, 4):
                sp.dma_start(w_raw[k], a[f"w{k}"]).then_inc(s_w, 16)
            with nc.allow_non_contiguous_dma(reason="a few bias columns"):
                sp.dma_start(cb[:, 0:1], a["conv1_b"].rearrange("(p o) -> p o", o=1)).then_inc(s_c, 16)
                sp.dma_start(cb[:, 1:2], a["conv2_b"].rearrange("(p o) -> p o", o=1)).then_inc(s_c, 16)
                sp.dma_start(cb[:, 2:4], a["conv3_b"].rearrange("(h p) -> p h", h=2)).then_inc(s_c, 16)
                for h in range(2):
                    sp.dma_start(cb[64 * h:64 * h + 64, 4:5], a["out_b"].rearrange("(p o) -> p o", o=1)).then_inc(s_c, 16)
            for n, name in enumerate(("ln0_g", "ln0_b", "ln1_g", "ln1_b")):
                m = 192 if n < 2 else 128
                sp.dma_start(gb_raw[:, n, 0:m], a[name].rearrange("(o n) -> o n", o=1).to_broadcast([128, m])).then_inc(s_c, 16)

            def load_x(i):
                wait(sp, s_full[0], i)
                sp.dma_start(x_in[:, :, :].rearrange("p b f -> p (b f)"), a["x"][i]).then_inc(s_x, 16)

            load_x(0)
            sp.wait_ge(s_az, 1)
            for r in range(0, ROWS, 128 * 8):
                n = min(8, (ROWS - r) // 128)
                sp.dma_start(xs_dram[r:r + 128 * n].rearrange("(p n) f -> p (n f)", p=128), zeros[:, 0:64 * n]).then_inc(s_zero, 16)
            sp.wait_ge(s_az, 1)
            for h in range(2):
                q = slice(64 * h, 64 * h + 64)
                for n in PROJ:
                    sp.dma_start(w_proj[n][q, q], a["w_" + n]).then_inc(s_aw, 16)
                sp.dma_start(w_gate[q, 16 * h:16 * h + 16], a["gate_w"]).then_inc(s_aw, 16)
                sp.dma_start(acol[q, :], a["acol"]).then_inc(s_ac, 16)
            sp.dma_start(gate_bias[:, :], a["gate_b"].rearrange("(o n) -> o n", o=1).to_broadcast([128, 16])).then_inc(s_ac, 16)

            def text(g):
                wait(sp, s_hres, g)
                wait(sp, s_cx1, g)
                sp.dma_start(A["tokens"][:, :, T:S], a["txt"][g]).then_inc(s_txt, 16)

            def save(g):
                sp.wait_ge(s_tmD, g + 1)
                sp.wait_ge(s_tmA, g + 1)
                sp.wait_ge(s_lg, g + 1)
                rows = tok_dram[bass.ds(g * GB, GB)].rearrange("b t f -> t b f")
                sp.dma_start(rows[0:128], tm0[:, :, :]).then_inc(s_sav, 16)
                sp.dma_start(rows[128:S], tm1[0:T2, :, :]).then_inc(s_sav, 16)

            def turn(t):
                if on(t + 1):
                    load_x(t + 1)
                if on(t - 1):
                    text(t - 1)
                if on(t - 3):
                    save(t - 3)

            turns(sp, None, 0, turn)
            sp.wait_ge(s_sav, 32 * NG)
            sp.wait_ge(filled["hacc"], 2 * NG)
            sp.dma_start(raw1.rearrange("p (e f) -> p e f", e=E)[0:64], a["ffn_w1"]).then_inc(s_fw, 16)
            sp.dma_start(raw1.rearrange("p (e f) -> p e f", e=E)[64:128], a["ffn_w1"]).then_inc(s_fw, 16)
            sp.dma_start(raw2.rearrange("p (e f) -> p e f", e=E), a["ffn_w2"]).then_inc(s_fw, 16)
            for r in range(2):
                sp.dma_start(rawb[r:r + 1, :], a["ffn_b2"]).then_inc(s_fw, 16)
            sp.dma_start(fb1[:, :], a["ffn_b1"]).then_inc(s_fw, 16)
            sp.dma_start(row_sel[:, :], a["row_sel"]).then_inc(s_fw, 16)
            for k, name in enumerate(("ffn_gamma", "ffn_beta")):
                sp.dma_start(ff_gb[:, k, :], a[name].rearrange("(o n) -> o n", o=1).to_broadcast([128, D_])).then_inc(s_fw, 16)
            sp.wait_ge(s_fmade, 4)
            sp.dma_start(logit, tok_dram[:, :, 128:144]).then_inc(s_lgin, 16)
            sp.wait_ge(s_slot, 2)
            for k in range(CHUNKS):
                for h, (lo, hi) in enumerate(PARTS):
                    if k:
                        sp.wait_ge(s_scat[h], 16 * 2 * (hi - lo) * k)
                    sp.dma_start(xn_part[:, lo:hi, :], tok_dram[:, k * CH + lo:k * CH + hi, 0:D_]).then_inc(s_xpart[h], 16)
            for h, (lo, hi) in enumerate(PARTS):
                sp.wait_ge(s_scat[h], 16 * 2 * (hi - lo) * CHUNKS)

            def load_tiles(q, turn, h):
                wait(sp, s_xturn, q + (1 - RING))
                sp.dma_start(x_tiles[h], xs_dram[bass.ds(q * 512, 512)].rearrange("(n p) f -> p n f", p=128)).then_inc(s_xt[h], 16)

            def step(m, h):
                ahead, stored = behind(m, h, -RING), behind(m, h, 3)
                if ahead:
                    q, turn, ring, _ = ahead
                    load_tiles(q, turn, ring)
                if stored:
                    q, turn, ring, _ = stored
                    sp.wait_ge(s_o, q + 1)
                    sp.dma_start(es_dram[bass.ds(q * 512, 512)].rearrange("(n p) f -> p n f", p=128), o_tiles[ring]).then_inc(s_ost[ring], 16)

            for h in range(RING):
                load_tiles(h, 0, h)
            slots(sp, step)
            for h in range(RING):
                sp.wait_ge(s_ost[h], 16 * ((QUADS + RING - 1 - h) // RING))
            sp.sem_inc(s_done, 1)
            for k in range(CHUNKS):
                for h, (lo, hi) in enumerate(PARTS):
                    if k:
                        sp.wait_ge(s_out2[h], 16 * k)
                    sp.dma_start(stream[:, lo:hi], tok_dram[:, k * CH + lo:k * CH + hi, 0:2 * D_].rearrange("b t (k f) -> b t k f", k=2)).then_inc(s_strm[h], 16)
                for h, (lo, hi) in enumerate(PARTS):
                    sp.wait_ge(s_yout[h], k + 1)
                    sp.dma_start(out[:, k * CH + lo:k * CH + hi, :], y[:, lo:hi, :]).then_inc(s_out2[h], 16)
            for h in range(2):
                sp.wait_ge(s_out2[h], 16 * CHUNKS)

        @block.vector
        def _(dve):
            c = Chain(dve, s_dve)
            dve.memset(one[:, :], 1.0)
            dve.memset(eps8[:, :], 1e-8)
            dve.memset(m_ext[:, :, 0:1], 0.0)
            dve.memset(u1[:, :, 0:64], 0.0)
            dve.memset(not_start[:, :], 1.0)
            c.link(dve.memset(eps[:, :], EPS))
            starts = not_start[:, :].rearrange("p (g s) -> p g s", g=GP)
            for lo, _ in BLOCKS:
                dve.memset(starts[:, :, lo:lo + 1], 0.0)
            dve.wait_ge(s_c, 16 * 9)
            for k in range(4):
                for n, dst in ((0, gam[k]), (1, bet[k])):
                    raw = gb_raw[:, 2 * (k >= 2) + n, 0:64 * COLS[k]]
                    raw = raw.rearrange("p (j w) -> p w j", w=COLS[k]) if k < 3 else columns(raw, k)
                    last = dve.tensor_scalar(columns(dst[:, :], k), raw, XS, None, ALU.mult)
            c.link(last)
            for k in (1, 2, 3, 4):
                dve.wait_ge(s_w, 16 * 4)
                dve.wait_ge(s_whi, k)
                dve.scalar_tensor_tensor(w_lo[k][:, :], w_raw[k], WS, w_hi[k][:, :], ALU.mult, ALU.subtract).then_inc(s_wlo, 1)
            dve.wait_ge(s_pad, 10)
            dve.tensor_tensor(centre[:, :], ident32[:, :], average[:, :], ALU.subtract)
            dve.wait_ge(s_ac, 16 * 3)
            dve.tensor_scalar(bias_k[:, :], acol[:, 1:2], 0.125, None, ALU.mult)
            c.link(dve.tensor_tensor(bias_i[:, :], acol[:, 3:4], acol[:, 6:7], ALU.add))
            dve.tensor_scalar(bias_i[:, :], bias_i[:, :], 0.2, None, ALU.mult)
            dve.tensor_scalar(bias_o[:, :], acol[:, 5:6], -1.0, None, ALU.mult).then_inc(s_acon, 1)

            def norm(k, i, in_sem, in_count, full_free, full_count):
                dve.wait_ge(in_sem, in_count)
                for b in range(GB):
                    last = dve.bn_stats(stats[k][:, b, :], source(k, b))
                c.link(last)
                even, odd = stats[k][:, :, 0:3], stats[k][:, :, 3:6]
                dve.tensor_tensor(spread[:, :], even[:, :, 2], odd[:, :, 2], ALU.add)
                dve.tensor_scalar(half_mean[:, :], even[:, :, 1], 0.5, None, ALU.mult)
                c.link(dve.tensor_tensor(gap[:, :], even[:, :, 1], odd[:, :, 1], ALU.subtract))
                dve.scalar_tensor_tensor(mean[k][:, :], odd[:, :, 1], 0.5, half_mean[:, :], ALU.mult, ALU.add)
                c.link(dve.tensor_tensor(gap2[:, :], gap[:, :], gap[:, :], ALU.mult))
                dve.scalar_tensor_tensor(var4[k][:, :], spread[:, :], 4.0 / (64 * COLS[k]), gap2[:, :],
                                         ALU.mult, ALU.add).then_inc(s_var[k], 1)
                dve.wait_ge(s_var[k], i + 1)
                for b in range(GB):
                    last = dve.scalar_tensor_tensor(columns(centred[:, b, 0:64 * COLS[k]], k), source(k, b), mean[k][:, b:b + 1],
                                                    columns(gam[k][:, :], k), ALU.subtract, ALU.mult)
                c.link(last)
                dve.wait_ge(s_rstd[k], i + 1)
                wait(dve, full_free, full_count)
                for b in range(GB):
                    last = dve.scalar_tensor_tensor(full_of(k)[:, :, b, :], columns(centred[:, b, 0:64 * COLS[k]], k),
                                                    rstd[k][:, b:b + 1], columns(bet[k][:, :], k), ALU.mult, ALU.add)
                last.then_inc(s_full[k], 1)

            def norm0(i):
                norm(0, i, s_x, i * 16 + 16, s_lo[2], i - 1)

            def norm1(i):
                norm(1, i, s_relu[1], i * 3 + 3, s_lo[3], i - 1)

            def norm3(i, norm1_done):
                norm(3, i, s_relu[3], i * 2 + 2, s_lo[1], norm1_done)

            def norm2(i, norm0_done):
                norm(2, i, s_relu[2], i * 2 + 2, s_lo[0], norm0_done)

            def bank2(name):
                return TILE[name][:, :, 0:HALF]

            def normed(g):
                dve.wait_ge(s_rs1, g + 1)
                dve.tensor_tensor(A["xn"], A["xn"], A["rs"], ALU.mult).then_inc(s_xn, 1)

            def keep(g):
                dve.wait_ge(s_H, g * 2 + 2)
                dve.wait_ge(s_txt, g * 16 + 16)
                wait(dve, s_h2, g)
                dve.tensor_copy(A["resid"], A["tokens"]).then_inc(s_hres, 1)

            def gates(g):
                dve.wait_ge(filled["f"], g + 1)
                dve.tensor_scalar(halves2("t_f"), bank2("f"), acol[:, 4:5], 0.0, ALU.add, ALU.max).then_inc(s_fpos, 1)
                dve.wait_ge(s_fpos, g + 1)
                dve.wait_ge(s_l1, g + 1)
                dve.scalar_tensor_tensor(A["lf"], A["t_f"], -1.0, A["lf"], ALU.mult, ALU.subtract).then_inc(s_lf, 1)
                dve.wait_ge(s_ti, g + 1)
                dve.tensor_scalar(A["li"], A["li"], -20.0, 10.0, ALU.mult, ALU.add).then_inc(s_li, 1)

            def scans(g):
                dve.wait_ge(s_lf, g + 1)
                dve.wait_ge(s_li, g + 1)
                for p in range(GP):
                    last = dve.tensor_tensor_scan(m_ext[:, p, 1:S + 1], A["lf"][:, p, :], A["li"][:, p, :], 0.0, ALU.add, ALU.max)
                last.then_inc(s_m, 1)
                c.link(dve.tensor_tensor_scan(flat("cum"), not_start[:, :], flat("lf"), 0.0, ALU.mult, ALU.add))
                dve.wait_ge(s_m, g + 1)
                mids = [(lo + hi) // 2 for lo, hi in BLOCKS]
                for n in range(3):
                    last = dve.tensor_copy(mid[:, :, n:n + 1], A["cum"][:, :, mids[n]:mids[n] + 1])
                c.link(last)
                for n, (lo, hi) in enumerate(BLOCKS):
                    last = dve.tensor_tensor(A["cum"][:, :, lo:hi], A["cum"][:, :, lo:hi],
                                             mid[:, :, n:n + 1].to_broadcast([128, GP, hi - lo]), ALU.subtract)
                c.link(last)
                dve.tensor_tensor(A["wv"], A["li"], A["cum"], ALU.subtract).then_inc(s_e_arg, 1)
                for n in range(2):
                    end = BLOCKS[n][1] - 1
                    last = dve.tensor_tensor(s_arg[:, :, n:n + 1], A["cum"][:, :, end:end + 1], mid[:, :, n + 1:n + 2], ALU.add)
                last.then_inc(s_s_arg, 1)
                c.link(dve.tensor_tensor(A["t_f"], A["lf"], m_ext[:, :, 0:S], ALU.add))
                dve.tensor_tensor(A["t_f"], A["t_f"], m_ext[:, :, 1:S + 1], ALU.subtract).then_inc(s_fs_arg, 1)
                dve.tensor_tensor(A["t_i"], A["li"], m_ext[:, :, 1:S + 1], ALU.subtract).then_inc(s_is_arg, 1)
                wait(dve, s_g, g)
                dve.tensor_tensor(A["gexp"], A["cum"], m_ext[:, :, 1:S + 1], ALU.subtract).then_inc(s_garg, 1)

            def weigh(g):
                dve.wait_ge(s_e, g + 1)
                dve.wait_ge(s_v, g + 1)
                dve.tensor_tensor(A["wv"], A["wv"], A["vT"], ALU.mult).then_inc(s_vp, 1)
                dve.wait_ge(s_s, g + 1)
                c.link(dve.tensor_tensor(s_dec[:, :, 2:3], s_dec[:, :, 0:1], s_dec[:, :, 1:2], ALU.mult))

            def normalizer(g):
                dve.wait_ge(s_fs, g + 1)
                dve.wait_ge(s_is, g + 1)
                dve.wait_ge(s_k, g + 1)
                dve.memset(A["t_f"][:, :, 0:1], 0.0)
                c.link(dve.tensor_tensor(A["t_i"], A["t_i"], A["kT"], ALU.mult))
                wait(dve, filled["den"], g)
                c.link(dve.tensor_tensor_scan(flat("nq"), flat("t_f"), flat("t_i"), 0.0, ALU.mult, ALU.add))
                dve.wait_ge(s_q, g + 1)
                dve.tensor_tensor(A["nq"], A["nq"], A["qT"], ALU.mult).then_inc(s_nq, 1)

            def mask(g, n):
                dve.wait_ge(filled["sc"], g * 4 + (n + 1))
                if n == 0:
                    wait(dve, filled["hacc"], g * 2)
                tile = TILE[f"sc{n}"]
                dve.tensor_tensor(st[:, 2 * n:2 * n + 2, 0:S], tile[:, :, 0:S],
                                  causal[:, 0:S].unsqueeze(1).to_broadcast([128, 2, S]), ALU.mult)
                dve.tensor_tensor(st[0:T2, 2 * n:2 * n + 2, S:], tile[0:T2, :, S:S + T2],
                                  causal[0:T2, S:].unsqueeze(1).to_broadcast([T2, 2, T2]), ALU.mult).then_inc(s_st, 1)

            def denominator(g):
                dve.wait_ge(s_den, g + 1)
                dve.tensor_scalar(A["den"], A["den"], 1e-6, None, ALU.max).then_inc(s_dmax, 1)

            def exponent(g):
                dve.wait_ge(s_garg, g * 2 + 1)
                dve.wait_ge(s_og, g + 1)
                c.link(dve.tensor_tensor(A["gexp"], A["gexp"], A["o_log"], ALU.subtract))
                dve.wait_ge(s_lden, g + 1)
                dve.tensor_tensor(A["gexp"], A["gexp"], A["den"], ALU.subtract).then_inc(s_garg, 1)

            def combine(g, n):
                dve.wait_ge(filled["hacc"], g * 2 + (n + 1))
                tile, pairs = TILE[f"hacc{n}"], slice(2 * n, 2 * n + 2)
                def dec(k, width):
                    return s_dec[:, pairs, k:k + 1].to_broadcast([128, 2, width])
                own0 = tile[:, 0, 0:2 * S].rearrange("p (g s) -> p g s", g=2)
                own12 = tile[:, 1, 0:436].rearrange("p (g s) -> p g s", g=2)
                dve.tensor_tensor(u1[:, pairs, 64:128], own0[:, :, 64:128], dec(0, 64), ALU.mult)
                dve.tensor_tensor(u1[:, pairs, 128:S], own12[:, :, 64:141], dec(1, T2), ALU.mult)
                c.link(dve.tensor_tensor(u2[:, pairs, :], own0[:, :, 128:S], dec(2, T2), ALU.mult))
                dve.tensor_tensor(u1[:, pairs, 64:128], own12[:, :, 0:64], u1[:, pairs, 64:128], ALU.add)
                c.link(dve.tensor_tensor(u1[:, pairs, 128:S], u1[:, pairs, 128:S], u2[:, pairs, :], ALU.add))
                c.link(dve.tensor_tensor(u1[:, pairs, 128:S], own12[:, :, 141:218], u1[:, pairs, 128:S], ALU.add))
                if n == 0:
                    dve.wait_ge(s_g, g + 1)
                dve.tensor_tensor(A["h"][:, pairs, 0:64], own0[:, :, 0:64], A["gexp"][:, pairs, 0:64], ALU.mult)
                dve.tensor_tensor(A["h"][:, pairs, 64:S], u1[:, pairs, 64:S], A["gexp"][:, pairs, 64:S], ALU.mult).then_inc(s_h, 1)

            def residual(g):
                dve.wait_ge(s_rs2, g + 1)
                c.link(dve.tensor_tensor(A["h"], A["h"], A["rs_b"], ALU.mult))
                dve.wait_ge(s_hres, g + 1)
                wait(dve, filled["tm"], g * 2)
                dve.scalar_tensor_tensor(A["h2"], A["h"], acol[:, 7:8], A["resid"], ALU.mult, ALU.add).then_inc(s_h2, 1)

            def normed2(g):
                dve.wait_ge(s_rs3, g + 1)
                dve.tensor_tensor(A["xn2"], A["xn2"], A["rs_b"], ALU.mult).then_inc(s_xn2, 1)

            def turned_copy(g):
                dve.wait_ge(filled["tm"], g * 2 + 1)
                wait(dve, s_sav, g * 32)
                copy_turned(dve.tensor_copy, 0).then_inc(s_tmD, 1)

            def logits(g):
                dve.wait_ge(filled["lg"], g + 1)
                tile = TILE["lg"][:, 0, 0:256].rearrange("p (s b e) -> p s b e", s=2, b=GB)
                for s_, (dst, rows) in enumerate(((tm0, 128), (tm1, T2))):
                    last = dve.tensor_tensor(dst[0:rows, :, 128:144], tile[0:rows, s_],
                                             gate_bias[0:rows, :].unsqueeze(1).to_broadcast([rows, GB, 16]), ALU.add)
                last.then_inc(s_lg, 1)

            norm0(0)

            def turn(t):
                if on(t - 1):
                    norm2(t - 1, t + 1 if on(t) else NG)
                if on(t - 3):
                    for n in range(2):
                        combine(t - 3, n)
                    residual(t - 3)
                if on(t - 2):
                    keep(t - 2)
                    normed(t - 2)
                if on(t):
                    norm1(t)
                if on(t - 3):
                    normed2(t - 3)
                if on(t - 2):
                    gates(t - 2)
                    scans(t - 2)
                if on(t - 1):
                    norm3(t - 1, t + 1 if on(t) else NG)
                if on(t - 2):
                    normalizer(t - 2)
                    weigh(t - 2)
                if on(t - 3):
                    turned_copy(t - 3)
                    logits(t - 3)
                if on(t - 2):
                    for n in range(4):
                        mask(t - 2, n)
                if on(t + 1):
                    norm0(t + 1)
                if on(t - 2):
                    denominator(t - 2)
                    exponent(t - 2)

            turns(dve, c, DVE_LINKS, turn)

            dve.wait_ge(s_fw, 16 * 9)
            dve.wait_ge(s_fhi, 3)
            dve.scalar_tensor_tensor(fw1_lo, raw1, FW_SCALE, fw1_hi, ALU.mult, ALU.subtract).then_inc(s_fmade, 1)
            dve.scalar_tensor_tensor(fw2_lo, raw2, FW_SCALE, fw2_hi, ALU.mult, ALU.subtract).then_inc(s_fmade, 1)
            c.link(dve.scalar_tensor_tensor(rawb[0:2, :], rawb[0:2, :], FW_SCALE, fb2[0:2, :], ALU.mult, ALU.subtract))
            c.link(dve.tensor_scalar(rawb[0:2, :], rawb[0:2, :], row_sel[:, 1:2], None, ALU.mult))
            dve.scalar_tensor_tensor(fb2[0:2, :], fb2[0:2, :], row_sel[:, 0:1], rawb[0:2, :], ALU.mult, ALU.add).then_inc(s_fmade, 1)
            dve.memset(ones_h[:, :], H_SCALE)
            dve.tensor_scalar(fb1s[:, :], fb1[:, :], H_SCALE, None, ALU.mult).then_inc(s_fmade, 1)

            dve.wait_ge(s_lgin, 16)
            for k in range(2):
                c.link(dve.tensor_reduce(top[k], logit, AX.X, ALU.max))
                c.link(dve.tensor_tensor(work_te, logit, top[k].unsqueeze(2).to_broadcast([128, S, E]), ALU.is_equal))
                c.link(dve.tensor_tensor(work_te, work_te, e_minus[:, :].unsqueeze(1).to_broadcast([128, S, E]), ALU.mult))
                c.link(dve.tensor_reduce(which, work_te, AX.X, ALU.min))
                c.link(dve.tensor_tensor(chosen[k], e_minus[:, :].unsqueeze(1).to_broadcast([128, S, E]),
                                         which.unsqueeze(2).to_broadcast([128, S, E]), ALU.is_equal))
                if k == 0:
                    c.link(dve.scalar_tensor_tensor(logit, chosen[0], -1e30, logit, ALU.mult, ALU.add))
            dve.tensor_tensor(gate[1], top[1], top[0], ALU.subtract).then_inc(s_gexp, 1)
            dve.memset(ones_s, 1.0)
            c.link(dve.tensor_tensor(work_et, chosen[0].rearrange("p t e -> p e t"), chosen[1].rearrange("p t e -> p e t"), ALU.add))
            for e in range(E):
                last = dve.tensor_tensor_scan(rank[:, e, :], ones_s, work_et[:, e, :], 0.0, ALU.mult, ALU.add)
            c.link(last)
            dve.tensor_copy(counts[:, :], rank[:, :, S - 1]).then_inc(s_cnt, 1)
            dve.wait_ge(s_off, 1)
            dve.tensor_copy(off[:, :], double[0][:, 0, 0:E])
            c.link(dve.tensor_scalar(quads_i[:, :], double[0][:, 0, E:2 * E], QR - 1.0, None, ALU.add))
            c.link(dve.tensor_scalar(quads_i[:, :], quads_i[:, :], 9, None, ALU.logical_shift_right))
            c.link(dve.tensor_copy(quads_e[:, :], quads_i[:, :]))
            c.link(dve.tensor_tensor_scan(ends[:, :], ones_s[:, 0:E], quads_e[:, :], 0.0, ALU.mult, ALU.add))
            c.link(dve.tensor_tensor(quads_e[:, :], ends[:, :], quads_e[:, :], ALU.subtract))
            c.link(dve.scalar_tensor_tensor(off[:, :], quads_e[:, :], float(QR), off[:, :], ALU.mult, ALU.add))
            c.link(dve.tensor_scalar(off[:, :], off[:, :], -1.0, None, ALU.add))
            c.link(dve.tensor_tensor(rank, rank, off[:, :].unsqueeze(2).to_broadcast([128, E, S]), ALU.add))
            for k in range(2):
                c.link(dve.tensor_tensor(work_te, chosen[k], rank.rearrange("p e t -> p t e"), ALU.mult))
                c.link(dve.tensor_reduce(slot_f, work_te, AX.X, ALU.add))
                dve.tensor_copy(slot[k], slot_f).then_inc(s_slot, 1)
            c.link(dve.memset(quad_exp, 0.0))
            dve.wait_ge(s_tmap, 1)
            for e in range(E):
                c.link(dve.scalar_tensor_tensor(quad_exp, quad_no, ends[:, e:e + 1], quad_exp, ALU.is_ge, ALU.add))
            dve.tensor_scalar(quad_i[:, :], quad_exp, float(E - 1), None, ALU.min).then_inc(s_tmap, 1)
            dve.wait_ge(s_gexp2, 1)
            c.link(dve.tensor_scalar(gate[0], gate[1], 1.0, None, ALU.add))
            c.link(dve.reciprocal(gate[0], gate[0]))
            c.link(dve.tensor_tensor(gate[1], gate[1], gate[0], ALU.mult))

            def step(m, h):
                hidden, turned, result = behind(m, h, 2), behind(m, h, 0), behind(m, h, 3)
                if hidden:
                    q, _, _, two = hidden
                    dve.wait_ge(s_hid, q + 1)
                    wait(dve, s_mm2, q + (-1))
                    dve.tensor_copy(hid_hi[two], hid[two]).then_inc(s_hhi, 1)
                if turned:
                    q, _, _, two = turned
                    dve.wait_ge(s_xhi, q + 1)
                    dve.scalar_tensor_tensor(xT[two][64:128, :], double[0][0:64, two, :], XS, xT[two][0:64, :], ALU.mult, ALU.subtract).then_inc(s_xlo, 1)
                if result:
                    q, turn, ring, two = result
                    dve.wait_ge(s_mm2, q + 1)
                    wait(dve, s_ost[ring], turn * 16)
                    dve.tensor_scalar(o_tiles[ring], double[2][:, two, 0:256].rearrange("p (n f) -> p n f", f=D_),
                                      1.0 / (H_SCALE * FW_SCALE), None, ALU.mult).then_inc(s_o, 1)

            slots(dve, step)

            for k in range(CHUNKS):
                for h, (lo, hi) in enumerate(PARTS):
                    r, n = slice(lo, hi), hi - lo
                    o = slice(k * CH + lo, k * CH + hi)
                    dve.wait_ge(s_got[h], 16 * 2 * n * (k + 1))
                    def over(v):
                        return v.unsqueeze(2).to_broadcast([128, n, D_])
                    for m in range(2):
                        last = dve.tensor_tensor(got[:, r, m, :], got[:, r, m, :], over(gate[m][:, o]), ALU.mult)
                    c.link(last)
                    if k:
                        dve.wait_ge(s_out2[h], 16 * k)
                    c.link(dve.tensor_tensor(y[:, r], got[:, r, 0, :], got[:, r, 1, :], ALU.add))
                    dve.wait_ge(s_strm[h], 16 * (k + 1))
                    c.link(dve.tensor_tensor(y[:, r], y[:, r], stream[:, r, 0, :], ALU.add))
                    c.link(dve.tensor_reduce(y_mean[:, r], y[:, r], AX.X, ALU.add))
                    c.link(dve.tensor_scalar(y_mean[:, r], y_mean[:, r], 1.0 / D_, None, ALU.mult))
                    c.link(dve.tensor_tensor(y[:, r], y[:, r], over(y_mean[:, r]), ALU.subtract))
                    c.link(dve.tensor_tensor(got[:, r, 0, :], y[:, r], y[:, r], ALU.mult))
                    dve.tensor_reduce(y_var[:, r], got[:, r, 0, :], AX.X, ALU.add).then_inc(s_yvar, 1)
                    dve.wait_ge(s_yr, 2 * k + h + 1)
                    c.link(dve.tensor_tensor(y[:, r], y[:, r], over(y_rstd[:, r]), ALU.mult))
                    c.link(dve.tensor_tensor(y[:, r], y[:, r], ff_gb[:, 0, :].unsqueeze(1).to_broadcast([128, n, D_]), ALU.mult))
                    c.link(dve.tensor_tensor(y[:, r], y[:, r], ff_gb[:, 1, :].unsqueeze(1).to_broadcast([128, n, D_]), ALU.add))
                    dve.tensor_tensor(y[:, r], y[:, r], stream[:, r, 1, :], ALU.add).then_inc(s_yout[h], 1)

        @block.scalar
        def _(act):
            c = Chain(act, s_act)
            act.preload_act_table_set("natural_log_exp_and_others")
            act.wait_ge(s_w, 16 * 4)
            for k in (1, 2, 3, 4):
                act.activation(w_hi[k][:, :], w_raw[k], ACT.Copy, scale=WS).then_inc(s_whi, 1)
            act.wait_ge(s_c, 16 * 9)

            def root(k, i):
                act.wait_ge(s_var[k], i + 1)
                c.link(act.activation(lnv[k][:, :], var4[k][:, :], ACT.Ln, bias=eps[:, 0:1], scale=0.25))
                act.activation(rstd[k][:, :], lnv[k][:, :], ACT.Exp, scale=-0.5).then_inc(s_rstd[k], 1)

            def high(k, i, free, count):
                act.wait_ge(s_full[k], i + 1)
                wait(act, free, count)
                for b in range(COLS[k]):
                    last = act.activation(halves(k, 0)[:, b], full_of(k)[:, b], ACT.Copy)
                last.then_inc(s_hi[k], 1)

            def relu(k, i, w):
                n = COLS[k]
                act.wait_ge(s_conv[k], i * n + (w + 1))
                if w == 0:
                    wait(act, s_full[k], i)
                dst = h_relu[k][:, w] if k < 3 else h_relu[3][:, :, w]
                src = TILE[f"c{k}{w}"][:, :].rearrange("p (b j) -> p b j", b=GB)
                bias = (0, 0, 1, 2 + w)[k]
                act.activation(dst, src, ACT.Relu, bias=cb[:, bias:bias + 1], scale=UNSCALE).then_inc(s_relu[k], 1)

            def turned(i):
                act.wait_ge(s_turn, i + 1)
                wait(act, s_tok, i)
                act.activation(resT[:, :].rearrange("p h b t -> p h (b t)"), TILE["turned"][:, :, :].bitcast(F16), ACT.Copy).then_inc(s_rT, 1)

            def tokens(i):
                act.wait_ge(s_tok, i + 1)
                wait(act, s_hres, i)
                for h in range(2):
                    q = slice(64 * h, 64 * h + 64)
                    act.activation(A["tokens"][q, :, 0:T], TILE["tok"][q, 0, :].rearrange("p (b t) -> p b t", b=GP),
                                   ACT.Identity, bias=cb[q, 4:5], scale=UNSCALE).then_inc(s_H, 1)

            def bank2(name):
                return TILE[name][:, :, 0:HALF]

            def centred_square(g, name, dst, read, count, sq, sem_copied, sem_out):
                act.wait_ge(filled[name], g + 1)
                wait(act, read, count)
                act.activation(halves2(dst), bank2(name), ACT.Copy).then_inc(sem_copied, 1)
                act.wait_ge(sem_copied, g + 1)
                act.activation(A[sq], A[dst], ACT.Square).then_inc(sem_out, 1)

            def inverse_root(g, name, rs, sem_out, e):
                act.wait_ge(filled[name], g + 1)
                c.link(act.activation(halves2(rs), bank2(name), ACT.Ln, bias=e[:, 0:1]))
                act.activation(A[rs], A[rs], ACT.Exp, scale=-0.5).then_inc(sem_out, 1)

            def square_h(g):
                act.wait_ge(s_h, g * 2 + 2)
                wait(act, filled["var3"], g)
                act.activation(A["sq_b"], A["h"], ACT.Square).then_inc(s_sq2, 1)

            def forget(g):
                act.wait_ge(s_fpos, g + 1)
                wait(act, s_fs_arg, g)
                c.link(act.activation(halves2("lf"), bank2("f"), ACT.Abs, bias=acol[:, 4:5]))
                c.link(act.activation(A["lf"], A["lf"], ACT.Exp, scale=-1.0))
                act.activation(A["lf"], A["lf"], ACT.Ln, bias=one[:, 0:1]).then_inc(s_l1, 1)

            def inputs(g):
                act.wait_ge(filled["i"], g + 1)
                wait(act, s_is_arg, g)
                c.link(act.activation(halves2("li"), bank2("i"), ACT.Exp, bias=bias_i[:, 0:1], scale=0.2))
                c.link(act.activation(A["li"], A["li"], ACT.Ln, bias=one[:, 0:1]))
                act.activation(A["li"], A["li"], ACT.Exp, scale=-1.0).then_inc(s_ti, 1)

            def project(g, name, dst, bias, scale, sem_out, free, count):
                act.wait_ge(filled[name], g + 1)
                wait(act, free, count)
                act.activation(halves2(dst), bank2(name), ACT.Identity, bias=bias, scale=scale).then_inc(sem_out, 1)

            def output_gate(g):
                act.wait_ge(filled["o"], g + 1)
                wait(act, s_garg, g * 2)
                c.link(act.activation(halves2("o_log"), bank2("o"), ACT.Exp, bias=bias_o[:, 0:1], scale=-1.0))
                act.activation(A["o_log"], A["o_log"], ACT.Ln, bias=one[:, 0:1]).then_inc(s_og, 1)

            def exp_in_place(g, name, sem_in, count, sem_out, free=None, free_count=0):
                act.wait_ge(sem_in, count)
                act.activation(A[name], A[name], ACT.Exp).then_inc(sem_out, 1)

            def decays(g):
                act.wait_ge(s_s_arg, g + 1)
                wait(act, s_h, g * 2)
                act.activation(s_dec[:, :, 0:2], s_arg[:, :, :], ACT.Exp).then_inc(s_s, 1)

            def values(g):
                act.wait_ge(filled["vt"], g + 1)
                wait(act, filled["hacc"], g * 2)
                tile = TILE["vt"][:, :, :].rearrange("p c (g s) -> p c g s", g=2)
                act.activation(vt[:, :, 0:128].rearrange("p (c g) s -> p c g s", g=2), tile[:, :, :, 0:128], ACT.Copy)
                act.activation(vt[0:T2, :, 128:256].rearrange("p (c g) s -> p c g s", g=2), tile[0:T2, :, :, 128:256],
                               ACT.Copy).then_inc(s_vt, 1)

            def abs_den(g):
                act.wait_ge(filled["den"], g + 1)
                wait(act, s_garg, g * 2)
                act.activation(halves2("den"), bank2("den"), ACT.Abs).then_inc(s_den, 1)

            def log_den(g):
                act.wait_ge(s_dmax, g + 1)
                act.activation(A["den"], A["den"], ACT.Ln).then_inc(s_lden, 1)

            def turned_copy(g):
                act.wait_ge(filled["tm"], g * 2 + 2)
                wait(act, s_sav, g * 32)
                copy_turned(lambda o, i: act.activation(o, i, ACT.Copy), 1).then_inc(s_tmA, 1)

            root(0, 0)
            high(0, 0, s_conv[1], 0)
            act.wait_ge(s_acon, 1)

            def turn(t):
                if on(t - 1):
                    root(2, t - 1)
                    high(2, t - 1, s_conv[3], (t - 1) * 2)
                if on(t):
                    relu(1, t, 0)
                if on(t - 2):
                    tokens(t - 2)
                if on(t - 3):
                    square_h(t - 3)
                if on(t):
                    relu(1, t, 1)
                if on(t - 3):
                    inverse_root(t - 3, "ms", "rs_b", s_rs2, eps8)
                if on(t - 2):
                    centred_square(t - 2, "cx1", "xn", filled["o"], t - 2, "sq", s_cx1, s_sq1)
                if on(t):
                    relu(1, t, 2)
                if on(t - 2):
                    inverse_root(t - 2, "var1", "rs", s_rs1, eps)
                if on(t - 3):
                    centred_square(t - 3, "cx3", "xn2", filled["lg"], t - 3, "sq_b", s_cx3, s_sq3)
                if on(t):
                    root(1, t)
                if on(t - 1):
                    relu(3, t - 1, 0)
                if on(t - 3):
                    inverse_root(t - 3, "var3", "rs_b", s_rs3, eps)
                if on(t):
                    high(1, t, s_conv[2], t * 2)
                if on(t - 2):
                    forget(t - 2)
                    inputs(t - 2)
                    project(t - 2, "k", "kT", bias_k[:, 0:1], 0.125, s_k, filled["sc"], (t - 2) * 4)
                if on(t - 1):
                    relu(3, t - 1, 1)
                if on(t - 2):
                    project(t - 2, "v", "vT", acol[:, 2:3], 1.0, s_v, s_vp, t - 2)
                    project(t - 2, "q", "qT", acol[:, 0:1], 1.0, s_q, filled["sc"], (t - 2) * 4)
                    output_gate(t - 2)
                    exp_in_place(t - 2, "wv", s_e_arg, t - 1, s_e)
                    decays(t - 2)
                    exp_in_place(t - 2, "t_f", s_fs_arg, t - 1, s_fs)
                    exp_in_place(t - 2, "t_i", s_is_arg, t - 1, s_is)
                if on(t - 1):
                    root(3, t - 1)
                    high(3, t - 1, s_turn, t - 1)
                if on(t):
                    relu(2, t, 0)
                if on(t - 3):
                    turned_copy(t - 3)
                if on(t + 1):
                    root(0, t + 1)
                    high(0, t + 1, s_conv[1], t * 3 + 3)
                if on(t):
                    relu(2, t, 1)
                if on(t - 2):
                    abs_den(t - 2)
                    values(t - 2)
                    log_den(t - 2)
                    exp_in_place(t - 2, "gexp", s_garg, (t - 2) * 2 + 2, s_g)
                if on(t - 1):
                    turned(t - 1)

            turns(act, c, ACT_LINKS, turn)

            act.wait_ge(s_fw, 16 * 9)
            act.activation(fw1_hi, raw1, ACT.Copy, scale=FW_SCALE).then_inc(s_fhi, 1)
            act.activation(fw2_hi, raw2, ACT.Copy, scale=FW_SCALE).then_inc(s_fhi, 1)
            act.activation(fb2[0:2, :], rawb[0:2, :], ACT.Copy, scale=FW_SCALE).then_inc(s_fhi, 1)
            act.wait_ge(s_gexp, 1)
            act.activation(gate[1], gate[1], ACT.Exp).then_inc(s_gexp2, 1)
            act.wait_ge(s_fmade, 4)
            act.wait_ge(s_tmap, 2)

            def step(m, h):
                turned, hidden = behind(m, h, 0), behind(m, h, 1)
                if hidden:
                    e = act.value_load(quad_i[0:1, bass.ds(hidden[0], 1)], min_val=0, max_val=E - 1)
                if turned:
                    q, _, _, two = turned
                    act.wait_ge(s_xturn, q + 1)
                    wait(act, s_mm1, q + (-1))
                    act.activation(xT[two][0:64, :], double[0][0:64, two, :], ACT.Copy, scale=XS).then_inc(s_xhi, 1)
                if hidden:
                    q, _, _, two = hidden
                    act.wait_ge(s_mm1, q + 1)
                    wait(act, s_hlo, q + (-1))
                    act.activation(hid[two], double[1][:, two, :], ACT.Relu, bias=fb1s[:, bass.ds(e, 1)],
                                   scale=H_SCALE / (XS * FW_SCALE)).then_inc(s_hid, 1)

            slots(act, step)
            for k in range(CHUNKS):
                for h, (lo, hi) in enumerate(PARTS):
                    r = slice(lo, hi)
                    act.wait_ge(s_yvar, 2 * k + h + 1)
                    c.link(act.activation(y_rstd[:, r], y_var[:, r], ACT.Ln, bias=eps[:, 0:1], scale=1.0 / D_))
                    act.activation(y_rstd[:, r], y_rstd[:, r], ACT.Exp, scale=-0.5).then_inc(s_yr, 1)

        @block.gpsimd
        def _(pool):
            for n in PROJ:
                pool.memset(w_proj[n][:, :], 0.0)
            pool.memset(zeros[:, :], 0.0)
            pool.memset(w_gate[:, :], 0.0).then_inc(s_az, 1)
            pool.iota(e_minus[:, :], pattern=[[1, E]], base=-E, channel_multiplier=0, allow_small_or_imprecise_dtypes=True)
            pool.memset(before[:, :], 1.0)
            pool.memset(all_ones[:, :], 1.0)
            for k, t in enumerate((act1, act2, act3)):
                v = t[:, :, :, :, :].rearrange("p h w b j -> p (h w b) j")
                pool.memset(v[:, :, 0:2], 0.0)
                pool.memset(v[:, :, 2 + J:JP], 0.0)
            pool.memset(average[:, :], 0.0)
            pool.memset(total[:, :], 0.0)
            pool.memset(causal[:, :], 1.0)
            pool.memset(ident32[:, :], 0.0)
            pool.memset(ident[:, :], 0.0).then_inc(s_pad, 1)
            pool.wait_ge(s_pad, 1)
            for h in range(2):
                q = slice(64 * h, 64 * h + 64)
                pool.memset(average[q, q], 1.0 / 64).then_inc(s_pad, 1)
                pool.wait_ge(s_pad, 2 + 2 * h)
                pool.memset(total[q, q], 1.0).then_inc(s_pad, 1)
                pool.wait_ge(s_pad, 3 + 2 * h)
            for m in (ident, ident32):
                pool.affine_select(out=m[:, :], in_=m[:, :], compare_op=ALU.not_equal, fill=1.0, base=0,
                                   pattern=[[-1, 128]], channel_multiplier=1).then_inc(s_pad, 1)
            for lo, n in ((0, S), (S, T2)):
                pool.affine_select(out=causal[:, lo:lo + n], in_=causal[:, lo:lo + n], compare_op=ALU.is_ge, fill=0.0, base=0,
                                   pattern=[[1, n]], channel_multiplier=-1).then_inc(s_pad, 1)
            pool.affine_select(out=before[:, :], in_=before[:, :], compare_op=ALU.is_gt, fill=0.0, base=0,
                               pattern=[[1, 128]], channel_multiplier=-1).then_inc(s_pad, 1)
            pool.wait_ge(s_pad, 10)

            def low(k, i, free, count):
                pool.wait_ge(s_hi[k], i + 1)
                wait(pool, free, count)
                for w in range(COLS[k]):
                    last = pool.tensor_tensor(halves(k, 1)[:, w], full_of(k)[:, w], halves(k, 0)[:, w], ALU.subtract)
                last.then_inc(s_lo[k], 1)

            low(0, 0, s_conv[1], 0)

            def turn(t):
                if on(t - 1):
                    low(2, t - 1, s_conv[3], (t - 1) * 2)
                if on(t):
                    low(1, t, s_conv[2], t * 2)
                if on(t - 1):
                    low(3, t - 1, s_turn, t - 1)
                if on(t + 1):
                    low(0, t + 1, s_conv[1], t * 3 + 3)

            turns(pool, None, 0, turn)

            pool.wait_ge(s_lgin, 16)
            pool.iota(quad_no, pattern=[[1, QUADS]], base=0, channel_multiplier=0, allow_small_or_imprecise_dtypes=True).then_inc(s_tmap, 1)
            pool.wait_ge(s_slot, 2)
            pool.wait_ge(s_zero, 16 * -(-ROWS // 1024))
            for k in range(CHUNKS):
                for h, (lo, hi) in enumerate(PARTS):
                    pool.wait_ge(s_xpart[h], 16 * (k + 1))
                    for t in range(lo, hi):
                        for m in range(2):
                            pool.indirect_dma_start(xs_dram, bass.IndirectOffsetOnAxis(ap=slot[m][:, k * CH + t:k * CH + t + 1], axis=0),
                                                    xn_part[:, t, :], None).then_inc(s_scat[h], 16)
            def step(m, h):
                hidden = behind(m, h, 2)
                if hidden:
                    q, _, _, two = hidden
                    pool.wait_ge(s_hhi, q + 1)
                    pool.tensor_tensor(hid_lo[two], hid[two], hid_hi[two], ALU.subtract).then_inc(s_hlo, 1)

            slots(pool, step)
            pool.wait_ge(s_done, 1)
            for k in range(CHUNKS):
                for h, (lo, hi) in enumerate(PARTS):
                    if k:
                        pool.wait_ge(s_yvar, 2 * k + h - 1)
                    for t in range(lo, hi):
                        for m in range(2):
                            pool.indirect_dma_start(got[:, t, m, :], None, es_dram,
                                                    bass.IndirectOffsetOnAxis(ap=slot[m][:, k * CH + t:k * CH + t + 1], axis=0)).then_inc(s_got[h], 16)

        @block.tensor
        def _(pe):
            def conv(k, i, w):
                wide = 2 * T if k == 3 else T
                src = (act1, act2, act3)[k - 1]
                if k == 1:
                    taps = [(kh, w_in - w + 1, w_in) for w_in in range(3) if 0 <= w_in - w + 1 < 3 for kh in range(5)]
                elif k == 2:
                    taps = [(kh, kw, w + kw) for kw in range(2) for kh in range(5)]
                else:
                    taps = [(kh, kw, kw) for kw in range(2) for kh in range(5)]
                kws = 3 if k == 1 else 2
                pe.wait_ge(s_lo[k - 1], i + 1)
                dst = take(pe, f"c{k}{w}", i)[:, :].rearrange("p (b j) -> p b j", b=GB)
                n, last_n = 0, 3 * len(taps) - 1
                for kh, kw, w_in in taps:
                    o = (kh * kws + kw) * wide + (w * T if k == 3 else 0)
                    for wt, half in ((w_hi, 0), (w_hi, 1), (w_lo, 0)):
                        mm = pe.matmul(dst, wt[k][:, o:o + T], src[:, half, w_in, :, kh:kh + J], start=(n == 0), stop=(n == last_n))
                        n += 1
                mm.then_inc(s_conv[k], 1)

            def turn_result(i):
                pe.wait_ge(s_lo[3], i + 1)
                tile = take(pe, "turned", i)
                for h in range(2):
                    for b in range(GB):
                        mm = pe.transpose(tile[:, h, :].bitcast(F16)[:, 128 * b:128 * b + 128], res[:, h, b, :], ident[:, :])
                mm.then_inc(s_turn, 1)

            def tokens(i):
                pe.wait_ge(s_rT, i + 1)
                tile = take(pe, "tok", i)
                for q in range(2):
                    for n, (wt, half) in enumerate(((w_hi, 0), (w_hi, 1), (w_lo, 0))):
                        mm = pe.matmul(tile[64 * q:64 * q + 64, 0, :].rearrange("p (b t) -> p b t", b=4), wt[4][:, :],
                                       resT[:, half].rearrange("p (b q) t -> p q b t", q=2)[:, q], start=(n == 0), stop=(n == 2))
                mm.then_inc(s_tok, 1)

            def product(g, name, weights, src):
                tile = take(pe, name, g)
                for n in range(2):
                    mm = pe.matmul(tile[:, n, 0:HALF], weights[:, :], halves2(src)[:, n], start=True, stop=True)
                mm.then_inc(filled[name], 1)

            def scores(g, n):
                if n == 0:
                    pe.wait_ge(s_k, g + 1)
                    pe.wait_ge(s_q, g + 1)
                tile = take(pe, f"sc{n}", g)
                for h in range(2):
                    q = slice(64 * h, 64 * h + 64)
                    k_, q_ = A["kT"][q, n, :], A["qT"][q, n, :]
                    pe.matmul(tile[:, h, 0:S], k_[:, 0:128], q_, start=True, stop=True)
                    mm = pe.matmul(tile[0:T2, h, S:S + T2], k_[:, 128:S], q_[:, 128:S], start=True, stop=True)
                mm.then_inc(filled["sc"], 1)

            def turn_values(g):
                pe.wait_ge(s_vp, g + 1)
                tile = take(pe, "vt", g)
                for p in range(GP):
                    o = 256 * (p % 2)
                    pe.transpose(tile[:, p // 2, o:o + 128], A["wv"][:, p, 0:128], ident32[:, :])
                    mm = pe.transpose(tile[0:T2, p // 2, o + 128:o + 256], A["wv"][:, p, 128:S], ident32[:, :])
                mm.then_inc(filled["vt"], 1)

            def sums(g, n):
                pe.wait_ge(s_vt, g + 1)
                pe.wait_ge(s_st, g * 4 + 4)
                tile = take(pe, f"hacc{n}", g)
                for c_ in range(2):
                    p = 2 * n + c_
                    for h in range(2):
                        o = slice(64 * h, 64 * h + 64)
                        b = 2 * p + h
                        v0, v1, v2 = (vt[r, p, 128 * s_ + 64 * h:128 * s_ + 64 * h + 64]
                                      for r, s_ in ((slice(0, 64), 0), (slice(64, 128), 0), (slice(0, T2), 1)))
                        at = 218 * c_
                        pe.matmul(tile[o, 1, at + 141:at + 218], v2, st[0:T2, b, S:S + T2], start=True, stop=True)
                        pe.matmul(tile[o, 0, S * c_:S * c_ + S], v0, st[0:64, b, 0:S], start=True, stop=True)
                        mm = pe.matmul(tile[o, 1, at:at + 141], v1, st[64:128, b, 64:S], start=True, stop=True)
                mm.then_inc(filled["hacc"], 1)

            def turn_tokens(g, n):
                tile = take(pe, f"tm{n}", g)
                for c_ in range(2):
                    for k, name in enumerate(("xn2", "h2")):
                        src = A[name][:, 2 * n + c_, :]
                        pe.transpose(tile[:, c_, 256 * k:256 * k + 128], src[:, 0:128], ident32[:, :])
                        mm = pe.transpose(tile[0:T2, c_, 256 * k + 128:256 * k + 256], src[:, 128:S], ident32[:, :])
                mm.then_inc(filled["tm"], 1)

            def logits(g):
                tile = take(pe, "lg", g)
                for p in range(GP):
                    src = A["xn2"][:, p, :]
                    pe.matmul(tile[:, 0, 32 * p:32 * p + 32], src[:, 0:128], w_gate[:, :], start=True, stop=True)
                    mm = pe.matmul(tile[0:T2, 0, 128 + 32 * p:160 + 32 * p], src[:, 128:S], w_gate[:, :], start=True, stop=True)
                mm.then_inc(filled["lg"], 1)

            pe.wait_ge(s_wlo, 4)
            pe.wait_ge(s_pad, 10)
            pe.wait_ge(s_acon, 1)
            pe.wait_ge(s_aw, 16 * 14)

            def turn(t):
                if on(t):
                    conv(1, t, 0)
                if on(t - 3):
                    for n in range(2):
                        sums(t - 3, n)
                if on(t - 2):
                    tokens(t - 2)
                if on(t):
                    conv(1, t, 1)
                if on(t - 3):
                    pe.wait_ge(s_sq2, t - 2)
                    product(t - 3, "ms", average, "sq_b")
                if on(t - 2):
                    pe.wait_ge(s_H, (t - 2) * 2 + 2)
                    pe.wait_ge(s_txt, (t - 2) * 16 + 16)
                    product(t - 2, "cx1", centre, "tokens")
                if on(t):
                    conv(1, t, 2)
                if on(t - 2):
                    pe.wait_ge(s_sq1, t - 1)
                    product(t - 2, "var1", average, "sq")
                if on(t - 3):
                    pe.wait_ge(s_h2, t - 2)
                    product(t - 3, "cx3", centre, "h2")
                if on(t - 1):
                    conv(3, t - 1, 0)
                if on(t - 3):
                    pe.wait_ge(s_sq3, t - 2)
                    product(t - 3, "var3", average, "sq_b")
                if on(t - 2):
                    pe.wait_ge(s_xn, t - 1)
                    for name in PROJ[0:3]:
                        product(t - 2, name, w_proj[name], "xn")
                if on(t - 1):
                    conv(3, t - 1, 1)
                if on(t - 2):
                    for name in PROJ[3:6]:
                        product(t - 2, name, w_proj[name], "xn")
                if on(t):
                    conv(2, t, 0)
                if on(t - 3):
                    pe.wait_ge(s_xn2, t - 2)
                    for n in range(2):
                        turn_tokens(t - 3, n)
                    logits(t - 3)
                if on(t - 2):
                    for n in range(4):
                        scores(t - 2, n)
                if on(t):
                    conv(2, t, 1)
                if on(t - 2):
                    pe.wait_ge(s_nq, t - 1)
                    product(t - 2, "den", total, "nq")
                    turn_values(t - 2)
                if on(t - 1):
                    turn_result(t - 1)

            turns(pe, None, 0, turn)

            pe.wait_ge(s_cnt, 1)
            pe.matmul(double[0][:, 0, 0:E], before[:, :], counts[:, :], start=True, stop=True)
            pe.matmul(double[0][:, 0, E:2 * E], all_ones[:, :], counts[:, :], start=True, stop=True).then_inc(s_off, 1)
            pe.wait_ge(s_fmade, 4)
            pe.wait_ge(s_tmap, 2)

            def expert_of(q):
                return pe.value_load(quad_i[0:1, bass.ds(q, 1)], min_val=0, max_val=E - 1)

            def step(m, h):
                result, turned, hidden = behind(m, h, 3), behind(m, h, 0), behind(m, h, 1)
                if result:
                    w2_ = bass.ds(expert_of(result[0]) * D_, D_)
                if hidden:
                    w1_ = bass.ds(expert_of(hidden[0]) * F, F)
                if result:
                    q, _, _, two = result
                    pe.wait_ge(s_hlo, q + 1)
                    wait(pe, s_o, q + (-1))
                    for n in range(4):
                        dst, c_ = double[2][:, two, 64 * n:64 * n + 64], slice(128 * n, 128 * n + 128)
                        pe.matmul(dst, hid_hi[two][:, c_], fw2_hi[:, w2_], start=True, stop=False)
                        pe.matmul(dst, hid_hi[two][:, c_], fw2_lo[:, w2_], start=False, stop=False)
                        pe.matmul(dst, hid_lo[two][:, c_], fw2_hi[:, w2_], start=False, stop=False)
                        mm = pe.matmul(dst, ones_h[:, :], fb2[0:2, w2_], start=False, stop=True)
                    mm.then_inc(s_mm2, 1)
                if turned:
                    q, turn, ring, two = turned
                    pe.wait_ge(s_xt[ring], turn * 16 + 16)
                    wait(pe, s_xlo, q + (-1))
                    for n in range(4):
                        mm = pe.matmul(double[0][0:64, two, 128 * n:128 * n + 128], x_tiles[ring][:, n, :], ident32[:, :], start=True, stop=True)
                    mm.then_inc(s_xturn, 1)
                if hidden:
                    q, _, _, two = hidden
                    pe.wait_ge(s_xlo, q + 1)
                    wait(pe, s_hid, q + (-1))
                    pe.matmul(double[1][:, two, :], fw1_hi[:, w1_], xT[two], start=True, stop=False)
                    pe.matmul(double[1][:, two, :], fw1_lo[:, w1_], xT[two], start=False, stop=True).then_inc(s_mm1, 1)

            slots(pe, step)


def kernel(**kw):
    import numpy as np
    import concourse.bacc as bacc
    from concourse.bass_utils import run_bass_kernel_spmd as run

    nc = bacc.Bacc("TRN2", target_bir_lowering=False, num_devices=1)
    kw = {n: np.asarray(v) for n, v in kw.items()}
    k = {n[7:]: v for n, v in kw.items() if n.startswith("L0_tok")}
    at = {n[8:]: v for n, v in kw.items() if n.startswith("L0_attn")}
    ff = {n[7:]: v for n, v in kw.items() if n.startswith("L0_ffn")}
    c = np.ascontiguousarray
    bg = at["bg"]
    arr = {
        "x": c(kw["x"].reshape(16, 8, 128, 192).transpose(0, 2, 1, 3).reshape(16, 128, 1536)),
        "txt": c(kw["txt"].reshape(16, 4, 2, 77, 64).transpose(0, 2, 4, 1, 3).reshape(16, 128, 4, 77)),
        "w1": c(k["conv1_w"].transpose(1, 2, 3, 0).reshape(128, -1)),
        "w2": c(k["conv2_w"].transpose(1, 2, 3, 0).reshape(128, -1)),
        "w3": c(k["conv3_w"].transpose(1, 2, 3, 0).reshape(128, -1)),
        "w4": k["out_w"],
        **{n: k[n] for n in ("conv1_b", "conv2_b", "conv3_b", "out_b", "ln0_g", "ln0_b", "ln1_g", "ln1_b")},
        "w_q": at["Wq"], "w_k": at["Wk"], "w_v": at["Wv"],
        "w_i": c(at["Wg"][:, 0:64]), "w_f": c(at["Wg"][:, 64:128]), "w_o": c(at["Wg"][:, 128:192]),
        "acol": c(np.stack([at["bq"], at["bk"], at["bv"], bg[0:64], bg[64:128], bg[128:192], at["input_bias"], at["norm_scale"]], axis=1)),
        "gate_w": ff["gate_w"], "gate_b": ff["gate_b"],
        "ffn_w1": c(ff["w1"].transpose(1, 0, 2)), "ffn_w2": c(ff["w2"].transpose(1, 0, 2)),
        "ffn_b1": c(ff["b1"].T), "ffn_b2": c(ff["b2"].reshape(1, -1)),
        "ffn_gamma": ff["gamma"], "ffn_beta": ff["beta"],
        "row_sel": np.eye(2, dtype=np.float32),
    }
    aps = {n: nc.dram_tensor("in_" + n, v.shape, mybir.dt.from_np(v.dtype), kind="ExternalInput").ap() for n, v in arr.items()}
    o = nc.dram_tensor("o_d", (128, 205, 64), F32, kind="ExternalOutput").ap()
    build(nc, aps, o)
    r = run(nc, [{"in_" + n: v for n, v in arr.items()}], core_ids=[0])
    return r.results[0]["o_d"]
```

```python
import concourse.bass as bass
from concourse import mybir
from contextlib import ExitStack

F32 = mybir.dt.float32
F16 = mybir.dt.float16
ALU = mybir.AluOpType
ACT = mybir.ActivationFunctionType
AX = mybir.AxisListType


class Chain:

    def __init__(self, eng, sem):
        self.eng, self.sem, self.base, self.n = eng, sem, 0, 0

    def link(self, ins):
        self.n += 1
        ins.then_inc(self.sem, 1)
        self.eng.wait_ge(self.sem, self.base + self.n)

    def enter(self, i, first, per_turn):
        self.start, self.per_turn = self.base + self.n, per_turn
        self.base, self.n = i * per_turn + (self.start - first * per_turn), 0

    def leave(self, turns):
        assert self.n == self.per_turn, (self.n, self.per_turn)
        self.base, self.n = self.start + turns * self.per_turn, 0


def build(nc, a, out):
    B, T, J = 128, 128, 64
    GB = 8
    NG = B // GB
    JP = J + 4
    T2 = 77
    S = T + T2
    NP = B // 2
    XS, WS = 256.0, 1024.0
    UNSCALE = 1.0 / (XS * WS)
    EPS = 1e-5

    with ExitStack() as ctx:
        def sb(name, shape, dt=F32):
            return ctx.enter_context(nc.sbuf_tensor(name, shape, dt))

        def sem(name):
            return ctx.enter_context(nc.semaphore(name))

        conv_bank = [ctx.enter_context(nc.psum_tensor(f"conv_bank{k}", [128, 512], F32)) for k in range(2)]

        WID = {1: 15 * T, 2: 10 * T, 3: 10 * 2 * T, 4: 64}
        w_hi = {k: sb(f"w_hi{k}", [128, n], F16) for k, n in WID.items()}
        w_lo = {k: sb(f"w_lo{k}", [128, n], F16) for k, n in WID.items()}
        cb = sb("cb", [128, 5])
        eps = sb("eps", [128, 1])
        gam, bet = ([sb(f"{kind}{k}", [128, n]) for k, n in enumerate((192, 128, 128))] for kind in ("gam", "bet"))
        gam, bet = gam[:1] + gam, bet[:1] + bet

        x_in = sb("x_in", [128, GB, 192])
        h_relu = [None, sb("h1", [128, 3, GB, J]), sb("h2", [128, 2, GB, J]), sb("h3", [128, GB, 2, J])]
        stats = [sb(f"stats{k}", [128, GB, 6]) for k in range(4)]
        mean = [sb(f"mean{k}", [128, GB]) for k in range(4)]
        var4 = [sb(f"var4_{k}", [128, GB]) for k in range(4)]
        spread, half_mean, gap, gap2 = (sb(n, [128, GB]) for n in ("spread", "half_mean", "gap", "gap2"))
        lnv = [sb(f"lnv{k}", [128, GB]) for k in range(4)]
        rstd = [sb(f"rstd{k}", [128, GB]) for k in range(4)]
        centred = sb("centred", [128, GB, 192])
        full = [sb(f"full{k}", [128, 3 * GB * J]) for k in range(2)]
        act1 = sb("act1", [128, 2, 3, GB, JP], F16)
        act2 = sb("act2", [128, 2, 3, GB, JP], F16)
        act3 = sb("act3", [128, 2, 2, GB, JP], F16)
        res = sb("res", [128, 2, GB, 128], F16)
        resT = sb("resT", [128, 2, GB, 128], F16)

        GP = GB // 2
        N = GP * S
        HALF = N // 2
        BLOCKS = ((0, 64), (64, 128), (128, S))
        double = [ctx.enter_context(nc.psum_tensor(f"double{k}", [128, 2, 512], F32)) for k in range(3)]
        PROJ = ("f", "i", "k", "v", "q", "o")
        ident32 = sb("ident32", [128, 128])
        w_proj = {n: sb(f"w_proj_{n}", [128, 128]) for n in PROJ}
        w_gate = sb("w_gate", [128, 32])
        centre = sb("centre", [128, 128])
        average = sb("average", [128, 128])
        total = sb("total", [128, 128])
        acol = sb("acol", [128, 8])
        bias_k, bias_i, bias_o = (sb(n, [128, 1]) for n in ("bias_k", "bias_i", "bias_o"))
        gate_bias = sb("gate_bias", [128, 16])
        eps8 = sb("eps8", [128, 1])
        one = sb("one", [128, 1])
        causal = sb("causal", [128, S + T2])
        not_start = sb("not_start", [128, N])
        names = ("tokens", "resid", "xn", "lf", "li", "kT", "vT", "qT", "o_log", "cum", "t_f",
                 "t_i", "wv", "nq", "gexp", "den", "h2", "xn2")
        arena = sb("arena", [128, len(names), GP, S])
        A = {n: arena[:, k] for k, n in enumerate(names)}
        for n, place in (("h", "wv"), ("sq", "t_f"), ("sq_b", "t_i"), ("rs", "nq"), ("rs_b", "den")):
            A[n] = A[place]
        def flat(name):
            return A[name].rearrange("p g s -> p (g s)")

        gb_raw = flat("xn")[:, 0:4 * 192].rearrange("p (n f) -> p n f", n=4)
        zeros = flat("lf")[:, 0:512]
        raw_room = arena[:, 10:18].rearrange("p k g s -> p (k g s)")
        w_raw, at = {}, 0
        for k, n in WID.items():
            w_raw[k] = raw_room[:, at:at + n]
            at += n
        m_ext = sb("m_ext", [128, GP, S + 1])
        decay_arg = sb("decay_arg", [128, GP, 2])
        decay = sb("decay", [128, GP, 3])
        st = sb("st", [128, GB, S + T2])
        vt = sb("vt", [128, GP, 256])
        u1 = sb("u1", [128, GP, S])
        u2 = sb("u2", [128, GP, T2])
        tm0 = sb("tm0", [128, GB, 144])
        tm1 = sb("tm1", [128, GB, 144])

        E, F, D_ = 16, 128, 64
        W = (S + 1) // 2
        STARTS = (0, S - W)
        CH = 12
        CHUNKS = [(p, c, min(c + CH, W)) for p in range(2) for c in range(0, W, CH)]
        NC = len(CHUNKS) // 2
        PIECES = 2
        PW = -(-W // PIECES)
        ROUTE = NG // 2 + 3
        TURN_COLS = -(-W // (NG + 2 - ROUTE))
        SUBS = (0, (TURN_COLS + 1) // 2, TURN_COLS)
        QR = 4 * 128
        RING = 4
        QP = -(-((2 * B * W + E * (QR - 1)) // QR) // RING) * RING
        QUADS = 2 * QP
        ZERO_ROWS = QP * QR // 2
        assert ZERO_ROWS % 1024 == 0
        H_SCALE, FW_SCALE = 64.0, 256.0
        room = arena[:, :, :, :].rearrange("p k g s -> p (k g s)")
        lay = [0]

        def carve(n):
            lay[0] += n
            assert lay[0] <= len(names) * N
            return room[:, lay[0] - n:lay[0]]

        routed = sb("routed", [128, 3, W])
        gate = [[carve(W), routed[:, 0]], [carve(W), carve(W)]]
        slot = [[routed[:, 1 + k].bitcast(mybir.dt.uint32) for k in range(2)], [carve(W).bitcast(mybir.dt.uint32) for _ in range(2)]]
        scratch_at = lay[0]

        def routing_tiles(at):
            small = [room[:, at + W * k:at + W * (k + 1)] for k in range(4)]
            at += 4 * W
            return small + [room[:, at + W * E * k:at + W * E * (k + 1)] for k in range(4)]

        ROUTING = [routing_tiles(2 * N), routing_tiles(scratch_at)]
        assert 4 * W + 4 * W * E <= 12 * N
        carve(4 * W)
        got = room[:, lay[0]:lay[0] + W * 2 * D_].rearrange("p (t k f) -> p t k f", k=2, f=D_)
        assert lay[0] + W * 2 * D_ <= len(names) * N
        carve(4 * W * E)
        xn_part = carve(W * D_).rearrange("p (t f) -> p t f", f=D_)
        xn_turn = sb("xn_turn", [128, TURN_COLS, D_])

        def flat32(t):
            letters = "abcd"[:len(t.shape) - 1]
            t = t.rearrange(f"p {' '.join(letters)} -> p ({' '.join(letters)})")
            return t

        raw1 = [flat32(t)[:, 0:E * F // 2] for t in (x_in[:, :, :], h_relu[1][:, :, :, :])]
        raw2, rawb = flat32(centred[:, :, :])[:, 0:E * D_], flat32(h_relu[2][:, :, :, :])
        x_tiles = [flat32(x_in[:, :, :])[:, 4 * D_ * k:4 * D_ * (k + 1)].rearrange("p (n f) -> p n f", f=D_) for k in range(RING)]
        o_tiles = [flat32(centred[:, :, :])[:, 4 * D_ * k:4 * D_ * (k + 1)].rearrange("p (n f) -> p n f", f=D_) for k in range(RING)]
        hid = [full[1][:, 512 * k:512 * k + 512] for k in range(2)]
        xT, hid_hi, hid_lo = ([flat32(h_relu[1][:, :, :, :])[:, 512 * n + 256 * k:512 * n + 256 * k + 256].bitcast(F16) for k in range(2)]
                              for n in range(3))
        quad_no, quad_exp = (flat32(h_relu[2][:, :, :, :])[:, k:k + QP] for k in (0, QP))
        stream = [flat32(t[:, :, :, :, :]).bitcast(F32)[:, 0:CH * 2 * D_].rearrange("p (t k f) -> p t k f", k=2, f=D_) for t in (act1, act2)]
        y_ = [flat32(t[:, :, :])[:, 0:CH * D_].rearrange("p (t f) -> p t f", f=D_) for t in (tm0, tm1)]
        st_room = st[:, :, :].rearrange("p b s -> p (b s)")
        fw1_hi, fw1_lo = (st_room[:, 1024 * k:1024 * k + 1024].bitcast(F16) for k in range(2))
        fw2_hi, fw2_lo, fb2 = (full[0][:, 512 * k:512 * k + 512].bitcast(F16) for k in range(3))
        fb1 = sb("fb1", [128, E])
        fb1s = sb("fb1s", [128, E])
        ff_gb = sb("ff_gb", [128, 2, D_])
        row_sel = sb("row_sel", [2, 2])
        ones_h = sb("ones_h", [2, 128], F16)
        e_minus = sb("e_minus", [128, E])
        all_ones = sb("all_ones", [128, 128])
        before = sb("before", [128, 128])
        counts, off, quads_e = (sb(n, [128, E]) for n in ("counts", "off", "quads_e"))
        ends = [sb(f"ends{p}", [128, E]) for p in range(2)]
        quads_i = sb("quads_i", [128, E], mybir.dt.int32)
        quad_i = sb("quad_i", [128, QUADS], mybir.dt.int32)
        y_mean, y_var, y_rstd = (sb(n, [128, CH]) for n in ("y_mean", "y_var", "y_rstd"))
        xs_dram = [nc.dram_tensor(f"xs_dram{p}", [QP * QR, D_], F32).ap() for p in range(2)]
        es_dram = [nc.dram_tensor(f"es_dram{p}", [QP * QR, D_], F32).ap() for p in range(2)]

        def halves2(name):
            return flat(name).rearrange("p (c n) -> p c n", c=2)

        ident = sb("ident", [128, 128], F16)
        DVE_LINKS, ACT_LINKS = 31, 12
        mid = sb("mid", [128, GP, 3])
        tok_dram = nc.dram_tensor("tok_dram", [B, S, 144], F32).ap()
        weights_loaded = sem("weights_loaded")
        constants_loaded = sem("constants_loaded")
        x_loaded = sem("x_loaded")
        patterns_made = sem("patterns_made")
        conv_weights_hi_made = sem("conv_weights_hi_made")
        conv_weights_lo_made = sem("conv_weights_lo_made")
        dve_step_done = sem("dve_step_done")
        act_step_done = sem("act_step_done")
        variance_ready = [sem(f"var_ready{k}") for k in range(4)]
        inv_dev_ready = [sem(f"rstd_ready{k}") for k in range(4)]
        norm_ready = [sem(f"full_ready{k}") for k in range(4)]
        norm_hi_ready = [sem(f"hi_ready{k}") for k in range(4)]
        norm_lo_ready = [sem(f"lo_ready{k}") for k in range(4)]
        conv_done = [None] + [sem(f"conv_done{k}") for k in (1, 2, 3)]
        relu_done = [None] + [sem(f"relu_done{k}") for k in (1, 2, 3)]
        result_turned = sem("result_turned")
        turned_result_copied = sem("turned_result_copied")
        token_product_done = sem("token_product_done")
        tokens_ready = sem("tokens_ready")
        rows_zeroed = sem("rows_zeroed")
        expert_weights_loaded = sem("expert_weights_loaded")
        expert_weights_hi_made = sem("expert_weights_hi_made")
        expert_weights_made = sem("expert_weights_made")
        logits_loaded = sem("logits_loaded")
        counts_made = sem("counts_made")
        offsets_made = sem("offsets_made")
        gate_difference_made = sem("gate_difference_made")
        gate_exp_made = sem("gate_exp_made")
        slots_made = sem("slots_made")
        quad_numbers_made = sem("quad_numbers_made")
        quad_experts_made = sem("quad_experts_made")
        rows_loaded = [sem(f"rows_loaded{k}") for k in range(PIECES)]
        rows_scattered = [sem(f"rows_scattered{k}") for k in range(PIECES)]
        offsets_read = sem("offsets_read")
        quad_rows_loaded = [sem(f"x_tiles_loaded{k}") for k in range(4)]
        quad_rows_turned = sem("quad_rows_turned")
        quad_hi_made = sem("quad_hi_made")
        quad_lo_made = sem("quad_lo_made")
        hidden_product_done = sem("hidden_product_done")
        hidden_ready = sem("hidden_ready")
        hidden_hi_made = sem("hidden_hi_made")
        hidden_lo_made = sem("hidden_lo_made")
        expert_product_done = sem("expert_product_done")
        expert_result_copied = sem("expert_result_copied")
        expert_result_stored = [sem(f"expert_out_stored{k}") for k in range(4)]
        chunk_gathered = [sem(f"chunk_gathered{k}") for k in range(NC)]
        stream_loaded = [sem("stream_loaded0"), sem("stream_loaded1")]
        out_variance_ready = sem("out_variance_ready")
        out_inv_dev_ready = sem("out_inv_dev_ready")
        chunk_done = sem("chunk_done")
        text_loaded = sem("text_loaded")
        attn_weights_loaded = sem("attn_weights_loaded")
        attn_columns_loaded = sem("attn_columns_loaded")
        attn_weights_zeroed = sem("attn_weights_zeroed")
        attn_constants_made = sem("attn_constants_made")
        residual_kept = sem("residual_kept")
        filled = {n: sem("filled_" + n) for n in ("cx1", "var1", "f", "i", "k", "v", "q", "o", "sc", "den", "vt", "hacc",
                                                  "ms", "cx3", "var3", "tm", "lg")}
        (squares1_ready, inv_dev1_ready, xn_ready, forget_log_made, log_forget_ready, input_exp_made,
         log_input_ready, keys_ready, values_ready, queries_ready, output_gate_ready, running_max_ready,
         forget_arg_made, forget_scale_ready, input_arg_made, input_scale_ready, weight_arg_made, weight_ready,
         block_decay_arg_made, block_decay_ready, weighted_values_ready, n_times_q_ready, masked_scores_ready, turned_values_copied,
         denominator_copied, log_denominator_ready, exponent_steps_made, factor_ready, attention_out_ready, out_squares_ready,
         inv_rms_ready, new_stream_ready, squares3_ready, inv_dev3_ready, xn2_ready, logits_ready,
         tokens_saved, denominator_bounded, forget_positive_part_made, centred1_copied, centred3_copied) = (sem(n) for n in (
            "squares1_ready", "inv_dev1_ready", "xn_ready", "forget_log_made", "log_forget_ready", "input_exp_made",
            "log_input_ready", "keys_ready", "values_ready", "queries_ready", "output_gate_ready", "running_max_ready",
            "forget_arg_made", "forget_scale_ready", "input_arg_made", "input_scale_ready", "weight_arg_made", "weight_ready",
            "block_decay_arg_made", "block_decay_ready", "weighted_values_ready", "n_times_q_ready", "masked_scores_ready", "turned_values_copied",
            "denominator_copied", "log_denominator_ready", "exponent_steps_made", "factor_ready", "attention_out_ready", "out_squares_ready",
            "inv_rms_ready", "new_stream_ready", "squares3_ready", "inv_dev3_ready", "xn2_ready", "logits_ready",
            "tokens_saved", "denominator_bounded", "forget_positive_part_made", "centred1_copied", "centred3_copied"))
        token_rows_copied = [sem(f"turned_tokens_copied{k}") for k in range(2)]
        chunk_stored = [sem("out_stored0"), sem("out_stored1")]

        block = ctx.enter_context(nc.Block())

        COLS = (3, 3, 2, 2)

        def source(k, b):
            if k == 0:
                return x_in[:, b, :].rearrange("p (j w) -> p w j", w=3)
            return h_relu[k][:, :, b, :] if k < 3 else h_relu[3][:, b, :, :]

        def full_of(k):
            w = COLS[k]
            f = full[k % 2][:, 0:w * GB * J]
            return f.rearrange("p (w b j) -> p w b j", w=w, b=GB) if k < 3 else f.rearrange("p (b w j) -> p w b j", w=w, b=GB)

        def halves(k, h):
            if k == 3:
                return res[:, h].rearrange("p b (w j) -> p w b j", w=2)
            return (act1, act2, act3)[k][:, h, :, :, 2:2 + J]

        def columns(t, k):
            return t.rearrange("p (w j) -> p w j", w=COLS[k])

        ORDER, D = [], 0
        for name, lag, reader, per, at in (
                ("c10", 0, relu_done[1], 3, 1), ("turned", 2, turned_result_copied, 1, 1), ("hacc0", 3, attention_out_ready, 2, 1), ("hacc1", 3, attention_out_ready, 2, 2), ("tok", 2, tokens_ready, 2, 2),
                ("c11", 0, relu_done[1], 3, 2), ("ms", 3, inv_rms_ready, 1, 1), ("cx1", 2, centred1_copied, 1, 1),
                ("c12", 0, relu_done[1], 3, 3), ("var1", 2, inv_dev1_ready, 1, 1), ("cx3", 3, centred3_copied, 1, 1),
                ("c30", 1, relu_done[3], 2, 1), ("var3", 3, inv_dev3_ready, 1, 1), ("f", 2, forget_log_made, 1, 1), ("i", 2, input_exp_made, 1, 1), ("k", 2, keys_ready, 1, 1),
                ("c31", 1, relu_done[3], 2, 2), ("v", 2, values_ready, 1, 1), ("q", 2, queries_ready, 1, 1), ("o", 2, output_gate_ready, 1, 1),
                ("c20", 0, relu_done[2], 2, 1), ("tm0", 3, token_rows_copied[0], 1, 1), ("tm1", 3, token_rows_copied[1], 1, 1), ("lg", 3, logits_ready, 1, 1),
                ("sc0", 2, masked_scores_ready, 4, 1), ("sc1", 2, masked_scores_ready, 4, 2), ("sc2", 2, masked_scores_ready, 4, 3), ("sc3", 2, masked_scores_ready, 4, 4),
                ("c21", 0, relu_done[2], 2, 2), ("den", 2, denominator_copied, 1, 1), ("vt", 2, turned_values_copied, 1, 1)):
            if name[0] == "c" and name[1] in "123":
                tile = conv_bank[(len(ORDER) - D) % 2]
            else:
                tile = double[D % 3]
                D += 1
            ORDER.append((name, lag, tile, reader, per, at))
        assert D == 24
        TURNS = NG + 3
        TILE = {name: tile for name, _, tile, _, _, _ in ORDER}
        LAG = {name: lag for name, lag, *_ in ORDER}
        BEFORE = {}
        last_in = {}
        for t in range(TURNS):
            for name, lag, tile, reader, per, at in ORDER:
                g = t - lag
                if 0 <= g < NG:
                    BEFORE[name, g] = last_in.get(id(tile))
                    last_in[id(tile)] = (reader, per, at, g)

        STEADY = 5
        LOOP = (4, ROUTE)
        for t in range(*LOOP):
            for name, lag, *_ in ORDER:
                b, c = BEFORE[name, t - lag], BEFORE[name, STEADY - lag]
                assert b[:3] == c[:3] and b[3] - t == c[3] - STEADY

        def take(pe, name, g):
            like = g if isinstance(g, int) else STEADY - LAG[name]
            before = BEFORE[name, like]
            if before:
                reader, per, at, b = before
                pe.wait_ge(reader, g * per + ((b - like) * per + at))
            return TILE[name]

        def on(g):
            return not isinstance(g, int) or 0 <= g < NG

        def piece(k):
            return k * PW, min((k + 1) * PW, W)

        def sub(t, h):
            at = (t - ROUTE - 1) * TURN_COLS
            return at + SUBS[h], min(at + SUBS[h + 1], W)

        def sub_total(t, h):
            return sum(sub(u, h)[1] - sub(u, h)[0] for u in range(ROUTE + 1, t))

        def both_halves(eng, p, lo, hi, sem, move):
            for h in range(2):
                dst, src = move(slice(64 * h, 64 * h + 64), slice(64 * p, 64 * p + 64), STARTS[h] + lo, STARTS[h] + hi)
                eng.dma_start(dst, src).then_inc(sem, 16)

        def slots(eng, step, first=2, last=(QUADS - RING) // RING, prologue=0, end=QUADS + 3):
            for j in range(prologue * RING, first * RING):
                step(j // RING, j % RING)
            with eng.Fori(first, last) as m:
                for h in range(RING):
                    step(m, h)
            for j in range(last * RING, end):
                step(j // RING, j % RING)

        def behind(m, h, lag):
            q = m * RING + (h - lag)
            if isinstance(q, int) and not 0 <= q < QUADS:
                return None
            return q, m + (h - lag) // RING, (h - lag) % RING, (h - lag) % 2

        def turns(eng, c, links, turn):
            for t in range(0, LOOP[0]):
                turn(t)
            with eng.Fori(*LOOP) as t:
                if c:
                    c.enter(t, LOOP[0], links)
                turn(t)
            if c:
                c.leave(LOOP[1] - LOOP[0])
            for t in range(LOOP[1], TURNS):
                turn(t)

        def wait(eng, s, count):
            if not (isinstance(count, int) and count <= 0):
                eng.wait_ge(s, count)

        def copy_turned(copy, n):
            tile = TILE[f"tm{n}"][:, :, :].rearrange("p g (k s b f) -> p k s g b f", k=2, s=2, b=2)
            for s_, (dst, rows) in enumerate(((tm0, 128), (tm1, T2))):
                for k in range(2):
                    rowsof = dst[0:rows, 4 * n:4 * n + 4, 64 * k:64 * k + 64].rearrange("p (g b) f -> p g b f", g=2)
                    last = copy(rowsof, tile[0:rows, k, s_])
            return last

        @block.sync
        def _(sp):
            for k in (1, 2, 3, 4):
                sp.dma_start(w_raw[k], a[f"w{k}"]).then_inc(weights_loaded, 16)
            with nc.allow_non_contiguous_dma(reason="a few bias columns"):
                sp.dma_start(cb[:, 0:1], a["conv1_b"].rearrange("(p o) -> p o", o=1)).then_inc(constants_loaded, 16)
                sp.dma_start(cb[:, 1:2], a["conv2_b"].rearrange("(p o) -> p o", o=1)).then_inc(constants_loaded, 16)
                sp.dma_start(cb[:, 2:4], a["conv3_b"].rearrange("(h p) -> p h", h=2)).then_inc(constants_loaded, 16)
                for h in range(2):
                    sp.dma_start(cb[64 * h:64 * h + 64, 4:5], a["out_b"].rearrange("(p o) -> p o", o=1)).then_inc(constants_loaded, 16)
            for n, name in enumerate(("ln0_g", "ln0_b", "ln1_g", "ln1_b")):
                m = 192 if n < 2 else 128
                sp.dma_start(gb_raw[:, n, 0:m], a[name].rearrange("(o n) -> o n", o=1).to_broadcast([128, m])).then_inc(constants_loaded, 16)

            def load_x(i):
                wait(sp, norm_ready[0], i)
                sp.dma_start(x_in[:, :, :].rearrange("p b f -> p (b f)"), a["x"][i]).then_inc(x_loaded, 16)

            load_x(0)
            sp.wait_ge(attn_weights_zeroed, 1)
            for h in range(2):
                q = slice(64 * h, 64 * h + 64)
                for n in PROJ:
                    sp.dma_start(w_proj[n][q, q], a["w_" + n]).then_inc(attn_weights_loaded, 16)
                sp.dma_start(w_gate[q, 16 * h:16 * h + 16], a["gate_w"]).then_inc(attn_weights_loaded, 16)
                sp.dma_start(acol[q, :], a["acol"]).then_inc(attn_columns_loaded, 16)
            sp.dma_start(gate_bias[:, :], a["gate_b"].rearrange("(o n) -> o n", o=1).to_broadcast([128, 16])).then_inc(attn_columns_loaded, 16)
            for x in xs_dram:
                for r in range(0, QP * QR, ZERO_ROWS):
                    sp.dma_start(x[r:r + ZERO_ROWS].rearrange("(p n f) d -> p n (f d)", p=128, f=8),
                                 zeros.unsqueeze(1).to_broadcast([128, ZERO_ROWS // 1024, 512])).then_inc(rows_zeroed, 16)

            def text(g):
                wait(sp, residual_kept, g)
                wait(sp, centred1_copied, g)
                sp.dma_start(A["tokens"][:, :, T:S], a["txt"][g]).then_inc(text_loaded, 16)

            def save(g):
                sp.wait_ge(token_rows_copied[0], g + 1)
                sp.wait_ge(token_rows_copied[1], g + 1)
                sp.wait_ge(logits_ready, g + 1)
                rows = tok_dram[bass.ds(g * GB, GB)].rearrange("b t f -> t b f")
                sp.dma_start(rows[0:128], tm0[:, :, :]).then_inc(tokens_saved, 16)
                sp.dma_start(rows[128:S], tm1[0:T2, :, :]).then_inc(tokens_saved, 16)

            def logits_of(p):
                both_halves(sp, p, 0, W, logits_loaded, lambda parts, batches, lo, hi: (
                    ROUTING[p][4][parts].rearrange("p (t e) -> p t e", e=E), tok_dram[batches, lo:hi, 128:144]))

            def load_sub(t, h):
                wait(sp, rows_scattered[h], 16 * 2 * sub_total(t, h))
                lo, hi = sub(t, h)
                both_halves(sp, 0, lo, hi, rows_loaded[h], lambda parts, batches, a_, b_: (
                    xn_turn[parts, SUBS[h]:SUBS[h] + hi - lo, :], tok_dram[batches, a_:b_, 0:D_]))

            def load_experts():
                for k, w in enumerate(raw1):
                    for h in range(2):
                        sp.dma_start(w[64 * h:64 * h + 64].rearrange("p (e f) -> p e f", e=E // 2),
                                     a["ffn_w1"][:, E // 2 * k:E // 2 * (k + 1)]).then_inc(expert_weights_loaded, 16)
                sp.dma_start(raw2.rearrange("p (e f) -> p e f", e=E), a["ffn_w2"]).then_inc(expert_weights_loaded, 16)
                for r in range(2):
                    sp.dma_start(rawb[r:r + 1, :], a["ffn_b2"]).then_inc(expert_weights_loaded, 16)
                sp.dma_start(fb1[:, :], a["ffn_b1"]).then_inc(expert_weights_loaded, 16)
                sp.dma_start(row_sel[:, :], a["row_sel"]).then_inc(expert_weights_loaded, 16)
                for k, name in enumerate(("ffn_gamma", "ffn_beta")):
                    sp.dma_start(ff_gb[:, k, :], a[name].rearrange("(o n) -> o n", o=1).to_broadcast([128, D_])).then_inc(expert_weights_loaded, 16)

            def turn(t):
                if isinstance(t, int) and t == TURNS - 1:
                    sp.wait_ge(norm_ready[3], NG)
                    load_experts()
                if isinstance(t, int) and t > ROUTE:
                    load_sub(t, 1)
                if on(t + 1):
                    load_x(t + 1)
                if on(t - 1):
                    text(t - 1)
                if on(t - 3):
                    save(t - 3)
                if isinstance(t, int) and t == ROUTE:
                    sp.wait_ge(tokens_saved, 32 * (NG // 2))
                    sp.wait_ge(exponent_steps_made, 2 * (t - 1))
                    sp.wait_ge(turned_values_copied, t - 1)
                    logits_of(0)
                if isinstance(t, int) and ROUTE <= t < TURNS - 1:
                    load_sub(t + 1, 0)

            turns(sp, None, 0, turn)
            sp.wait_ge(tokens_saved, 32 * NG)
            logits_of(1)
            for h in range(2):
                sp.wait_ge(rows_scattered[h], 16 * 2 * sub_total(TURNS, h))
            for k in range(PIECES):
                lo, hi = piece(k)
                both_halves(sp, 1, lo, hi, rows_loaded[k], lambda parts, batches, a_, b_: (xn_part[parts, lo:hi, :], tok_dram[batches, a_:b_, 0:D_]))
            def rows_of(dram, q, p):
                p = q // QP if isinstance(q, int) else p
                return dram[p][bass.ds((q - QP * p) * QR if isinstance(q, int) else q * QR + (-QP * p * QR), QR)].rearrange("(n p) f -> p n f", p=128)

            def load_tiles(q, p, h):
                wait(sp, quad_rows_turned, q + (1 - RING))
                sp.dma_start(x_tiles[h], rows_of(xs_dram, q, p)).then_inc(quad_rows_loaded[h], 16)

            def step(m, h, p):
                ahead, stored = behind(m, h, -RING), behind(m, h, 3)
                if stored:
                    q, _, ring, _ = stored
                    sp.wait_ge(expert_result_copied, q + 1)
                    sp.dma_start(rows_of(es_dram, q, p), o_tiles[ring]).then_inc(expert_result_stored[ring], 16)
                if ahead:
                    q, _, ring, _ = ahead
                    load_tiles(q, p, ring)

            sp.wait_ge(expert_weights_made, 5)
            for h in range(RING):
                load_tiles(h, 0, h)
            slots(sp, lambda m, h: step(m, h, 0), last=QP // RING - 1, end=QP - RING)
            for k in range(PIECES):
                sp.wait_ge(rows_scattered[k], 16 * 2 * (sub_total(TURNS, k) + piece(k)[1] - piece(k)[0]))
            slots(sp, lambda m, h: step(m, h, 1), prologue=QP // RING - 1, first=QP // RING + 1)

            def load_stream(i):
                p, lo, hi = CHUNKS[i]
                wait(sp, chunk_done, i - 1)
                both_halves(sp, p, lo, hi, stream_loaded[i % 2], lambda parts, batches, a_, b_: (
                    stream[i % 2][parts, 0:hi - lo], tok_dram[batches, a_:b_, 0:2 * D_].rearrange("b t (k f) -> b t k f", k=2)))

            for i in range(2):
                load_stream(i)
            for i, (p, lo, hi) in enumerate(CHUNKS):
                sp.wait_ge(chunk_done, i + 1)
                for h in range(2):
                    skip = int(h and not lo)
                    sp.dma_start(out[64 * p:64 * p + 64, STARTS[h] + lo + skip:STARTS[h] + hi, :],
                                 y_[i % 2][64 * h:64 * h + 64, skip:hi - lo]).then_inc(chunk_stored[i % 2], 16)
                if i + 2 < len(CHUNKS):
                    load_stream(i + 2)
            for h in range(2):
                sp.wait_ge(chunk_stored[h], 32 * NC)

        @block.vector
        def _(dve):
            c = Chain(dve, dve_step_done)
            dve.memset(one[:, :], 1.0)
            dve.memset(eps8[:, :], 1e-8)
            dve.memset(m_ext[:, :, 0:1], 0.0)
            dve.memset(u1[:, :, 0:64], 0.0)
            dve.memset(not_start[:, :], 1.0)
            c.link(dve.memset(eps[:, :], EPS))
            starts = not_start[:, :].rearrange("p (g s) -> p g s", g=GP)
            for lo, _ in BLOCKS:
                dve.memset(starts[:, :, lo:lo + 1], 0.0)
            dve.wait_ge(constants_loaded, 16 * 9)
            for k in range(1, 4):
                for n, dst in ((0, gam[k]), (1, bet[k])):
                    raw = gb_raw[:, 2 * (k >= 2) + n, 0:64 * COLS[k]]
                    raw = raw.rearrange("p (j w) -> p w j", w=COLS[k]) if k < 3 else columns(raw, k)
                    last = dve.tensor_scalar(columns(dst[:, :], k), raw, XS, None, ALU.mult)
            c.link(last)
            for k in (1, 2, 3, 4):
                dve.wait_ge(weights_loaded, 16 * 4)
                dve.wait_ge(conv_weights_hi_made, k)
                dve.scalar_tensor_tensor(w_lo[k][:, :], w_raw[k], WS, w_hi[k][:, :], ALU.mult, ALU.subtract).then_inc(conv_weights_lo_made, 1)
            dve.wait_ge(patterns_made, 10)
            dve.tensor_tensor(centre[:, :], ident32[:, :], average[:, :], ALU.subtract)
            dve.wait_ge(attn_columns_loaded, 16 * 3)
            dve.tensor_scalar(bias_k[:, :], acol[:, 1:2], 0.125, None, ALU.mult)
            c.link(dve.tensor_tensor(bias_i[:, :], acol[:, 3:4], acol[:, 6:7], ALU.add))
            dve.tensor_scalar(bias_i[:, :], bias_i[:, :], 0.2, None, ALU.mult)
            dve.tensor_scalar(bias_o[:, :], acol[:, 5:6], -1.0, None, ALU.mult).then_inc(attn_constants_made, 1)

            def norm(k, i, in_sem, in_count, full_free, full_count, meanwhile=None):
                dve.wait_ge(in_sem, in_count)
                for b in range(GB):
                    last = dve.bn_stats(stats[k][:, b, :], source(k, b))
                c.link(last)
                even, odd = stats[k][:, :, 0:3], stats[k][:, :, 3:6]
                dve.tensor_tensor(spread[:, :], even[:, :, 2], odd[:, :, 2], ALU.add)
                dve.tensor_scalar(half_mean[:, :], even[:, :, 1], 0.5, None, ALU.mult)
                c.link(dve.tensor_tensor(gap[:, :], even[:, :, 1], odd[:, :, 1], ALU.subtract))
                dve.scalar_tensor_tensor(mean[k][:, :], odd[:, :, 1], 0.5, half_mean[:, :], ALU.mult, ALU.add)
                c.link(dve.tensor_tensor(gap2[:, :], gap[:, :], gap[:, :], ALU.mult))
                dve.scalar_tensor_tensor(var4[k][:, :], spread[:, :], 4.0 / (64 * COLS[k]), gap2[:, :],
                                         ALU.mult, ALU.add).then_inc(variance_ready[k], 1)
                dve.wait_ge(variance_ready[k], i + 1)
                for b in range(GB):
                    last = dve.scalar_tensor_tensor(columns(centred[:, b, 0:64 * COLS[k]], k), source(k, b), mean[k][:, b:b + 1],
                                                    columns(gam[k][:, :], k), ALU.subtract, ALU.mult)
                c.link(last)
                if meanwhile:
                    meanwhile()
                dve.wait_ge(inv_dev_ready[k], i + 1)
                wait(dve, full_free, full_count)
                for b in range(GB):
                    last = dve.scalar_tensor_tensor(full_of(k)[:, :, b, :], columns(centred[:, b, 0:64 * COLS[k]], k),
                                                    rstd[k][:, b:b + 1], columns(bet[k][:, :], k), ALU.mult, ALU.add)
                last.then_inc(norm_ready[k], 1)

            def route(p):
                top, other, which, row, logit, chosen0, chosen1, work = ROUTING[p]
                top, chosen = (top, other), [x.rearrange("p (t e) -> p t e", e=E) for x in (chosen0, chosen1)]
                logit, rank = (logit.rearrange(how, e=E) for how in ("p (t e) -> p t e", "p (e t) -> p e t"))
                work_te, work_et = (work.rearrange(how, e=E) for how in ("p (t e) -> p t e", "p (e t) -> p e t"))
                numbers = e_minus[:, :].unsqueeze(1).to_broadcast([128, W, E])
                dve.wait_ge(logits_loaded, 32 * (p + 1))
                for k in range(2):
                    c.link(dve.tensor_reduce(top[k], logit, AX.X, ALU.max))
                    c.link(dve.tensor_tensor(work_te, logit, top[k].unsqueeze(2).to_broadcast([128, W, E]), ALU.is_equal))
                    c.link(dve.tensor_tensor(work_te, work_te, numbers, ALU.mult))
                    c.link(dve.tensor_reduce(which, work_te, AX.X, ALU.min))
                    c.link(dve.tensor_tensor(chosen[k], numbers, which.unsqueeze(2).to_broadcast([128, W, E]), ALU.is_equal))
                    if k == 0:
                        c.link(dve.scalar_tensor_tensor(logit, chosen[0], -1e30, logit, ALU.mult, ALU.add))
                dve.tensor_tensor(gate[p][1], top[1], top[0], ALU.subtract).then_inc(gate_difference_made, 1)
                c.link(dve.tensor_tensor(work_et, chosen[0].rearrange("p t e -> p e t"), chosen[1].rearrange("p t e -> p e t"), ALU.add))
                for e in range(E):
                    last = dve.tensor_tensor_scan(rank[:, e, :], all_ones[:, 0:W], work_et[:, e, :], 0.0, ALU.mult, ALU.add)
                c.link(last)
                dve.tensor_copy(counts[:, :], rank[:, :, W - 1]).then_inc(counts_made, 1)
                dve.wait_ge(offsets_made, p + 1)
                dve.tensor_copy(off[:, :], double[0][:, 0, 0:E])
                dve.tensor_scalar(quads_i[:, :], double[0][:, 0, E:2 * E], QR - 1.0, None, ALU.add).then_inc(offsets_read, 1)
                dve.wait_ge(offsets_read, p + 1)
                c.link(dve.tensor_scalar(quads_i[:, :], quads_i[:, :], QR.bit_length() - 1, None, ALU.logical_shift_right))
                c.link(dve.tensor_copy(quads_e[:, :], quads_i[:, :]))
                c.link(dve.tensor_tensor_scan(ends[p][:, :], all_ones[:, 0:E], quads_e[:, :], 0.0, ALU.mult, ALU.add))
                c.link(dve.tensor_tensor(quads_e[:, :], ends[p][:, :], quads_e[:, :], ALU.subtract))
                c.link(dve.scalar_tensor_tensor(off[:, :], quads_e[:, :], float(QR), off[:, :], ALU.mult, ALU.add))
                c.link(dve.tensor_scalar(off[:, :], off[:, :], -1.0, None, ALU.add))
                c.link(dve.tensor_tensor(rank, rank, off[:, :].unsqueeze(2).to_broadcast([128, E, W]), ALU.add))
                for k in range(2):
                    c.link(dve.tensor_tensor(work_te, chosen[k], rank.rearrange("p e t -> p t e"), ALU.mult))
                    c.link(dve.tensor_reduce(row, work_te, AX.X, ALU.add))
                    dve.tensor_copy(slot[p][k], row).then_inc(slots_made, 1)

            def norm0(i, meanwhile=None):
                norm(0, i, x_loaded, i * 16 + 16, norm_lo_ready[2], i - 1, meanwhile)

            def norm1(i):
                norm(1, i, relu_done[1], i * 3 + 3, norm_lo_ready[3], i - 1)

            def norm3(i, norm1_done):
                norm(3, i, relu_done[3], i * 2 + 2, norm_lo_ready[1], norm1_done)

            def norm2(i, norm0_done):
                norm(2, i, relu_done[2], i * 2 + 2, norm_lo_ready[0], norm0_done)

            def bank2(name):
                return TILE[name][:, :, 0:HALF]

            def normed(g):
                dve.wait_ge(inv_dev1_ready, g + 1)
                dve.tensor_tensor(A["xn"], A["xn"], A["rs"], ALU.mult).then_inc(xn_ready, 1)

            def keep(g):
                dve.wait_ge(tokens_ready, g * 2 + 2)
                dve.wait_ge(text_loaded, g * 16 + 16)
                wait(dve, new_stream_ready, g)
                dve.tensor_copy(A["resid"], A["tokens"]).then_inc(residual_kept, 1)

            def gates(g):
                dve.wait_ge(filled["f"], g + 1)
                dve.tensor_scalar(halves2("t_f"), bank2("f"), acol[:, 4:5], 0.0, ALU.add, ALU.max).then_inc(forget_positive_part_made, 1)
                dve.wait_ge(forget_positive_part_made, g + 1)
                dve.wait_ge(forget_log_made, g + 1)
                dve.scalar_tensor_tensor(A["lf"], A["t_f"], -1.0, A["lf"], ALU.mult, ALU.subtract).then_inc(log_forget_ready, 1)
                dve.wait_ge(input_exp_made, g + 1)
                dve.tensor_scalar(A["li"], A["li"], -20.0, 10.0, ALU.mult, ALU.add).then_inc(log_input_ready, 1)

            def scans(g):
                dve.wait_ge(log_forget_ready, g + 1)
                dve.wait_ge(log_input_ready, g + 1)
                for p in range(GP):
                    last = dve.tensor_tensor_scan(m_ext[:, p, 1:S + 1], A["lf"][:, p, :], A["li"][:, p, :], 0.0, ALU.add, ALU.max)
                last.then_inc(running_max_ready, 1)
                c.link(dve.tensor_tensor_scan(flat("cum"), not_start[:, :], flat("lf"), 0.0, ALU.mult, ALU.add))
                dve.wait_ge(running_max_ready, g + 1)
                mids = [(lo + hi) // 2 for lo, hi in BLOCKS]
                for n in range(3):
                    last = dve.tensor_copy(mid[:, :, n:n + 1], A["cum"][:, :, mids[n]:mids[n] + 1])
                c.link(last)
                for n, (lo, hi) in enumerate(BLOCKS):
                    last = dve.tensor_tensor(A["cum"][:, :, lo:hi], A["cum"][:, :, lo:hi],
                                             mid[:, :, n:n + 1].to_broadcast([128, GP, hi - lo]), ALU.subtract)
                c.link(last)
                dve.tensor_tensor(A["wv"], A["li"], A["cum"], ALU.subtract).then_inc(weight_arg_made, 1)
                for n in range(2):
                    end = BLOCKS[n][1] - 1
                    last = dve.tensor_tensor(decay_arg[:, :, n:n + 1], A["cum"][:, :, end:end + 1], mid[:, :, n + 1:n + 2], ALU.add)
                last.then_inc(block_decay_arg_made, 1)
                c.link(dve.tensor_tensor(A["t_f"], A["lf"], m_ext[:, :, 0:S], ALU.add))
                dve.tensor_tensor(A["t_f"], A["t_f"], m_ext[:, :, 1:S + 1], ALU.subtract).then_inc(forget_arg_made, 1)
                dve.tensor_tensor(A["t_i"], A["li"], m_ext[:, :, 1:S + 1], ALU.subtract).then_inc(input_arg_made, 1)
                wait(dve, factor_ready, g)
                dve.tensor_tensor(A["gexp"], A["cum"], m_ext[:, :, 1:S + 1], ALU.subtract).then_inc(exponent_steps_made, 1)

            def weigh(g):
                dve.wait_ge(weight_ready, g + 1)
                dve.wait_ge(values_ready, g + 1)
                dve.tensor_tensor(A["wv"], A["wv"], A["vT"], ALU.mult).then_inc(weighted_values_ready, 1)
                dve.wait_ge(block_decay_ready, g + 1)
                c.link(dve.tensor_tensor(decay[:, :, 2:3], decay[:, :, 0:1], decay[:, :, 1:2], ALU.mult))

            def normalizer(g):
                dve.wait_ge(forget_scale_ready, g + 1)
                dve.wait_ge(input_scale_ready, g + 1)
                dve.wait_ge(keys_ready, g + 1)
                dve.memset(A["t_f"][:, :, 0:1], 0.0)
                c.link(dve.tensor_tensor(A["t_i"], A["t_i"], A["kT"], ALU.mult))
                wait(dve, filled["den"], g)
                c.link(dve.tensor_tensor_scan(flat("nq"), flat("t_f"), flat("t_i"), 0.0, ALU.mult, ALU.add))
                dve.wait_ge(queries_ready, g + 1)
                dve.tensor_tensor(A["nq"], A["nq"], A["qT"], ALU.mult).then_inc(n_times_q_ready, 1)

            def mask(g, n):
                dve.wait_ge(filled["sc"], g * 4 + (n + 1))
                if n == 0:
                    wait(dve, filled["hacc"], g * 2)
                tile = TILE[f"sc{n}"]
                dve.tensor_tensor(st[:, 2 * n:2 * n + 2, 0:S], tile[:, :, 0:S],
                                  causal[:, 0:S].unsqueeze(1).to_broadcast([128, 2, S]), ALU.mult)
                dve.tensor_tensor(st[0:T2, 2 * n:2 * n + 2, S:], tile[0:T2, :, S:S + T2],
                                  causal[0:T2, S:].unsqueeze(1).to_broadcast([T2, 2, T2]), ALU.mult).then_inc(masked_scores_ready, 1)

            def denominator(g):
                dve.wait_ge(denominator_copied, g + 1)
                dve.tensor_scalar(A["den"], A["den"], 1e-6, None, ALU.max).then_inc(denominator_bounded, 1)

            def exponent(g):
                dve.wait_ge(exponent_steps_made, g * 2 + 1)
                dve.wait_ge(output_gate_ready, g + 1)
                c.link(dve.tensor_tensor(A["gexp"], A["gexp"], A["o_log"], ALU.subtract))
                dve.wait_ge(log_denominator_ready, g + 1)
                dve.tensor_tensor(A["gexp"], A["gexp"], A["den"], ALU.subtract).then_inc(exponent_steps_made, 1)

            def combine(g, n):
                dve.wait_ge(filled["hacc"], g * 2 + (n + 1))
                tile, pairs = TILE[f"hacc{n}"], slice(2 * n, 2 * n + 2)
                def dec(k, width):
                    return decay[:, pairs, k:k + 1].to_broadcast([128, 2, width])
                own0 = tile[:, 0, 0:2 * S].rearrange("p (g s) -> p g s", g=2)
                own12 = tile[:, 1, 0:436].rearrange("p (g s) -> p g s", g=2)
                dve.tensor_tensor(u1[:, pairs, 64:128], own0[:, :, 64:128], dec(0, 64), ALU.mult)
                dve.tensor_tensor(u1[:, pairs, 128:S], own12[:, :, 64:141], dec(1, T2), ALU.mult)
                c.link(dve.tensor_tensor(u2[:, pairs, :], own0[:, :, 128:S], dec(2, T2), ALU.mult))
                dve.tensor_tensor(u1[:, pairs, 64:128], own12[:, :, 0:64], u1[:, pairs, 64:128], ALU.add)
                c.link(dve.tensor_tensor(u1[:, pairs, 128:S], u1[:, pairs, 128:S], u2[:, pairs, :], ALU.add))
                c.link(dve.tensor_tensor(u1[:, pairs, 128:S], own12[:, :, 141:218], u1[:, pairs, 128:S], ALU.add))
                if n == 0:
                    dve.wait_ge(factor_ready, g + 1)
                dve.tensor_tensor(A["h"][:, pairs, 0:64], own0[:, :, 0:64], A["gexp"][:, pairs, 0:64], ALU.mult)
                dve.tensor_tensor(A["h"][:, pairs, 64:S], u1[:, pairs, 64:S], A["gexp"][:, pairs, 64:S], ALU.mult).then_inc(attention_out_ready, 1)

            def residual(g):
                dve.wait_ge(inv_rms_ready, g + 1)
                c.link(dve.tensor_tensor(A["h"], A["h"], A["rs_b"], ALU.mult))
                dve.wait_ge(residual_kept, g + 1)
                wait(dve, filled["tm"], g * 2)
                dve.scalar_tensor_tensor(A["h2"], A["h"], acol[:, 7:8], A["resid"], ALU.mult, ALU.add).then_inc(new_stream_ready, 1)

            def normed2(g):
                dve.wait_ge(inv_dev3_ready, g + 1)
                dve.tensor_tensor(A["xn2"], A["xn2"], A["rs_b"], ALU.mult).then_inc(xn2_ready, 1)

            def logits(g):
                dve.wait_ge(filled["lg"], g + 1)
                wait(dve, tokens_saved, g * 32)
                tile = TILE["lg"][:, 0, 0:256].rearrange("p (s b e) -> p s b e", s=2, b=GB)
                for s_, (dst, rows) in enumerate(((tm0, 128), (tm1, T2))):
                    last = dve.tensor_tensor(dst[0:rows, :, 128:144], tile[0:rows, s_],
                                             gate_bias[0:rows, :].unsqueeze(1).to_broadcast([rows, GB, 16]), ALU.add)
                last.then_inc(logits_ready, 1)

            norm0(0)

            def turn(t):
                if on(t - 1):
                    norm2(t - 1, t + 1 if on(t) else NG)
                if on(t - 3):
                    for n in range(2):
                        combine(t - 3, n)
                    residual(t - 3)
                if on(t - 2):
                    keep(t - 2)
                    normed(t - 2)
                if on(t):
                    norm1(t)
                if on(t - 3):
                    normed2(t - 3)
                if on(t - 2):
                    gates(t - 2)
                    scans(t - 2)
                if on(t + 1):
                    norm0(t + 1, (lambda: logits(t - 3)) if on(t - 3) else None)
                elif on(t - 3):
                    logits(t - 3)
                if on(t - 2):
                    for n in range(3):
                        mask(t - 2, n)
                    normalizer(t - 2)
                    mask(t - 2, 3)
                    weigh(t - 2)
                if on(t - 1):
                    norm3(t - 1, t + 1 if on(t) else NG)
                if on(t - 2):
                    denominator(t - 2)
                    exponent(t - 2)
                if isinstance(t, int) and t == ROUTE:
                    route(0)

            turns(dve, c, DVE_LINKS, turn)

            dve.wait_ge(expert_weights_loaded, 16 * 11)
            dve.wait_ge(expert_weights_hi_made, 4)
            for k, w in enumerate(raw1):
                half = slice(E * F // 2 * k, E * F // 2 * (k + 1))
                dve.scalar_tensor_tensor(fw1_lo[:, half], w, FW_SCALE, fw1_hi[:, half], ALU.mult, ALU.subtract).then_inc(expert_weights_made, 1)
            dve.scalar_tensor_tensor(fw2_lo, raw2, FW_SCALE, fw2_hi, ALU.mult, ALU.subtract).then_inc(expert_weights_made, 1)
            c.link(dve.scalar_tensor_tensor(rawb[0:2, :], rawb[0:2, :], FW_SCALE, fb2[0:2, :], ALU.mult, ALU.subtract))
            c.link(dve.tensor_scalar(rawb[0:2, :], rawb[0:2, :], row_sel[:, 1:2], None, ALU.mult))
            dve.scalar_tensor_tensor(fb2[0:2, :], fb2[0:2, :], row_sel[:, 0:1], rawb[0:2, :], ALU.mult, ALU.add).then_inc(expert_weights_made, 1)
            dve.memset(ones_h[:, :], H_SCALE)
            dve.tensor_scalar(fb1s[:, :], fb1[:, :], H_SCALE, None, ALU.mult).then_inc(expert_weights_made, 1)

            route(1)
            dve.wait_ge(quad_numbers_made, 1)
            for p in range(2):
                if p:
                    dve.wait_ge(quad_experts_made, p)
                c.link(dve.memset(quad_exp, 0.0))
                for e in range(E):
                    c.link(dve.scalar_tensor_tensor(quad_exp, quad_no, ends[p][:, e:e + 1], quad_exp, ALU.is_ge, ALU.add))
                dve.tensor_scalar(quad_i[:, QP * p:QP * (p + 1)], quad_exp, float(E - 1), None, ALU.min).then_inc(quad_experts_made, 1)
            for p in range(2):
                dve.wait_ge(gate_exp_made, p + 1)
                c.link(dve.tensor_scalar(gate[p][0], gate[p][1], 1.0, None, ALU.add))
                c.link(dve.reciprocal(gate[p][0], gate[p][0]))
                c.link(dve.tensor_tensor(gate[p][1], gate[p][1], gate[p][0], ALU.mult))
            def step(m, h):
                hidden, turned, result = behind(m, h, 2), behind(m, h, 0), behind(m, h, 3)
                if hidden:
                    q, _, _, two = hidden
                    dve.wait_ge(hidden_ready, q + 1)
                    wait(dve, expert_product_done, q + (-1))
                    dve.tensor_copy(hid_hi[two], hid[two]).then_inc(hidden_hi_made, 1)
                    dve.wait_ge(hidden_hi_made, q + 1)
                    dve.tensor_tensor(hid_lo[two], hid[two], hid_hi[two], ALU.subtract).then_inc(hidden_lo_made, 1)
                if turned:
                    q, _, _, two = turned
                    dve.wait_ge(quad_hi_made, q + 1)
                    dve.scalar_tensor_tensor(xT[two][64:128, :], double[0][0:64, two, :], XS, xT[two][0:64, :], ALU.mult, ALU.subtract).then_inc(quad_lo_made, 1)
                if result:
                    q, turn, ring, two = result
                    dve.wait_ge(expert_product_done, q + 1)
                    wait(dve, expert_result_stored[ring], turn * 16)
                    dve.tensor_scalar(o_tiles[ring], double[2][:, two, 0:256].rearrange("p (n f) -> p n f", f=D_),
                                      1.0 / (H_SCALE * FW_SCALE), None, ALU.mult).then_inc(expert_result_copied, 1)

            slots(dve, step)

            for i, (p, lo, hi) in enumerate(CHUNKS):
                n, g, y, strm = hi - lo, got[:, lo:hi], y_[i % 2][:, 0:hi - lo], stream[i % 2][:, 0:hi - lo]

                def over(v):
                    return v.unsqueeze(2).to_broadcast([128, n, D_])

                dve.wait_ge(chunk_gathered[i % NC], 16 * 2 * sum(CHUNKS[j][2] - CHUNKS[j][1] for j in range(i % NC, i + 1, NC)))
                for m in range(2):
                    last = dve.tensor_tensor(g[:, :, m, :], g[:, :, m, :], over(gate[p][m][:, lo:hi]), ALU.mult)
                c.link(last)
                wait(dve, chunk_stored[i % 2], i // 2 * 32)
                c.link(dve.tensor_tensor(y, g[:, :, 0, :], g[:, :, 1, :], ALU.add))
                dve.wait_ge(stream_loaded[i % 2], 32 * (i // 2 + 1))
                c.link(dve.tensor_tensor(y, y, strm[:, :, 0, :], ALU.add))
                c.link(dve.tensor_reduce(y_mean[:, 0:n], y, AX.X, ALU.add))
                c.link(dve.tensor_scalar(y_mean[:, 0:n], y_mean[:, 0:n], 1.0 / D_, None, ALU.mult))
                c.link(dve.tensor_tensor(y, y, over(y_mean[:, 0:n]), ALU.subtract))
                c.link(dve.tensor_tensor(g[:, :, 0, :], y, y, ALU.mult))
                dve.tensor_reduce(y_var[:, 0:n], g[:, :, 0, :], AX.X, ALU.add).then_inc(out_variance_ready, 1)
                dve.wait_ge(out_inv_dev_ready, i + 1)
                c.link(dve.tensor_tensor(y, y, over(y_rstd[:, 0:n]), ALU.mult))
                c.link(dve.tensor_tensor(y, y, ff_gb[:, 0, :].unsqueeze(1).to_broadcast([128, n, D_]), ALU.mult))
                c.link(dve.tensor_tensor(y, y, ff_gb[:, 1, :].unsqueeze(1).to_broadcast([128, n, D_]), ALU.add))
                dve.tensor_tensor(y, y, strm[:, :, 1, :], ALU.add).then_inc(chunk_done, 1)

        @block.scalar
        def _(act):
            c = Chain(act, act_step_done)
            act.preload_act_table_set("natural_log_exp_and_others")
            act.wait_ge(weights_loaded, 16 * 4)
            for k in (1, 2, 3, 4):
                act.activation(w_hi[k][:, :], w_raw[k], ACT.Copy, scale=WS).then_inc(conv_weights_hi_made, 1)
            act.wait_ge(constants_loaded, 16 * 9)

            def root(k, i):
                act.wait_ge(variance_ready[k], i + 1)
                c.link(act.activation(lnv[k][:, :], var4[k][:, :], ACT.Ln, bias=eps[:, 0:1], scale=0.25))
                act.activation(rstd[k][:, :], lnv[k][:, :], ACT.Exp, scale=-0.5).then_inc(inv_dev_ready[k], 1)

            def high(k, i, free, count):
                act.wait_ge(norm_ready[k], i + 1)
                wait(act, free, count)
                for b in range(COLS[k]):
                    last = act.activation(halves(k, 0)[:, b], full_of(k)[:, b], ACT.Copy)
                last.then_inc(norm_hi_ready[k], 1)

            def relu(k, i, w):
                n = COLS[k]
                act.wait_ge(conv_done[k], i * n + (w + 1))
                if w == 0:
                    wait(act, norm_ready[k], i)
                dst = h_relu[k][:, w] if k < 3 else h_relu[3][:, :, w]
                src = TILE[f"c{k}{w}"][:, :].rearrange("p (b j) -> p b j", b=GB)
                bias = (0, 0, 1, 2 + w)[k]
                act.activation(dst, src, ACT.Relu, bias=cb[:, bias:bias + 1], scale=UNSCALE).then_inc(relu_done[k], 1)

            def turned(i):
                act.wait_ge(result_turned, i + 1)
                wait(act, token_product_done, i)
                act.activation(resT[:, :].rearrange("p h b t -> p h (b t)"), TILE["turned"][:, :, :].bitcast(F16), ACT.Copy).then_inc(turned_result_copied, 1)

            def tokens(i):
                act.wait_ge(token_product_done, i + 1)
                wait(act, residual_kept, i)
                for h in range(2):
                    q = slice(64 * h, 64 * h + 64)
                    act.activation(A["tokens"][q, :, 0:T], TILE["tok"][q, 0, :].rearrange("p (b t) -> p b t", b=GP),
                                   ACT.Identity, bias=cb[q, 4:5], scale=UNSCALE).then_inc(tokens_ready, 1)

            def bank2(name):
                return TILE[name][:, :, 0:HALF]

            def centred_square(g, name, dst, read, count, sq, sem_copied, sem_out):
                act.wait_ge(filled[name], g + 1)
                wait(act, read, count)
                act.activation(halves2(dst), bank2(name), ACT.Copy).then_inc(sem_copied, 1)
                act.wait_ge(sem_copied, g + 1)
                act.activation(A[sq], A[dst], ACT.Square).then_inc(sem_out, 1)

            def inverse_root(g, name, rs, sem_out, e):
                act.wait_ge(filled[name], g + 1)
                c.link(act.activation(halves2(rs), bank2(name), ACT.Ln, bias=e[:, 0:1]))
                act.activation(A[rs], A[rs], ACT.Exp, scale=-0.5).then_inc(sem_out, 1)

            def square_h(g):
                act.wait_ge(attention_out_ready, g * 2 + 2)
                wait(act, filled["var3"], g)
                act.activation(A["sq_b"], A["h"], ACT.Square).then_inc(out_squares_ready, 1)

            def forget(g):
                act.wait_ge(forget_positive_part_made, g + 1)
                wait(act, forget_arg_made, g)
                c.link(act.activation(halves2("lf"), bank2("f"), ACT.Abs, bias=acol[:, 4:5]))
                c.link(act.activation(A["lf"], A["lf"], ACT.Exp, scale=-1.0))
                act.activation(A["lf"], A["lf"], ACT.Ln, bias=one[:, 0:1]).then_inc(forget_log_made, 1)

            def inputs(g):
                act.wait_ge(filled["i"], g + 1)
                wait(act, input_arg_made, g)
                c.link(act.activation(halves2("li"), bank2("i"), ACT.Exp, bias=bias_i[:, 0:1], scale=0.2))
                c.link(act.activation(A["li"], A["li"], ACT.Ln, bias=one[:, 0:1]))
                act.activation(A["li"], A["li"], ACT.Exp, scale=-1.0).then_inc(input_exp_made, 1)

            def project(g, name, dst, bias, scale, sem_out, free, count):
                act.wait_ge(filled[name], g + 1)
                wait(act, free, count)
                act.activation(halves2(dst), bank2(name), ACT.Identity, bias=bias, scale=scale).then_inc(sem_out, 1)

            def output_gate(g):
                act.wait_ge(filled["o"], g + 1)
                wait(act, exponent_steps_made, g * 2)
                c.link(act.activation(halves2("o_log"), bank2("o"), ACT.Exp, bias=bias_o[:, 0:1], scale=-1.0))
                act.activation(A["o_log"], A["o_log"], ACT.Ln, bias=one[:, 0:1]).then_inc(output_gate_ready, 1)

            def exp_in_place(name, argument_made, count, exp_made):
                act.wait_ge(argument_made, count)
                act.activation(A[name], A[name], ACT.Exp).then_inc(exp_made, 1)

            def decays(g):
                act.wait_ge(block_decay_arg_made, g + 1)
                wait(act, attention_out_ready, g * 2)
                act.activation(decay[:, :, 0:2], decay_arg[:, :, :], ACT.Exp).then_inc(block_decay_ready, 1)

            def values(g):
                act.wait_ge(filled["vt"], g + 1)
                wait(act, filled["hacc"], g * 2)
                tile = TILE["vt"][:, :, :].rearrange("p c (g s) -> p c g s", g=2)
                act.activation(vt[:, :, 0:128].rearrange("p (c g) s -> p c g s", g=2), tile[:, :, :, 0:128], ACT.Copy)
                act.activation(vt[0:T2, :, 128:256].rearrange("p (c g) s -> p c g s", g=2), tile[0:T2, :, :, 128:256],
                               ACT.Copy).then_inc(turned_values_copied, 1)

            def abs_den(g):
                act.wait_ge(filled["den"], g + 1)
                wait(act, exponent_steps_made, g * 2)
                act.activation(halves2("den"), bank2("den"), ACT.Abs).then_inc(denominator_copied, 1)

            def log_den(g):
                act.wait_ge(denominator_bounded, g + 1)
                act.activation(A["den"], A["den"], ACT.Ln).then_inc(log_denominator_ready, 1)

            def turned_copy(g):
                wait(act, tokens_saved, g * 32)
                for n in range(2):
                    act.wait_ge(filled["tm"], g * 2 + (n + 1))
                    copy_turned(lambda o, i: act.activation(o, i, ACT.Copy), n).then_inc(token_rows_copied[n], 1)

            root(0, 0)
            high(0, 0, conv_done[1], 0)
            act.wait_ge(attn_constants_made, 1)

            def turn(t):
                if on(t - 1):
                    root(2, t - 1)
                if on(t):
                    relu(1, t, 0)
                if on(t - 2):
                    turned(t - 2)
                if on(t - 1):
                    high(2, t - 1, conv_done[3], (t - 1) * 2)
                if on(t - 2):
                    tokens(t - 2)
                if isinstance(t, int) and t == ROUTE + 1:
                    act.wait_ge(slots_made, 2)
                if on(t - 3):
                    square_h(t - 3)
                if on(t):
                    relu(1, t, 1)
                if on(t - 3):
                    inverse_root(t - 3, "ms", "rs_b", inv_rms_ready, eps8)
                if on(t - 2):
                    centred_square(t - 2, "cx1", "xn", filled["o"], t - 2, "sq", centred1_copied, squares1_ready)
                if on(t):
                    relu(1, t, 2)
                if on(t - 2):
                    inverse_root(t - 2, "var1", "rs", inv_dev1_ready, eps)
                if on(t - 3):
                    centred_square(t - 3, "cx3", "xn2", filled["lg"], t - 3, "sq_b", centred3_copied, squares3_ready)
                if on(t):
                    root(1, t)
                if on(t - 1):
                    relu(3, t - 1, 0)
                if on(t - 3):
                    inverse_root(t - 3, "var3", "rs_b", inv_dev3_ready, eps)
                if on(t):
                    high(1, t, conv_done[2], t * 2)
                if isinstance(t, int) and t == 2:
                    act.wait_ge(rows_zeroed, 16 * 2 * (QP * QR // ZERO_ROWS))
                if on(t - 2):
                    forget(t - 2)
                    inputs(t - 2)
                    project(t - 2, "k", "kT", bias_k[:, 0:1], 0.125, keys_ready, filled["sc"], (t - 2) * 4)
                if on(t - 1):
                    relu(3, t - 1, 1)
                if on(t - 2):
                    project(t - 2, "v", "vT", acol[:, 2:3], 1.0, values_ready, weighted_values_ready, t - 2)
                    project(t - 2, "q", "qT", acol[:, 0:1], 1.0, queries_ready, filled["sc"], (t - 2) * 4)
                    output_gate(t - 2)
                    exp_in_place("wv", weight_arg_made, t - 1, weight_ready)
                    decays(t - 2)
                    exp_in_place("t_f", forget_arg_made, t - 1, forget_scale_ready)
                    exp_in_place("t_i", input_arg_made, t - 1, input_scale_ready)
                if on(t + 1):
                    root(0, t + 1)
                if on(t):
                    relu(2, t, 0)
                if on(t - 3):
                    turned_copy(t - 3)
                if on(t + 1):
                    high(0, t + 1, conv_done[1], t * 3 + 3)
                if on(t - 1):
                    root(3, t - 1)
                if on(t):
                    relu(2, t, 1)
                if on(t - 1):
                    high(3, t - 1, result_turned, t - 1)
                if on(t - 2):
                    abs_den(t - 2)
                    values(t - 2)
                    log_den(t - 2)
                    exp_in_place("gexp", exponent_steps_made, (t - 2) * 2 + 2, factor_ready)

            turns(act, c, ACT_LINKS, turn)

            act.wait_ge(expert_weights_loaded, 16 * 11)
            for k, w in enumerate(raw1):
                half = slice(E * F // 2 * k, E * F // 2 * (k + 1))
                act.activation(fw1_hi[:, half], w, ACT.Copy, scale=FW_SCALE).then_inc(expert_weights_hi_made, 1)
            act.activation(fw2_hi, raw2, ACT.Copy, scale=FW_SCALE).then_inc(expert_weights_hi_made, 1)
            act.activation(fb2[0:2, :], rawb[0:2, :], ACT.Copy, scale=FW_SCALE).then_inc(expert_weights_hi_made, 1)
            for p in range(2):
                act.wait_ge(gate_difference_made, p + 1)
                act.activation(gate[p][1], gate[p][1], ACT.Exp).then_inc(gate_exp_made, 1)
            act.wait_ge(expert_weights_made, 5)
            act.wait_ge(quad_experts_made, 2)

            def step(m, h):
                turned, hidden = behind(m, h, 0), behind(m, h, 1)
                if hidden:
                    e = act.value_load(quad_i[0:1, bass.ds(hidden[0], 1)], min_val=0, max_val=E - 1)
                if turned:
                    q, _, _, two = turned
                    act.wait_ge(quad_rows_turned, q + 1)
                    wait(act, hidden_product_done, q + (-1))
                    act.activation(xT[two][0:64, :], double[0][0:64, two, :], ACT.Copy, scale=XS).then_inc(quad_hi_made, 1)
                if hidden:
                    q, _, _, two = hidden
                    act.wait_ge(hidden_product_done, q + 1)
                    wait(act, hidden_lo_made, q + (-1))
                    act.activation(hid[two], double[1][:, two, :], ACT.Relu, bias=fb1s[:, bass.ds(e, 1)],
                                   scale=H_SCALE / (XS * FW_SCALE)).then_inc(hidden_ready, 1)

            slots(act, step)
            for i, (p, lo, hi) in enumerate(CHUNKS):
                n = hi - lo
                act.wait_ge(out_variance_ready, i + 1)
                c.link(act.activation(y_rstd[:, 0:n], y_var[:, 0:n], ACT.Ln, bias=eps[:, 0:1], scale=1.0 / D_))
                act.activation(y_rstd[:, 0:n], y_rstd[:, 0:n], ACT.Exp, scale=-0.5).then_inc(out_inv_dev_ready, 1)

        @block.gpsimd
        def _(pool):
            for n in PROJ:
                pool.memset(w_proj[n][:, :], 0.0)
            pool.memset(zeros, 0.0)
            pool.memset(w_gate[:, :], 0.0).then_inc(attn_weights_zeroed, 1)
            pool.iota(e_minus[:, :], pattern=[[1, E]], base=-E, channel_multiplier=0, allow_small_or_imprecise_dtypes=True)
            pool.memset(before[:, :], 1.0)
            pool.memset(all_ones[:, :], 1.0)
            for k, t in enumerate((act1, act2, act3)):
                v = t[:, :, :, :, :].rearrange("p h w b j -> p (h w b) j")
                pool.memset(v[:, :, 0:2], 0.0)
                pool.memset(v[:, :, 2 + J:JP], 0.0)
            pool.memset(average[:, :], 0.0)
            pool.memset(total[:, :], 0.0)
            pool.memset(causal[:, :], 1.0)
            pool.memset(ident32[:, :], 0.0)
            pool.memset(ident[:, :], 0.0).then_inc(patterns_made, 1)
            pool.wait_ge(patterns_made, 1)
            for h in range(2):
                q = slice(64 * h, 64 * h + 64)
                pool.memset(average[q, q], 1.0 / 64).then_inc(patterns_made, 1)
                pool.wait_ge(patterns_made, 2 + 2 * h)
                pool.memset(total[q, q], 1.0).then_inc(patterns_made, 1)
                pool.wait_ge(patterns_made, 3 + 2 * h)
            for m in (ident, ident32):
                pool.affine_select(out=m[:, :], in_=m[:, :], compare_op=ALU.not_equal, fill=1.0, base=0,
                                   pattern=[[-1, 128]], channel_multiplier=1).then_inc(patterns_made, 1)
            for lo, n in ((0, S), (S, T2)):
                pool.affine_select(out=causal[:, lo:lo + n], in_=causal[:, lo:lo + n], compare_op=ALU.is_ge, fill=0.0, base=0,
                                   pattern=[[1, n]], channel_multiplier=-1).then_inc(patterns_made, 1)
            pool.affine_select(out=before[:, :], in_=before[:, :], compare_op=ALU.is_gt, fill=0.0, base=0,
                               pattern=[[1, 128]], channel_multiplier=-1).then_inc(patterns_made, 1)
            pool.wait_ge(patterns_made, 10)

            def low(k, i, free, count):
                pool.wait_ge(norm_hi_ready[k], i + 1)
                wait(pool, free, count)
                for w in range(COLS[k]):
                    last = pool.tensor_tensor(halves(k, 1)[:, w], full_of(k)[:, w], halves(k, 0)[:, w], ALU.subtract)
                last.then_inc(norm_lo_ready[k], 1)

            low(0, 0, conv_done[1], 0)

            def scatter_sub(t, h, quarter):
                if isinstance(t, int) and t > ROUTE:
                    pool.wait_ge(rows_loaded[h], 32 * (t - ROUTE))
                    lo, hi = sub(t, h)
                    mid_ = (lo + hi) // 2
                    for col in range(*((lo, mid_), (mid_, hi))[quarter]):
                        for m in range(2):
                            pool.indirect_dma_start(xs_dram[0], bass.IndirectOffsetOnAxis(ap=slot[0][m][:, col:col + 1], axis=0),
                                                    xn_turn[:, SUBS[h] + col - lo, :], None).then_inc(rows_scattered[h], 16)

            def turn(t):
                if isinstance(t, int) and t == ROUTE + 1:
                    pool.wait_ge(rows_zeroed, 16 * 2 * (QP * QR // ZERO_ROWS))
                if on(t - 1):
                    low(2, t - 1, conv_done[3], (t - 1) * 2)
                if isinstance(t, int) and t == ROUTE + 1:
                    pool.wait_ge(slots_made, 2)
                scatter_sub(t, 0, 0)
                if on(t):
                    low(1, t, conv_done[2], t * 2)
                scatter_sub(t, 0, 1)
                if on(t + 1):
                    low(0, t + 1, conv_done[1], t * 3 + 3)
                scatter_sub(t, 1, 0)
                if on(t - 1):
                    low(3, t - 1, result_turned, t - 1)
                scatter_sub(t, 1, 1)

            turns(pool, None, 0, turn)

            pool.wait_ge(expert_weights_made, 5)
            pool.iota(quad_no, pattern=[[1, QP]], base=0, channel_multiplier=0, allow_small_or_imprecise_dtypes=True).then_inc(quad_numbers_made, 1)
            pool.wait_ge(slots_made, 4)
            for k in range(PIECES):
                pool.wait_ge(rows_loaded[k], 32 * (TURNS - ROUTE))
                for t in range(*piece(k)):
                    for m in range(2):
                        pool.indirect_dma_start(xs_dram[1], bass.IndirectOffsetOnAxis(ap=slot[1][m][:, t:t + 1], axis=0),
                                                xn_part[:, t, :], None).then_inc(rows_scattered[k], 16)
            for k in range(PIECES):
                pool.wait_ge(rows_scattered[k], 16 * 2 * (sub_total(TURNS, k) + piece(k)[1] - piece(k)[0]))
            for i, (p, lo, hi) in enumerate(CHUNKS):
                if i % NC == 0:
                    for h in range(RING):
                        pool.wait_ge(expert_result_stored[h], 16 * QP // RING * (p + 1))
                if p:
                    pool.wait_ge(out_variance_ready, i - NC + 1)
                for t in range(lo, hi):
                    for m in range(2):
                        pool.indirect_dma_start(got[:, t, m, :], None, es_dram[p],
                                                bass.IndirectOffsetOnAxis(ap=slot[p][m][:, t:t + 1], axis=0)).then_inc(chunk_gathered[i % NC], 16)

        @block.tensor
        def _(pe):
            def conv(k, i, w):
                wide = 2 * T if k == 3 else T
                src = (act1, act2, act3)[k - 1]
                if k == 1:
                    taps = [(kh, w_in - w + 1, w_in) for w_in in range(3) if 0 <= w_in - w + 1 < 3 for kh in range(5)]
                elif k == 2:
                    taps = [(kh, kw, w + kw) for kw in range(2) for kh in range(5)]
                else:
                    taps = [(kh, kw, kw) for kw in range(2) for kh in range(5)]
                kws = 3 if k == 1 else 2
                pe.wait_ge(norm_lo_ready[k - 1], i + 1)
                dst = take(pe, f"c{k}{w}", i)[:, :].rearrange("p (b j) -> p b j", b=GB)
                n, last_n = 0, 3 * len(taps) - 1
                for kh, kw, w_in in taps:
                    o = (kh * kws + kw) * wide + (w * T if k == 3 else 0)
                    for wt, half in ((w_hi, 0), (w_hi, 1), (w_lo, 0)):
                        mm = pe.matmul(dst, wt[k][:, o:o + T], src[:, half, w_in, :, kh:kh + J], start=(n == 0), stop=(n == last_n))
                        n += 1
                mm.then_inc(conv_done[k], 1)

            def turn_result(i):
                pe.wait_ge(norm_lo_ready[3], i + 1)
                tile = take(pe, "turned", i)
                for h in range(2):
                    for b in range(GB):
                        mm = pe.transpose(tile[:, h, :].bitcast(F16)[:, 128 * b:128 * b + 128], res[:, h, b, :], ident[:, :])
                mm.then_inc(result_turned, 1)

            def tokens(i):
                pe.wait_ge(turned_result_copied, i + 1)
                tile = take(pe, "tok", i)
                for q in range(2):
                    for n, (wt, half) in enumerate(((w_hi, 0), (w_hi, 1), (w_lo, 0))):
                        mm = pe.matmul(tile[64 * q:64 * q + 64, 0, :].rearrange("p (b t) -> p b t", b=4), wt[4][:, :],
                                       resT[:, half].rearrange("p (b q) t -> p q b t", q=2)[:, q], start=(n == 0), stop=(n == 2))
                mm.then_inc(token_product_done, 1)

            def product(g, name, weights, src):
                tile = take(pe, name, g)
                for n in range(2):
                    mm = pe.matmul(tile[:, n, 0:HALF], weights[:, :], halves2(src)[:, n], start=True, stop=True)
                mm.then_inc(filled[name], 1)

            def scores(g, n):
                if n == 0:
                    pe.wait_ge(keys_ready, g + 1)
                    pe.wait_ge(queries_ready, g + 1)
                tile = take(pe, f"sc{n}", g)
                for h in range(2):
                    q = slice(64 * h, 64 * h + 64)
                    k_, q_ = A["kT"][q, n, :], A["qT"][q, n, :]
                    pe.matmul(tile[:, h, 0:S], k_[:, 0:128], q_, start=True, stop=True)
                    mm = pe.matmul(tile[0:T2, h, S:S + T2], k_[:, 128:S], q_[:, 128:S], start=True, stop=True)
                mm.then_inc(filled["sc"], 1)

            def turn_values(g):
                pe.wait_ge(weighted_values_ready, g + 1)
                tile = take(pe, "vt", g)
                for p in range(GP):
                    o = 256 * (p % 2)
                    pe.transpose(tile[:, p // 2, o:o + 128], A["wv"][:, p, 0:128], ident32[:, :])
                    mm = pe.transpose(tile[0:T2, p // 2, o + 128:o + 256], A["wv"][:, p, 128:S], ident32[:, :])
                mm.then_inc(filled["vt"], 1)

            def sums(g, n):
                pe.wait_ge(turned_values_copied, g + 1)
                pe.wait_ge(masked_scores_ready, g * 4 + 4)
                tile = take(pe, f"hacc{n}", g)
                for c_ in range(2):
                    p = 2 * n + c_
                    for h in range(2):
                        o = slice(64 * h, 64 * h + 64)
                        b = 2 * p + h
                        v0, v1, v2 = (vt[r, p, 128 * s_ + 64 * h:128 * s_ + 64 * h + 64]
                                      for r, s_ in ((slice(0, 64), 0), (slice(64, 128), 0), (slice(0, T2), 1)))
                        at = 218 * c_
                        pe.matmul(tile[o, 1, at + 141:at + 218], v2, st[0:T2, b, S:S + T2], start=True, stop=True)
                        pe.matmul(tile[o, 0, S * c_:S * c_ + S], v0, st[0:64, b, 0:S], start=True, stop=True)
                        mm = pe.matmul(tile[o, 1, at:at + 141], v1, st[64:128, b, 64:S], start=True, stop=True)
                mm.then_inc(filled["hacc"], 1)

            def turn_tokens(g, n):
                tile = take(pe, f"tm{n}", g)
                for c_ in range(2):
                    for k, name in enumerate(("xn2", "h2")):
                        src = A[name][:, 2 * n + c_, :]
                        pe.transpose(tile[:, c_, 256 * k:256 * k + 128], src[:, 0:128], ident32[:, :])
                        mm = pe.transpose(tile[0:T2, c_, 256 * k + 128:256 * k + 256], src[:, 128:S], ident32[:, :])
                mm.then_inc(filled["tm"], 1)

            def logits(g):
                tile = take(pe, "lg", g)
                for p in range(GP):
                    src = A["xn2"][:, p, :]
                    pe.matmul(tile[:, 0, 32 * p:32 * p + 32], src[:, 0:128], w_gate[:, :], start=True, stop=True)
                    mm = pe.matmul(tile[0:T2, 0, 128 + 32 * p:160 + 32 * p], src[:, 128:S], w_gate[:, :], start=True, stop=True)
                mm.then_inc(filled["lg"], 1)

            pe.wait_ge(conv_weights_lo_made, 4)
            pe.wait_ge(patterns_made, 10)
            pe.wait_ge(attn_constants_made, 1)
            pe.wait_ge(attn_weights_loaded, 16 * 14)

            def count(p):
                pe.wait_ge(counts_made, p + 1)
                pe.matmul(double[0][:, 0, 0:E], before[:, :], counts[:, :], start=True, stop=True)
                pe.matmul(double[0][:, 0, E:2 * E], all_ones[:, :], counts[:, :], start=True, stop=True).then_inc(offsets_made, 1)

            def turn(t):
                if on(t):
                    conv(1, t, 0)
                if isinstance(t, int) and t == ROUTE + 1:
                    assert TILE["turned"] is double[0]
                    take(pe, "turned", t - 2)
                    count(0)
                    pe.wait_ge(offsets_read, 1)
                if on(t - 2):
                    turn_result(t - 2)
                if on(t - 3):
                    for n in range(2):
                        sums(t - 3, n)
                if on(t - 2):
                    tokens(t - 2)
                if on(t):
                    conv(1, t, 1)
                if on(t - 3):
                    pe.wait_ge(out_squares_ready, t - 2)
                    product(t - 3, "ms", average, "sq_b")
                if on(t - 2):
                    pe.wait_ge(tokens_ready, (t - 2) * 2 + 2)
                    pe.wait_ge(text_loaded, (t - 2) * 16 + 16)
                    product(t - 2, "cx1", centre, "tokens")
                if on(t):
                    conv(1, t, 2)
                if on(t - 2):
                    pe.wait_ge(squares1_ready, t - 1)
                    product(t - 2, "var1", average, "sq")
                if on(t - 3):
                    pe.wait_ge(new_stream_ready, t - 2)
                    product(t - 3, "cx3", centre, "h2")
                if on(t - 1):
                    conv(3, t - 1, 0)
                if on(t - 3):
                    pe.wait_ge(squares3_ready, t - 2)
                    product(t - 3, "var3", average, "sq_b")
                if on(t - 2):
                    pe.wait_ge(xn_ready, t - 1)
                    for name in PROJ[0:3]:
                        product(t - 2, name, w_proj[name], "xn")
                if on(t - 1):
                    conv(3, t - 1, 1)
                if on(t - 2):
                    for name in PROJ[3:6]:
                        product(t - 2, name, w_proj[name], "xn")
                if on(t):
                    conv(2, t, 0)
                if on(t - 3):
                    pe.wait_ge(xn2_ready, t - 2)
                    for n in range(2):
                        turn_tokens(t - 3, n)
                    logits(t - 3)
                if on(t - 2):
                    for n in range(4):
                        scores(t - 2, n)
                if on(t):
                    conv(2, t, 1)
                if on(t - 2):
                    pe.wait_ge(n_times_q_ready, t - 1)
                    product(t - 2, "den", total, "nq")
                    turn_values(t - 2)

            turns(pe, None, 0, turn)

            count(1)
            pe.wait_ge(expert_weights_made, 5)
            pe.wait_ge(quad_experts_made, 2)

            def expert_of(q):
                return pe.value_load(quad_i[0:1, bass.ds(q, 1)], min_val=0, max_val=E - 1)

            def step(m, h):
                result, turned, hidden = behind(m, h, 3), behind(m, h, 0), behind(m, h, 1)
                if result:
                    w2_ = bass.ds(expert_of(result[0]) * D_, D_)
                if hidden:
                    w1_ = bass.ds(expert_of(hidden[0]) * F, F)
                if result:
                    q, _, _, two = result
                    pe.wait_ge(hidden_lo_made, q + 1)
                    wait(pe, expert_result_copied, q + (-1))
                    for n in range(4):
                        dst, c_ = double[2][:, two, 64 * n:64 * n + 64], slice(128 * n, 128 * n + 128)
                        pe.matmul(dst, hid_hi[two][:, c_], fw2_hi[:, w2_], start=True, stop=False)
                        pe.matmul(dst, hid_hi[two][:, c_], fw2_lo[:, w2_], start=False, stop=False)
                        pe.matmul(dst, hid_lo[two][:, c_], fw2_hi[:, w2_], start=False, stop=False)
                        mm = pe.matmul(dst, ones_h[:, :], fb2[0:2, w2_], start=False, stop=True)
                    mm.then_inc(expert_product_done, 1)
                if turned:
                    q, turn, ring, two = turned
                    pe.wait_ge(quad_rows_loaded[ring], turn * 16 + 16)
                    wait(pe, quad_lo_made, q + (-1))
                    for n in range(4):
                        mm = pe.matmul(double[0][0:64, two, 128 * n:128 * n + 128], x_tiles[ring][:, n, :], ident32[:, :], start=True, stop=True)
                    mm.then_inc(quad_rows_turned, 1)
                if hidden:
                    q, _, _, two = hidden
                    pe.wait_ge(quad_lo_made, q + 1)
                    wait(pe, hidden_ready, q + (-1))
                    pe.matmul(double[1][:, two, :], fw1_hi[:, w1_], xT[two], start=True, stop=False)
                    pe.matmul(double[1][:, two, :], fw1_lo[:, w1_], xT[two], start=False, stop=True).then_inc(hidden_product_done, 1)

            slots(pe, step)


def kernel(**kw):
    import numpy as np
    import concourse.bacc as bacc
    from concourse.bass_utils import run_bass_kernel_spmd as run

    nc = bacc.Bacc("TRN2", target_bir_lowering=False, num_devices=1)
    kw = {n: np.asarray(v) for n, v in kw.items()}
    k = {n[7:]: v for n, v in kw.items() if n.startswith("L0_tok")}
    at = {n[8:]: v for n, v in kw.items() if n.startswith("L0_attn")}
    ff = {n[7:]: v for n, v in kw.items() if n.startswith("L0_ffn")}
    c = np.ascontiguousarray
    bg = at["bg"]
    arr = {
        "x": c(kw["x"].reshape(16, 8, 128, 192).transpose(0, 2, 1, 3).reshape(16, 128, 1536)),
        "txt": c(kw["txt"].reshape(16, 4, 2, 77, 64).transpose(0, 2, 4, 1, 3).reshape(16, 128, 4, 77)),
        "w1": c(k["conv1_w"].transpose(1, 2, 3, 0).reshape(128, -1)),
        "w2": c(k["conv2_w"].transpose(1, 2, 3, 0).reshape(128, -1)),
        "w3": c(k["conv3_w"].transpose(1, 2, 3, 0).reshape(128, -1)),
        "w4": k["out_w"],
        **{n: k[n] for n in ("conv1_b", "conv2_b", "conv3_b", "out_b", "ln0_g", "ln0_b", "ln1_g", "ln1_b")},
        "w_q": at["Wq"], "w_k": at["Wk"], "w_v": at["Wv"],
        "w_i": c(at["Wg"][:, 0:64]), "w_f": c(at["Wg"][:, 64:128]), "w_o": c(at["Wg"][:, 128:192]),
        "acol": c(np.stack([at["bq"], at["bk"], at["bv"], bg[0:64], bg[64:128], bg[128:192], at["input_bias"], at["norm_scale"]], axis=1)),
        "gate_w": ff["gate_w"], "gate_b": ff["gate_b"],
        "ffn_w1": c(ff["w1"].transpose(1, 0, 2)), "ffn_w2": c(ff["w2"].transpose(1, 0, 2)),
        "ffn_b1": c(ff["b1"].T), "ffn_b2": c(ff["b2"].reshape(1, -1)),
        "ffn_gamma": ff["gamma"], "ffn_beta": ff["beta"],
        "row_sel": np.eye(2, dtype=np.float32),
    }
    aps = {n: nc.dram_tensor("in_" + n, v.shape, mybir.dt.from_np(v.dtype), kind="ExternalInput").ap() for n, v in arr.items()}
    o = nc.dram_tensor("o_d", (128, 205, 64), F32, kind="ExternalOutput").ap()
    build(nc, aps, o)
    r = run(nc, [{"in_" + n: v for n, v in arr.items()}], core_ids=[0])
    return r.results[0]["o_d"]
```
